# Optimizing a Trainium2 kernel written in Bass

```python
import numpy as np
import jax
import jax.numpy as jnp

def _softmax(x, axis=-1):
    return jax.nn.softmax(x, axis=axis)

def _gelu(x):
    return jax.nn.gelu(x, approximate=True)

def _silu(x):
    return jax.nn.silu(x)

def _sigmoid(x):
    return jax.nn.sigmoid(x)

def _layernorm(x, axis=-1, eps=1e-05):
    m = jnp.mean(x, axis=axis, keepdims=True)
    v = jnp.var(x, axis=axis, keepdims=True)
    return (x - m) / jnp.sqrt(v + eps)

def _scatter_add(tgt, idx, src, axis=0):
    return tgt.at[idx].add(src)

def _segment_sum(src, seg, n):
    return jax.ops.segment_sum(src, seg, n)
kernel_name = 'mk_lm_tower_d2_tok_ids1024_r4_674a60'

def setup_inputs(seed: int=0):
    np.random.seed(seed)
    _w = jnp.asarray

    def _rec_inputs():
        import jax
        import jax.numpy as jnp
        _rk = jax.random.key(seed)
        x = jax.random.randint(jax.random.fold_in(_rk, 1), (4, 512), 0, 127987, jnp.int32)
        return x
    x = _rec_inputs()

    def _L0_tok_setup():
        import jax, jax.numpy as jnp
        import numpy as np
        N_TOKENS = 32000
        D_EMBED = 256
        D_PROJ = 256
        CUTOFF_ENDS = [0, 5000, 15000, 25000, N_TOKENS]
        DIV_VAL = 4
        EMB_SCALE = D_PROJ ** 0.5
        key = jax.random.key(seed)
        keys = jax.random.split(key, 9)
        inp = {'input': jax.random.randint(keys[0], (4, 512), 0, N_TOKENS, dtype=jnp.int64) if jax.config.jax_enable_x64 else jax.random.randint(keys[0], (4, 512), 0, N_TOKENS, dtype=jnp.int32)}
        for i in range(4):
            left, right = (CUTOFF_ENDS[i], CUTOFF_ENDS[i + 1])
            d_emb_i = D_EMBED // DIV_VAL ** i
            inp[f'emb{i}'] = jax.random.normal(keys[1 + i], (right - left, d_emb_i), dtype=jnp.float32)
            inp[f'proj{i}'] = jax.random.normal(keys[5 + i], (D_PROJ, d_emb_i), dtype=jnp.float32)
        return inp
    _L0_tok_all = _L0_tok_setup()
    _L0_tok_in = {k: v for k, v in _L0_tok_all.items() if k in ('emb0', 'emb1', 'emb2', 'emb3', 'proj0', 'proj1', 'proj2', 'proj3')}
    del _L0_tok_all

    def _L0_attn_setup():
        import jax, jax.numpy as jnp
        import numpy as np
        NUM_HEADS = 16

        def _sb_attention(x, Wq, Wk, Wv, Wo):
            b, n, e = x.shape
            h = NUM_HEADS
            d = e // h
            q = (x @ Wq.T).reshape(b, n, h, d).transpose(0, 2, 1, 3)
            k = (x @ Wk.T).reshape(b, n, h, d).transpose(0, 2, 1, 3)
            v = (x @ Wv.T).reshape(b, n, h, d).transpose(0, 2, 1, 3)
            scale = d ** (-0.5)
            logits = jnp.einsum('bhid,bhjd->bhij', q, k) * scale
            mask = jnp.triu(jnp.ones((n, n), dtype=bool), 0)
            log_z = jnp.where(mask, jnp.float32(-100000.0), jax.nn.log_sigmoid(logits))
            log_beta = jnp.where(mask, jnp.float32(0.0), jax.nn.log_sigmoid(-logits))
            total = jnp.sum(log_beta, axis=-1, keepdims=True)
            re_cum_log_beta = total - jnp.cumsum(log_beta, axis=-1)
            att = jnp.exp(log_z + re_cum_log_beta)
            o = jnp.einsum('bhij,bhjd->bhid', att, v)
            rem = 1.0 - jnp.sum(att, axis=-1)
            o = o + rem[..., None] * v
            o = o.transpose(0, 2, 1, 3).reshape(b, n, e)
            return o @ Wo.T
        key = jax.random.key(seed)
        ks = jax.random.split(key, 5)
        b, n, e = (1, 512, 256)
        std = 0.02
        x = jax.random.normal(ks[0], (b, n, e), dtype=jnp.float32)
        Wq = jax.random.normal(ks[1], (e, e), dtype=jnp.float32) * std
        Wk = jax.random.normal(ks[2], (e, e), dtype=jnp.float32) * std
        Wv = jax.random.normal(ks[3], (e, e), dtype=jnp.float32) * std
        Wo = jax.random.normal(ks[4], (e, e), dtype=jnp.float32) * std
        return {'x': x, 'Wq': Wq, 'Wk': Wk, 'Wv': Wv, 'Wo': Wo}
    _L0_attn_all = _L0_attn_setup()
    _L0_attn_in = {k: v for k, v in _L0_attn_all.items() if k in ('Wq', 'Wk', 'Wv', 'Wo')}
    del _L0_attn_all

    def _L0_ffn_setup():
        import jax, jax.numpy as jnp
        import numpy as np
        NUM_EXPERTS = 8
        TOP_K = 2
        MOE_DIM = 512

        def _moe_forward(x, moe_router, moe_w13, moe_w2):
            b, s, d = x.shape
            x_flat = x.reshape(b * s, d)
            router_logits = jnp.einsum('td,de->te', x_flat, moe_router)
            topk_logits, topk_idx = jax.lax.top_k(router_logits, TOP_K)
            topk_weights = jax.nn.softmax(topk_logits, axis=-1).astype(x.dtype)
            tokens = x_flat.shape[0]
            expert_ids = topk_idx.reshape(tokens * TOP_K)
            dispatch_weights = topk_weights.reshape(tokens * TOP_K)
            sort_idx = jnp.argsort(expert_ids, axis=0)
            token_ids = jnp.arange(tokens * TOP_K, dtype=jnp.int32) // TOP_K
            token_ids_sort = token_ids[sort_idx]
            x_sort = x_flat[token_ids_sort]
            w_sort = dispatch_weights[sort_idx].astype(x_flat.dtype)
            group_sizes = jnp.bincount(expert_ids, length=NUM_EXPERTS).astype(jnp.int32)
            w13_out = jax.lax.ragged_dot(x_sort, moe_w13, group_sizes)
            gate, up = jnp.split(w13_out, [MOE_DIM], axis=-1)
            hidden = jax.nn.silu(gate) * up
            out_dispatch = jax.lax.ragged_dot(hidden, moe_w2, group_sizes)
            out_flat = jnp.zeros_like(x_flat).at[token_ids_sort].add(out_dispatch * w_sort[:, None], mode='drop')
            return out_flat.reshape(b, s, d)
        key = jax.random.key(seed)
        k1, k2, k3, k4 = jax.random.split(key, 4)
        B, S, D = (4, 512, 256)
        x = jax.random.normal(k1, (B, S, D), dtype=jnp.float32)
        moe_router = jax.random.normal(k2, (D, NUM_EXPERTS), dtype=jnp.float32) * 0.02
        moe_w13 = jax.random.normal(k3, (NUM_EXPERTS, D, 2 * MOE_DIM), dtype=jnp.float32) * 0.02
        moe_w2 = jax.random.normal(k4, (NUM_EXPERTS, MOE_DIM, D), dtype=jnp.float32) * 0.02
        return {'x': x, 'moe_router': moe_router, 'moe_w13': moe_w13, 'moe_w2': moe_w2}
    _L0_ffn_all = _L0_ffn_setup()
    _L0_ffn_in = {k: v for k, v in _L0_ffn_all.items() if k in ('moe_router', 'moe_w13', 'moe_w2')}
    del _L0_ffn_all

    def _L1_attn_setup():
        import jax, jax.numpy as jnp
        import numpy as np
        MAX_LR = 0.01
        NS_A, NS_B, NS_C = (3.4445, -4.775, 2.0315)

        def newtonschulz5(G, steps=5, eps=1e-07):
            transpose = G.shape[-2] > G.shape[-1]
            X = jnp.swapaxes(G, -2, -1) if transpose else G
            X = X / (jnp.linalg.norm(X, axis=(-2, -1), keepdims=True) + eps)
            for _ in range(steps):
                A = X @ jnp.swapaxes(X, -2, -1)
                Bm = NS_B * A + NS_C * (A @ A)
                X = NS_A * X + Bm @ X
            return jnp.swapaxes(X, -2, -1) if transpose else X

        def _reference_tuple_inner(tokens, wq, wk, wv, wo, w_lr, w_target, w_gates, rms_w):
            N = tokens.shape[1]
            scale = wq.shape[-1] ** (-0.5)
            eps = jnp.finfo(tokens.dtype).eps
            t = tokens * jax.lax.rsqrt(jnp.mean(tokens * tokens, -1, keepdims=True) + eps) * rms_w
            gates = jnp.swapaxes(jax.nn.sigmoid(t @ w_gates), -2, -1)[..., None]
            q = jnp.einsum('bnd,hde->bhne', t, wq)
            k = jnp.einsum('bnd,hde->bhne', t, wk)
            v = jnp.einsum('bnd,hde->bhne', t, wv)
            score = jnp.einsum('bhie,bhje->bhij', q, k) * scale
            causal_mask = jnp.triu(jnp.ones((N, N), bool), 1)
            score = jnp.where(causal_mask, -jnp.finfo(score.dtype).max, score)
            attn = jax.nn.softmax(score, axis=-1)
            out = jnp.einsum('bhij,bhje->bhie', attn, v) * gates
            pred_values = jnp.einsum('bhne,hed->bnd', out, wo)
            tv = t[:, 1:] @ w_target
            tv = (tv - tv.mean(-1, keepdims=True)) * jax.lax.rsqrt(tv.var(-1, keepdims=True) + 1e-05)
            ts = t[:, :-1]
            pv = pred_values[:, :-1]
            o = out[:, :, :-1]
            g = gates[:, :, :-1]
            a = attn[:, :, :-1, :-1]
            qs, ks_, vs = (q[:, :, :-1], k[:, :, :-1], v[:, :, :-1])
            lrs = jax.nn.sigmoid(ts @ w_lr) * MAX_LR
            lr, mlr = (lrs[..., 0], lrs[..., 1])
            error = tv - pv
            dout = jnp.einsum('bnd,hed->bhne', error, wo)
            du = dout * g
            delta = jnp.sum(dout * o, -1, keepdims=True)
            dv = jnp.einsum('bhij,bhie->bhje', a, du)
            dattn = jnp.einsum('bhje,bhie->bhij', vs, du)
            dscore = scale * a * (dattn - delta)
            dq = jnp.einsum('bhje,bhij->bhie', ks_, dscore)
            dk = jnp.einsum('bhie,bhij->bhje', qs, dscore)
            t_qk = ts * lr[..., None]
            t_v = ts * mlr[..., None]
            o_wo = o * mlr[:, None, :, None]
            dwq = jnp.einsum('bhie,bid->bhde', dq, t_qk)
            dwk = jnp.einsum('bhje,bjd->bhde', dk, t_qk)
            dwv = jnp.einsum('bhje,bjd->bhde', dv, t_v)
            dwo = jnp.einsum('bnd,bhne->bhed', error, o_wo)
            dwv = newtonschulz5(dwv)
            dwo = newtonschulz5(dwo)
            return (pred_values, dwq, dwk, dwv, dwo)
        key = jax.random.key(seed)
        ks = jax.random.split(key, 9)
        B, N, D, H, DH = (4, 256, 256, 8, 64)
        s = D ** (-0.5)
        return {'tokens': jax.random.normal(ks[0], (B, N, D), jnp.float32), 'wq': jax.random.normal(ks[1], (H, D, DH), jnp.float32) * s, 'wk': jax.random.normal(ks[2], (H, D, DH), jnp.float32) * s, 'wv': jax.random.normal(ks[3], (H, D, DH), jnp.float32) * s, 'wo': jax.random.normal(ks[4], (H, DH, D), jnp.float32) * s, 'w_lr': jax.random.normal(ks[5], (D, 2), jnp.float32) * 0.02, 'w_target': jax.random.normal(ks[6], (D, D), jnp.float32) * 0.02, 'w_gates': jax.random.normal(ks[7], (D, H), jnp.float32) * 0.02, 'rms_w': jnp.ones((D,), jnp.float32)}
    _L1_attn_all = _L1_attn_setup()
    _L1_attn_in = {k: v for k, v in _L1_attn_all.items() if k in ('wq', 'wk', 'wv', 'wo', 'w_lr', 'w_target', 'w_gates', 'rms_w')}
    del _L1_attn_all

    def _L1_ffn_setup():
        import jax, jax.numpy as jnp
        import numpy as np
        DIM = 256
        DEPTH = 2
        HEADS = 8
        DIM_HEAD = 64
        WINDOW = 128
        INNER = HEADS * DIM_HEAD
        HID = int(DIM * 4 * 2 / 3)
        B, N = (2, 2048)
        QK_SCALE = 8.0

        def shift_token(t):
            t1, t2 = jnp.split(t, 2, axis=-1)
            t2 = jnp.pad(t2, ((0, 0), (1, 0), (0, 0)))[:, :-1]
            return jnp.concatenate([t1, t2], axis=-1)

        def l2norm(t):
            return t / jnp.clip(jnp.linalg.norm(t, axis=-1, keepdims=True), 1e-12)

        def rotate_half(x):
            x1, x2 = jnp.split(x, 2, axis=-1)
            return jnp.concatenate([-x2, x1], axis=-1)

        def rotary_xpos(q, k):
            n = q.shape[-2]
            half_idx = jnp.arange(0, DIM_HEAD, 2, dtype=jnp.float32)
            inv_freq = 1.0 / 10000.0 ** (half_idx / DIM_HEAD)
            t = jnp.arange(n, dtype=jnp.float32)
            freqs = t[:, None] * inv_freq[None, :]
            freqs = jnp.concatenate([freqs, freqs], axis=-1)
            base = (half_idx + 0.4 * DIM_HEAD) / (1.4 * DIM_HEAD)
            power = (t - n // 2) / float(WINDOW // 2)
            scale = base[None, :] ** power[:, None]
            scale = jnp.concatenate([scale, scale], axis=-1)
            cos, sin = (jnp.cos(freqs), jnp.sin(freqs))
            q = q * cos * scale + rotate_half(q) * sin * scale
            k = k * cos / scale + rotate_half(k) * sin / scale
            return (q, k)

        def local_attention(q, k, v):
            b, h, n, d = q.shape
            w = n // WINDOW
            bq = q.reshape(b, h, w, WINDOW, d) * QK_SCALE
            bk = k.reshape(b, h, w, WINDOW, d)
            bv = v.reshape(b, h, w, WINDOW, d)

            def look_around(t):
                p = jnp.pad(t, ((0, 0), (0, 0), (1, 0), (0, 0), (0, 0)))
                return jnp.concatenate([p[:, :, :w], p[:, :, 1:]], axis=3)
            bk, bv = (look_around(bk), look_around(bv))
            bt = jnp.arange(n).reshape(w, WINDOW)
            btp = jnp.pad(bt, ((1, 0), (0, 0)), constant_values=-1)
            btk = jnp.concatenate([btp[:w], btp[1:]], axis=1)
            sim = jnp.einsum('bhwid,bhwjd->bhwij', bq, bk)
            i = bt[:, :, None]
            j = btk[:, None, :]
            mask = (i < j) | (i > j + WINDOW) | (j == -1)
            sim = jnp.where(mask, -jnp.finfo(sim.dtype).max, sim)
            attn = jax.nn.softmax(sim, axis=-1)
            out = jnp.einsum('bhwij,bhwjd->bhwid', attn, bv)
            return out.reshape(b, h, n, d)

        def _layer(x, wqkv, qs, ksc, wo, lg, lb, w1, b1, w2, b2):
            b, n, _ = x.shape
            h = shift_token(x)
            qkv = h @ wqkv
            q, k, v = jnp.split(qkv, 3, axis=-1)
            to_heads = lambda t: t.reshape(b, n, HEADS, DIM_HEAD).transpose(0, 2, 1, 3)
            q, k, v = (to_heads(q), to_heads(k), to_heads(v))
            q = l2norm(q) * qs
            k = l2norm(k) * ksc
            q, k = rotary_xpos(q, k)
            o = local_attention(q, k, v)
            o = o.transpose(0, 2, 1, 3).reshape(b, n, INNER)
            x = x + o @ wo
            h = shift_token(x)
            mu = h.mean(-1, keepdims=True)
            var = h.var(-1, keepdims=True)
            h = (h - mu) / jnp.sqrt(var + 1e-05) * lg + lb
            h = h @ w1 + b1
            a, g = jnp.split(h, 2, axis=-1)
            h = a * jax.nn.gelu(g, approximate=False)
            x = x + h @ w2 + b2
            return x
        key = jax.random.key(seed)
        ks = jax.random.split(key, 6)
        return {'x': jax.random.normal(ks[0], (B, N, DIM), jnp.float32), 'wqkv': jax.random.normal(ks[1], (DEPTH, DIM, 3 * INNER), jnp.float32) * 0.02, 'q_scale': jnp.ones((DEPTH, DIM_HEAD), jnp.float32), 'k_scale': jnp.ones((DEPTH, DIM_HEAD), jnp.float32), 'wo': jax.random.normal(ks[2], (DEPTH, INNER, DIM), jnp.float32) * 0.02, 'ln_g': jnp.ones((DEPTH, DIM), jnp.float32), 'ln_b': jnp.zeros((DEPTH, DIM), jnp.float32), 'w1': jax.random.normal(ks[3], (DEPTH, DIM, 2 * HID), jnp.float32) * 0.02, 'b1': jnp.zeros((DEPTH, 2 * HID), jnp.float32), 'w2': jax.random.normal(ks[4], (DEPTH, HID, DIM), jnp.float32) * 0.02, 'b2': jnp.zeros((DEPTH, DIM), jnp.float32)}
    _L1_ffn_all = _L1_ffn_setup()
    _L1_ffn_in = {k: v for k, v in _L1_ffn_all.items() if k in ('wqkv', 'q_scale', 'k_scale', 'wo', 'ln_g', 'ln_b', 'w1', 'b1', 'w2', 'b2')}
    del _L1_ffn_all
    return {'x': x, 'L0_tok_emb0': _L0_tok_in['emb0'], 'L0_tok_emb1': _L0_tok_in['emb1'], 'L0_tok_emb2': _L0_tok_in['emb2'], 'L0_tok_emb3': _L0_tok_in['emb3'], 'L0_tok_proj0': _L0_tok_in['proj0'], 'L0_tok_proj1': _L0_tok_in['proj1'], 'L0_tok_proj2': _L0_tok_in['proj2'], 'L0_tok_proj3': _L0_tok_in['proj3'], 'L0_attn_Wq': _L0_attn_in['Wq'], 'L0_attn_Wk': _L0_attn_in['Wk'], 'L0_attn_Wv': _L0_attn_in['Wv'], 'L0_attn_Wo': _L0_attn_in['Wo'], 'L0_ffn_moe_router': _L0_ffn_in['moe_router'], 'L0_ffn_moe_w13': _L0_ffn_in['moe_w13'], 'L0_ffn_moe_w2': _L0_ffn_in['moe_w2'], 'L1_attn_wq': _L1_attn_in['wq'], 'L1_attn_wk': _L1_attn_in['wk'], 'L1_attn_wv': _L1_attn_in['wv'], 'L1_attn_wo': _L1_attn_in['wo'], 'L1_attn_w_lr': _L1_attn_in['w_lr'], 'L1_attn_w_target': _L1_attn_in['w_target'], 'L1_attn_w_gates': _L1_attn_in['w_gates'], 'L1_attn_rms_w': _L1_attn_in['rms_w'], 'L1_ffn_wqkv': _L1_ffn_in['wqkv'], 'L1_ffn_q_scale': _L1_ffn_in['q_scale'], 'L1_ffn_k_scale': _L1_ffn_in['k_scale'], 'L1_ffn_wo': _L1_ffn_in['wo'], 'L1_ffn_ln_g': _L1_ffn_in['ln_g'], 'L1_ffn_ln_b': _L1_ffn_in['ln_b'], 'L1_ffn_w1': _L1_ffn_in['w1'], 'L1_ffn_b1': _L1_ffn_in['b1'], 'L1_ffn_w2': _L1_ffn_in['w2'], 'L1_ffn_b2': _L1_ffn_in['b2']}

def reference(x, L0_tok_emb0, L0_tok_emb1, L0_tok_emb2, L0_tok_emb3, L0_tok_proj0, L0_tok_proj1, L0_tok_proj2, L0_tok_proj3, L0_attn_Wq, L0_attn_Wk, L0_attn_Wv, L0_attn_Wo, L0_ffn_moe_router, L0_ffn_moe_w13, L0_ffn_moe_w2, L1_attn_wq, L1_attn_wk, L1_attn_wv, L1_attn_wo, L1_attn_w_lr, L1_attn_w_target, L1_attn_w_gates, L1_attn_rms_w, L1_ffn_wqkv, L1_ffn_q_scale, L1_ffn_k_scale, L1_ffn_wo, L1_ffn_ln_g, L1_ffn_ln_b, L1_ffn_w1, L1_ffn_b1, L1_ffn_w2, L1_ffn_b2):
    import jax
    import jax.numpy as jnp

    def _L0_tok_ref(input, emb0, emb1, emb2, emb3, proj0, proj1, proj2, proj3):
        import jax, jax.numpy as jnp
        import numpy as np
        N_TOKENS = 32000
        D_EMBED = 256
        D_PROJ = 256
        CUTOFF_ENDS = [0, 5000, 15000, 25000, N_TOKENS]
        DIV_VAL = 4
        EMB_SCALE = D_PROJ ** 0.5
        tables = [emb0, emb1, emb2, emb3]
        projs = [proj0, proj1, proj2, proj3]
        flat = input.reshape(-1)
        out = jnp.zeros((flat.shape[0], D_PROJ), dtype=jnp.float32)
        for i in range(4):
            left, right = (CUTOFF_ENDS[i], CUTOFF_ENDS[i + 1])
            mask = (flat >= left) & (flat < right)
            idx = jnp.clip(flat - left, 0, right - left - 1)
            e = jnp.einsum('td,pd->tp', tables[i][idx], projs[i])
            out = out + jnp.where(mask[:, None], e, 0.0)
        out = out * jnp.asarray(EMB_SCALE, out.dtype)
        return out.reshape(*input.shape, D_PROJ)

    def _L0_attn_ref(x, Wq, Wk, Wv, Wo):
        import jax, jax.numpy as jnp
        import numpy as np
        NUM_HEADS = 16

        def _sb_attention(x, Wq, Wk, Wv, Wo):
            b, n, e = x.shape
            h = NUM_HEADS
            d = e // h
            q = (x @ Wq.T).reshape(b, n, h, d).transpose(0, 2, 1, 3)
            k = (x @ Wk.T).reshape(b, n, h, d).transpose(0, 2, 1, 3)
            v = (x @ Wv.T).reshape(b, n, h, d).transpose(0, 2, 1, 3)
            scale = d ** (-0.5)
            logits = jnp.einsum('bhid,bhjd->bhij', q, k) * scale
            mask = jnp.triu(jnp.ones((n, n), dtype=bool), 0)
            log_z = jnp.where(mask, jnp.float32(-100000.0), jax.nn.log_sigmoid(logits))
            log_beta = jnp.where(mask, jnp.float32(0.0), jax.nn.log_sigmoid(-logits))
            total = jnp.sum(log_beta, axis=-1, keepdims=True)
            re_cum_log_beta = total - jnp.cumsum(log_beta, axis=-1)
            att = jnp.exp(log_z + re_cum_log_beta)
            o = jnp.einsum('bhij,bhjd->bhid', att, v)
            rem = 1.0 - jnp.sum(att, axis=-1)
            o = o + rem[..., None] * v
            o = o.transpose(0, 2, 1, 3).reshape(b, n, e)
            return o @ Wo.T
        return _sb_attention(x, Wq, Wk, Wv, Wo)

    def _L0_ffn_ref(x, moe_router, moe_w13, moe_w2):
        import jax, jax.numpy as jnp
        import numpy as np
        NUM_EXPERTS = 8
        TOP_K = 2
        MOE_DIM = 512

        def _moe_forward(x, moe_router, moe_w13, moe_w2):
            b, s, d = x.shape
            x_flat = x.reshape(b * s, d)
            router_logits = jnp.einsum('td,de->te', x_flat, moe_router)
            topk_logits, topk_idx = jax.lax.top_k(router_logits, TOP_K)
            topk_weights = jax.nn.softmax(topk_logits, axis=-1).astype(x.dtype)
            tokens = x_flat.shape[0]
            expert_ids = topk_idx.reshape(tokens * TOP_K)
            dispatch_weights = topk_weights.reshape(tokens * TOP_K)
            sort_idx = jnp.argsort(expert_ids, axis=0)
            token_ids = jnp.arange(tokens * TOP_K, dtype=jnp.int32) // TOP_K
            token_ids_sort = token_ids[sort_idx]
            x_sort = x_flat[token_ids_sort]
            w_sort = dispatch_weights[sort_idx].astype(x_flat.dtype)
            group_sizes = jnp.bincount(expert_ids, length=NUM_EXPERTS).astype(jnp.int32)
            w13_out = jax.lax.ragged_dot(x_sort, moe_w13, group_sizes)
            gate, up = jnp.split(w13_out, [MOE_DIM], axis=-1)
            hidden = jax.nn.silu(gate) * up
            out_dispatch = jax.lax.ragged_dot(hidden, moe_w2, group_sizes)
            out_flat = jnp.zeros_like(x_flat).at[token_ids_sort].add(out_dispatch * w_sort[:, None], mode='drop')
            return out_flat.reshape(b, s, d)
        return _moe_forward(x, moe_router, moe_w13, moe_w2)

    def _L1_attn_ref(tokens, wq, wk, wv, wo, w_lr, w_target, w_gates, rms_w):
        import jax, jax.numpy as jnp
        import numpy as np
        MAX_LR = 0.01
        NS_A, NS_B, NS_C = (3.4445, -4.775, 2.0315)

        def newtonschulz5(G, steps=5, eps=1e-07):
            transpose = G.shape[-2] > G.shape[-1]
            X = jnp.swapaxes(G, -2, -1) if transpose else G
            X = X / (jnp.linalg.norm(X, axis=(-2, -1), keepdims=True) + eps)
            for _ in range(steps):
                A = X @ jnp.swapaxes(X, -2, -1)
                Bm = NS_B * A + NS_C * (A @ A)
                X = NS_A * X + Bm @ X
            return jnp.swapaxes(X, -2, -1) if transpose else X

        def _reference_tuple_inner(tokens, wq, wk, wv, wo, w_lr, w_target, w_gates, rms_w):
            N = tokens.shape[1]
            scale = wq.shape[-1] ** (-0.5)
            eps = jnp.finfo(tokens.dtype).eps
            t = tokens * jax.lax.rsqrt(jnp.mean(tokens * tokens, -1, keepdims=True) + eps) * rms_w
            gates = jnp.swapaxes(jax.nn.sigmoid(t @ w_gates), -2, -1)[..., None]
            q = jnp.einsum('bnd,hde->bhne', t, wq)
            k = jnp.einsum('bnd,hde->bhne', t, wk)
            v = jnp.einsum('bnd,hde->bhne', t, wv)
            score = jnp.einsum('bhie,bhje->bhij', q, k) * scale
            causal_mask = jnp.triu(jnp.ones((N, N), bool), 1)
            score = jnp.where(causal_mask, -jnp.finfo(score.dtype).max, score)
            attn = jax.nn.softmax(score, axis=-1)
            out = jnp.einsum('bhij,bhje->bhie', attn, v) * gates
            pred_values = jnp.einsum('bhne,hed->bnd', out, wo)
            tv = t[:, 1:] @ w_target
            tv = (tv - tv.mean(-1, keepdims=True)) * jax.lax.rsqrt(tv.var(-1, keepdims=True) + 1e-05)
            ts = t[:, :-1]
            pv = pred_values[:, :-1]
            o = out[:, :, :-1]
            g = gates[:, :, :-1]
            a = attn[:, :, :-1, :-1]
            qs, ks_, vs = (q[:, :, :-1], k[:, :, :-1], v[:, :, :-1])
            lrs = jax.nn.sigmoid(ts @ w_lr) * MAX_LR
            lr, mlr = (lrs[..., 0], lrs[..., 1])
            error = tv - pv
            dout = jnp.einsum('bnd,hed->bhne', error, wo)
            du = dout * g
            delta = jnp.sum(dout * o, -1, keepdims=True)
            dv = jnp.einsum('bhij,bhie->bhje', a, du)
            dattn = jnp.einsum('bhje,bhie->bhij', vs, du)
            dscore = scale * a * (dattn - delta)
            dq = jnp.einsum('bhje,bhij->bhie', ks_, dscore)
            dk = jnp.einsum('bhie,bhij->bhje', qs, dscore)
            t_qk = ts * lr[..., None]
            t_v = ts * mlr[..., None]
            o_wo = o * mlr[:, None, :, None]
            dwq = jnp.einsum('bhie,bid->bhde', dq, t_qk)
            dwk = jnp.einsum('bhje,bjd->bhde', dk, t_qk)
            dwv = jnp.einsum('bhje,bjd->bhde', dv, t_v)
            dwo = jnp.einsum('bnd,bhne->bhed', error, o_wo)
            dwv = newtonschulz5(dwv)
            dwo = newtonschulz5(dwo)
            return (pred_values, dwq, dwk, dwv, dwo)
        return _reference_tuple_inner(tokens, wq, wk, wv, wo, w_lr, w_target, w_gates, rms_w)[0]

    def _L1_ffn_ref(x, wqkv, q_scale, k_scale, wo, ln_g, ln_b, w1, b1, w2, b2):
        import jax, jax.numpy as jnp
        import numpy as np
        DIM = 256
        DEPTH = 2
        HEADS = 8
        DIM_HEAD = 64
        WINDOW = 128
        INNER = HEADS * DIM_HEAD
        HID = int(DIM * 4 * 2 / 3)
        B, N = (2, 2048)
        QK_SCALE = 8.0

        def shift_token(t):
            t1, t2 = jnp.split(t, 2, axis=-1)
            t2 = jnp.pad(t2, ((0, 0), (1, 0), (0, 0)))[:, :-1]
            return jnp.concatenate([t1, t2], axis=-1)

        def l2norm(t):
            return t / jnp.clip(jnp.linalg.norm(t, axis=-1, keepdims=True), 1e-12)

        def rotate_half(x):
            x1, x2 = jnp.split(x, 2, axis=-1)
            return jnp.concatenate([-x2, x1], axis=-1)

        def rotary_xpos(q, k):
            n = q.shape[-2]
            half_idx = jnp.arange(0, DIM_HEAD, 2, dtype=jnp.float32)
            inv_freq = 1.0 / 10000.0 ** (half_idx / DIM_HEAD)
            t = jnp.arange(n, dtype=jnp.float32)
            freqs = t[:, None] * inv_freq[None, :]
            freqs = jnp.concatenate([freqs, freqs], axis=-1)
            base = (half_idx + 0.4 * DIM_HEAD) / (1.4 * DIM_HEAD)
            power = (t - n // 2) / float(WINDOW // 2)
            scale = base[None, :] ** power[:, None]
            scale = jnp.concatenate([scale, scale], axis=-1)
            cos, sin = (jnp.cos(freqs), jnp.sin(freqs))
            q = q * cos * scale + rotate_half(q) * sin * scale
            k = k * cos / scale + rotate_half(k) * sin / scale
            return (q, k)

        def local_attention(q, k, v):
            b, h, n, d = q.shape
            w = n // WINDOW
            bq = q.reshape(b, h, w, WINDOW, d) * QK_SCALE
            bk = k.reshape(b, h, w, WINDOW, d)
            bv = v.reshape(b, h, w, WINDOW, d)

            def look_around(t):
                p = jnp.pad(t, ((0, 0), (0, 0), (1, 0), (0, 0), (0, 0)))
                return jnp.concatenate([p[:, :, :w], p[:, :, 1:]], axis=3)
            bk, bv = (look_around(bk), look_around(bv))
            bt = jnp.arange(n).reshape(w, WINDOW)
            btp = jnp.pad(bt, ((1, 0), (0, 0)), constant_values=-1)
            btk = jnp.concatenate([btp[:w], btp[1:]], axis=1)
            sim = jnp.einsum('bhwid,bhwjd->bhwij', bq, bk)
            i = bt[:, :, None]
            j = btk[:, None, :]
            mask = (i < j) | (i > j + WINDOW) | (j == -1)
            sim = jnp.where(mask, -jnp.finfo(sim.dtype).max, sim)
            attn = jax.nn.softmax(sim, axis=-1)
            out = jnp.einsum('bhwij,bhwjd->bhwid', attn, bv)
            return out.reshape(b, h, n, d)

        def _layer(x, wqkv, qs, ksc, wo, lg, lb, w1, b1, w2, b2):
            b, n, _ = x.shape
            h = shift_token(x)
            qkv = h @ wqkv
            q, k, v = jnp.split(qkv, 3, axis=-1)
            to_heads = lambda t: t.reshape(b, n, HEADS, DIM_HEAD).transpose(0, 2, 1, 3)
            q, k, v = (to_heads(q), to_heads(k), to_heads(v))
            q = l2norm(q) * qs
            k = l2norm(k) * ksc
            q, k = rotary_xpos(q, k)
            o = local_attention(q, k, v)
            o = o.transpose(0, 2, 1, 3).reshape(b, n, INNER)
            x = x + o @ wo
            h = shift_token(x)
            mu = h.mean(-1, keepdims=True)
            var = h.var(-1, keepdims=True)
            h = (h - mu) / jnp.sqrt(var + 1e-05) * lg + lb
            h = h @ w1 + b1
            a, g = jnp.split(h, 2, axis=-1)
            h = a * jax.nn.gelu(g, approximate=False)
            x = x + h @ w2 + b2
            return x
        for l in range(DEPTH):
            x = _layer(x, wqkv[l], q_scale[l], k_scale[l], wo[l], ln_g[l], ln_b[l], w1[l], b1[l], w2[l], b2[l])
        return x
    h = _L0_tok_ref(x, L0_tok_emb0, L0_tok_emb1, L0_tok_emb2, L0_tok_emb3, L0_tok_proj0, L0_tok_proj1, L0_tok_proj2, L0_tok_proj3)
    h = h + _L0_attn_ref(_layernorm(h, axis=-1), L0_attn_Wq, L0_attn_Wk, L0_attn_Wv, L0_attn_Wo)
    h = h + _L0_ffn_ref(_layernorm(h, axis=-1), L0_ffn_moe_router, L0_ffn_moe_w13, L0_ffn_moe_w2)
    h = h + _L1_attn_ref(_layernorm(h, axis=-1), L1_attn_wq, L1_attn_wk, L1_attn_wv, L1_attn_wo, L1_attn_w_lr, L1_attn_w_target, L1_attn_w_gates, L1_attn_rms_w)
    h = h + _L1_ffn_ref(_layernorm(h, axis=-1), L1_ffn_wqkv, L1_ffn_q_scale, L1_ffn_k_scale, L1_ffn_wo, L1_ffn_ln_g, L1_ffn_ln_b, L1_ffn_w1, L1_ffn_b1, L1_ffn_w2, L1_ffn_b2)
    return h

_drawn_inputs = setup_inputs


def setup_inputs(seed=0):
    import zlib

    import numpy as np

    out = dict(_drawn_inputs(seed))
    spreads = {'L1_attn_rms_w': (1.0, 0.6),
     'L1_ffn_q_scale': (1.0, 0.6),
     'L1_ffn_k_scale': (1.0, 0.6),
     'L1_ffn_ln_g': (1.0, 0.6),
     'L1_ffn_ln_b': (0.0, 0.8),
     'L1_ffn_b1': (0.0, 0.8),
     'L1_ffn_b2': (0.0, 0.8)}
    factors = {'L0_attn_Wq': 8.0,
     'L0_attn_Wk': 8.0,
     'L0_attn_Wv': 3.689,
     'L0_attn_Wo': 3.733,
     'L0_ffn_moe_router': 5.487,
     'L0_ffn_moe_w13': 5.017,
     'L0_ffn_moe_w2': 5.046,
     'L1_attn_wq': 4.799,
     'L1_attn_wk': 4.853,
     'L1_attn_wv': 3.717,
     'L1_attn_wo': 3.757,
     'L1_attn_w_gates': 8.0,
     'L1_ffn_wqkv': 8.0,
     'L1_ffn_wo': 8.0,
     'L1_ffn_w1': 8.0,
     'L1_ffn_w2': 8.0}
    for name, (base, spread) in spreads.items():
        noise = np.random.default_rng([zlib.crc32(name.encode()), seed]).standard_normal(out[name].shape)
        drawn = base * np.exp(spread * noise) if base else spread * noise
        out[name] = jnp.asarray(drawn.astype(out[name].dtype))
    for name, factor in factors.items():
        out[name] = (out[name] * factor).astype(out[name].dtype)
    return out
```

```python
import concourse.bass as bass
from concourse import mybir
from contextlib import ExitStack
import numpy as np

F32 = mybir.dt.float32
BF16 = mybir.dt.bfloat16
I32 = mybir.dt.int32
U32 = mybir.dt.uint32
ALU = mybir.AluOpType
ACT = mybir.ActivationFunctionType
AX = mybir.AxisListType

P = 128
B, N, D = 4, 512, 256
T = N // P
NT = B * T
C = D // P
EPS_LN = 1e-5
EPS_RMS = float(np.finfo(np.float32).eps)
MASKED = -1e30

CUTOFFS = [0, 5000, 15000, 25000, 32000]
EMB_W = [256, 64, 16, 4]
EMB_AT = [0, 256, 320, 336]
EMB_K = 340
EMB_CHUNKS = [128, 128, 84]

SB_H, SB_D, SB_PAD = 16, 16, 32
MOE_E, MOE_F = 8, 512
CA_H, CA_D = 8, 64
INNER = CA_H * CA_D
DEPTH = 2
HID = 682
FC = 6
FW = [128, 128, 128, 128, 128, 42]


class Signal:

    def __init__(self, ctx, nc, name, per):
        self.sem = ctx.enter_context(nc.semaphore(name))
        self.per = per
        self.passed = 0

    def at(self, i, n):
        assert -self.per < n <= self.per, (n, self.per)
        return i * self.per + ((self.passed + 1) * self.per + n)


def batch_slice(tensor, b, t):
    return tensor[:, bass.ds(b * T + t, 1), :].rearrange("p a n -> p (a n)")


def program(nc, ids, emb, proj, sb_wq, sb_wk, sb_wv, sb_wo, router, w13, w2, ca_wq, ca_wk, ca_wv, ca_wo,
            w_gates, rms_w, trig, wqkv, qk_scale, ffn_wo, ln_g, ln_b, w1, b1, w2f, b2, out,
            stages=5):
    with ExitStack() as ctx:
        def sb(name, shape, dt=F32, where=ctx):
            return where.enter_context(nc.sbuf_tensor(name, shape, dt))

        bank = [ctx.enter_context(nc.psum_tensor(f"bank{i}", [P, 512], F32)) for i in range(8)]

        h = sb("h", [P, NT, D])
        ident = sb("ident", [P, P])
        ident_bf = sb("ident_bf", [P, P], BF16)
        scan_floor = sb("scan_floor", [P, N])
        window_mask = sb("window_mask", [P, 2, P], BF16)
        half = sb("half", [P, 16])
        one_row = sb("one_row", [1, P])
        pause = sb("pause", [P, 1])
        xn = sb("xn", [P, T, D])
        xT = sb("xT", [P, C, N + 1])
        proj_w = sb("proj_w", [P, 3, D])
        sb_w = sb("sb_w", [P, C, 2 * SB_H * SB_PAD + 2 * D])
        ca_w = sb("ca_w", [P, C, 3 * INNER])
        ca_wo_w = sb("ca_wo_w", [P, INNER // P, D])
        gates_w = sb("gates_w", [P, C, CA_H])
        router_w = sb("router_w", [P, C, MOE_E])
        rms_col = sb("rms_col", [P, C])
        b2_row = sb("b2_row", [1, DEPTH * D])
        big = sb("big", [P, MOE_E * (C * 2 * MOE_F + MOE_F // P * D)])

        W13 = big[:, 0:MOE_E * C * 2 * MOE_F].rearrange("p (e c f) -> p e c f", e=MOE_E, c=C)
        W2 = big[:, MOE_E * C * 2 * MOE_F:].rearrange("p (e c f) -> p e c f", e=MOE_E, c=MOE_F // P)

        def sem(name):
            return ctx.enter_context(nc.semaphore(name))

        loaded_sb = sem("loaded_sb")
        loaded_moe = [sem(f"loaded_moe{e}") for e in range(MOE_E)]
        loaded_ca = sem("loaded_ca")

        consts_and_embedding(nc, sb, bank, ids, emb, proj, proj_w, h, ident, ident_bf, scan_floor,
                             window_mask, half, one_row, xT,
                             [(sb_w[:, :, 0:512], sb_wq), (sb_w[:, :, 512:1024], sb_wk),
                              (sb_w[:, :, 1024:1280], sb_wv), (sb_w[:, :, 1280:1536], sb_wo)], loaded_sb)
        if stages >= 1:
            stick_breaking(nc, bank, h, pause, ident, scan_floor, half, xn, xT, sb_w, loaded_sb,
                           [(W13[:, e], w13[e], W2[:, e], w2[e], loaded_moe[e]) for e in range(MOE_E)],
                           [(router_w[:, :, :], router), (ca_w[:, :, 0:512], ca_wq),
                            (ca_w[:, :, 512:1024], ca_wk), (ca_w[:, :, 1024:1536], ca_wv),
                            (ca_wo_w[:, :, :], ca_wo), (gates_w[:, :, :], w_gates),
                            (rms_col[:, :], rms_w)], loaded_ca)
        if stages >= 2:
            experts(nc, bank, h, pause, ident, half, xn, xT, router_w, W13, W2, loaded_moe, loaded_ca)
        if stages >= 3:
            loaded_late = sem("loaded_late")
            late, _ = late_views(big)
            late["early_a"] = sb_w[:, :, :].rearrange("p c n -> p (c n)")
            late["early_b"] = ca_w[:, :, :].rearrange("p c n -> p (c n)")
            loads = late_loads(late, b2_row, wqkv, ffn_wo, w1, w2f, trig, qk_scale, ln_g, ln_b, b1, b2)
            causal(nc, bank, h, pause, ident, ident_bf, window_mask, half, xn, xT, ca_w, ca_wo_w, gates_w, rms_col, loads if stages > 3 else [],
                   loaded_late)
        kept = []
        if stages >= 4:
            late_size = sum(int(np.prod(x)) for x in LATE_SHAPES.values())
            kept = [late["early_b"][:, (b + 1) * T * D:(b + 2) * T * D] for b in range(2)]
            kept += [big[:, late_size + b * T * D:late_size + (b + 1) * T * D] for b in range(2)]
            enter_layers(nc, h, half, pause, kept)
            local_layers(nc, bank, h, pause, ident, ident_bf, window_mask, half, one_row, xn, xT, late, b2_row,
                         min(DEPTH, stages - 3), loaded_late, len(loads))
        store(nc, h, kept, out)


def enter_layers(nc, h, half, pause, kept):
    with ExitStack() as ctx:
        def st(name, shape):
            return ctx.enter_context(nc.sbuf_tensor(f"enter_{name}", shape, F32))

        stats, moments = st("stats", [P, NT, 6]), st("moments", [P, NT, 2])
        var_eps, rstd = st("var_eps", [P, NT]), st("rstd", [P, NT])
        copied = ctx.enter_context(nc.semaphore("enter_copied"))
        steps = ctx.enter_context(nc.semaphore("enter_steps"))
        rstd_done = ctx.enter_context(nc.semaphore("enter_rstd"))
        with nc.Block() as block:
            @block.scalar
            def _(act):
                for b in range(B):
                    act.activation(kept[b], h[:, b * T:(b + 1) * T, :].rearrange("p t d -> p (t d)"),
                                   ACT.Copy).then_inc(copied, 1)

            @block.gpsimd
            def _(pool):
                pool.wait_ge(steps, 2 * NT + 1)
                pool.tensor_tensor(rstd[:], var_eps[:], half[:], ALU.pow).then_inc(rstd_done, 1)

            @block.vector
            def _(dve):
                for t in range(NT):
                    dve.bn_stats(stats[:, t, :], h[:, t, :]).then_inc(steps, 1)
                dve.wait_ge(steps, NT)
                for t in range(NT):
                    dve.bn_aggr(moments[:, t, :], stats[:, t, :]).then_inc(steps, 1)
                dve.wait_ge(steps, 2 * NT)
                dve.tensor_scalar(var_eps[:], moments[:, :, 1], EPS_LN, None, ALU.add).then_inc(steps, 1)
                dve.wait_ge(rstd_done, 1)
                for t in range(NT):
                    dve.wait_ge(copied, t // T + 1)
                    dve.tensor_scalar(h[:, t, :], h[:, t, :], moments[:, t, 0:1], rstd[:, t:t + 1], ALU.subtract,
                                      ALU.mult)


def store(nc, h, kept, out):
    with ExitStack() as ctx:
        stored = ctx.enter_context(nc.semaphore("stored"))
        summed = ctx.enter_context(nc.semaphore("final_summed"))
        with nc.Block() as block:
            @block.vector
            def _(dve):
                for b in range(B if kept else 0):
                    hb = h[:, b * T:(b + 1) * T, :].rearrange("p t d -> p (t d)")
                    dve.tensor_tensor(hb, hb, kept[b], ALU.add).then_inc(summed, 1)

            @block.sync
            def _(sp):
                for b in range(B):
                    if kept:
                        sp.wait_ge(summed, b + 1)
                    sp.dma_start(out[b * N:(b + 1) * N, :].rearrange("(t p) d -> p t d", p=P),
                                 h[:, b * T:(b + 1) * T, :]).then_inc(stored, 16)
                sp.wait_ge(stored, 16 * B)


def consts_and_embedding(nc, sb, bank, ids, emb, proj, proj_w, h, ident, ident_bf, scan_floor,
                         window_mask, half, one_row, xT, weights, loaded_sb):
    with ExitStack() as ctx:
        def st(name, shape, dt=F32):
            return ctx.enter_context(nc.sbuf_tensor(name, shape, dt))

        def sem(name):
            return ctx.enter_context(nc.semaphore(name))

        ids_sb = st("ids_sb", [P, NT], I32)
        ids_f = st("ids_f", [P, NT])
        row = st("row", [P, NT])
        row_i = st("row_i", [P, NT], U32)
        at_least = st("at_least", [P, 5, NT])
        in_table = st("in_table", [P, 4, NT])
        gathered = st("gathered", [P, NT, D])
        feat = [st(f"feat{k}", [P, EMB_K]) for k in range(2)]
        featT = [st(f"featT{k}", [P, 3, P]) for k in range(2)]

        ids_in, proj_in = sem("ids_in"), sem("proj_in")
        rows_in = [sem(f"rows_in{t}") for t in range(NT)]
        made = sem("made")
        index = sem("index")
        masked = sem("masked")
        turned = sem("turned")
        turned_sb = sem("turned_sb")
        summed = sem("summed")
        kept = sem("kept")

        with nc.Block() as block:
            @block.sync
            def _(sp):
                sp.dma_start(ids_sb[:, :], ids).then_inc(ids_in, 16)
                sp.dma_start(proj_w[:, :, :], proj.rearrange("c p n -> p c n")).then_inc(proj_in, 16)
                for dst, src in weights:
                    sp.dma_start(dst, src.rearrange("(c p) n -> p c n", p=P)).then_inc(loaded_sb, 16)

            @block.gpsimd
            def _(pool):
                pool.wait_ge(index, 12)
                for t in range(NT):
                    pool.indirect_dma_start(
                        gathered[:, t, :], None, emb,
                        bass.IndirectOffsetOnAxis(ap=row_i[:, t:t + 1], axis=0)).then_inc(rows_in[t], 16)
                pool.memset(ident_bf[:], 0.0).then_inc(made, 1)
                pool.memset(scan_floor[:], 0.0).then_inc(made, 1)
                pool.memset(window_mask[:], 0.0).then_inc(made, 1)
                pool.memset(half[:], -0.5).then_inc(made, 1)
                pool.memset(one_row[:], 1.0).then_inc(made, 1)
                pool.memset(xT[:, :, 0:1], 0.0).then_inc(made, 1)
                pool.wait_ge(made, 6)
                pool.affine_select(out=ident_bf[:], in_=ident_bf[:], compare_op=ALU.not_equal, fill=1.0,
                                   base=0, pattern=[[-1, P]], channel_multiplier=1).then_inc(made, 1)
                own_key = scan_floor[:, N - P:N]
                pool.affine_select(out=own_key, in_=own_key, compare_op=ALU.not_equal, fill=1.0,
                                   base=0, pattern=[[-1, P]], channel_multiplier=1).then_inc(made, 1)
                before, own = window_mask[:, 0, :], window_mask[:, 1, :]
                pool.affine_select(out=before, in_=before, compare_op=ALU.is_ge, fill=MASKED,
                                   base=0, pattern=[[1, P]], channel_multiplier=-1).then_inc(made, 1)
                pool.affine_select(out=own, in_=own, compare_op=ALU.is_ge, fill=MASKED,
                                   base=0, pattern=[[-1, P]], channel_multiplier=1).then_inc(made, 1)

            @block.vector
            def _(dve):
                dve.memset(ident[:], 0.0).then_inc(index, 1)
                dve.wait_ge(ids_in, 16)
                dve.tensor_copy(ids_f[:], ids_sb[:]).then_inc(index, 1)
                dve.wait_ge(index, 2)
                dve.tensor_scalar(row[:], ids_f[:], 0.0, float(CUTOFFS[-1] - 1), ALU.max, ALU.min).then_inc(index, 1)
                for k in range(5):
                    dve.tensor_scalar(at_least[:, k, :], ids_f[:], float(CUTOFFS[k]), None,
                                      ALU.is_ge).then_inc(index, 1)
                dve.wait_ge(index, 8)
                for k in range(3):
                    dve.tensor_sub(in_table[:, k, :], at_least[:, k, :], at_least[:, k + 1, :]).then_inc(index, 1)
                dve.tensor_copy(row_i[:], row[:]).then_inc(index, 1)
                dve.tensor_sub(in_table[:, 3, :], at_least[:, 3, :], at_least[:, 4, :]).then_inc(index, 1)
                dve.wait_ge(index, 13)
                for t in range(NT):
                    dve.wait_ge(rows_in[t], 16)
                    if t >= 2:
                        dve.wait_ge(turned, t - 1)
                    for k in range(4):
                        last = dve.tensor_scalar(feat[t % 2][:, EMB_AT[k]:EMB_AT[k] + EMB_W[k]],
                                                 gathered[:, t, 0:EMB_W[k]], in_table[:, k, t:t + 1], None,
                                                 ALU.mult)
                    last.then_inc(masked, 1)
                    if t >= 1:
                        dve.wait_ge(summed, t)
                        dve.tensor_scalar(h[:, t - 1, :], bank[2 + (t - 1) % 2][:, 0:D], float(D) ** 0.5, None,
                                          ALU.mult).then_inc(kept, 1)
                dve.wait_ge(summed, NT)
                dve.tensor_scalar(h[:, NT - 1, :], bank[2 + (NT - 1) % 2][:, 0:D], float(D) ** 0.5, None,
                                  ALU.mult).then_inc(kept, 1)

            @block.scalar
            def _(act):
                act.wait_ge(made, 10)
                act.wait_ge(index, 1)
                act.activation(ident[:], ident_bf[:], ACT.Copy).then_inc(made, 1)
                for t in range(NT):
                    act.wait_ge(turned, t + 1)
                    if t >= 2:
                        act.wait_ge(summed, t - 1)
                    act.activation(featT[t % 2][:, 0:2, :].rearrange("p c n -> p (c n)"),
                                   bank[t % 2][:, 0:2 * P], ACT.Copy)
                    act.activation(featT[t % 2][0:EMB_CHUNKS[2], 2, :],
                                   bank[t % 2][0:EMB_CHUNKS[2], 2 * P:3 * P], ACT.Copy).then_inc(turned_sb, 1)

            @block.tensor
            def _(pe):
                pe.wait_ge(made, 11)
                pe.wait_ge(proj_in, 16)

                def project(t):
                    pe.wait_ge(turned_sb, t + 1)
                    if t >= 2:
                        pe.wait_ge(kept, t - 1)
                    for c, w in enumerate(EMB_CHUNKS):
                        last = pe.matmul(bank[2 + t % 2][:, 0:D], featT[t % 2][0:w, c, :], proj_w[0:w, c, :],
                                         start=(c == 0), stop=(c == 2))
                    last.then_inc(summed, 1)

                for t in range(NT):
                    pe.wait_ge(masked, t + 1)
                    if t >= 2:
                        pe.wait_ge(turned_sb, t - 1)
                    for c, w in enumerate(EMB_CHUNKS):
                        last = pe.transpose(bank[t % 2][0:w, c * P:(c + 1) * P],
                                            feat[t % 2][:, c * P:c * P + w], ident[:])
                    last.then_inc(turned, 1)
                    if t >= 1:
                        project(t - 1)
                project(NT - 1)


def stick_breaking(nc, bank, h, pause, ident, scan_floor, half, xn, xT, sb_w, loaded_sb, moe_loads,
                   other_loads, loaded_ca):
    UNITS = T * SB_H
    QKP = SB_H * SB_PAD // P
    wq, wk = sb_w[:, :, 0:512], sb_w[:, :, 512:1024]
    wv, wo = sb_w[:, :, 1024:1280], sb_w[:, :, 1280:1536]
    with ExitStack() as ctx:
        def st(name, shape, dt=F32):
            return ctx.enter_context(nc.sbuf_tensor(f"sb_{name}", shape, dt))

        def signal(name, per):
            return Signal(ctx, nc, name, per)

        stats, moments = st("stats", [P, T, 6]), st("moments", [P, T, 2])
        var_eps, rstd = st("var_eps", [P, T]), st("rstd", [P, T])
        qT, kT = st("qT", [P, QKP, N]), st("kT", [P, QKP, N])
        dxT = st("dxT", [P, C, N])
        v, u = st("v", [P, T, D]), st("u", [P, T, D])
        keep = [st(f"keep{i}", [P, N]) for i in range(2)]
        prod = [st(f"prod{i}", [P, N]) for i in range(3)]
        prodT = [st(f"prodT{i}", [P, N]) for i in range(2)]
        rest = [st(f"rest{i}", [P, D]) for i in range(2)]
        o = [st(f"o{i}", [P, D]) for i in range(2)]
        oT = [st(f"oT{i}", [P, C, P]) for i in range(2)]

        ps_a, ps_l, ps_t, ps_o = bank[0:2], bank[2:4], bank[4:6], bank[6:8]

        moments_done = signal("sb_moments", 9)
        rstd_done = signal("sb_rstd", 1)
        normed = signal("sb_normed", T)
        xT_ps = signal("sb_xT_ps", C)
        xT_done = signal("sb_xT", C)
        dx_done = signal("sb_dx", 1)
        proj_ps = signal("sb_proj_ps", 2 * QKP + 2 * T)
        proj_done = signal("sb_proj", 2 * QKP + 2 * T)
        logits = signal("sb_logits", UNITS)
        kept = signal("sb_keep", UNITS)
        prods = signal("sb_prods", UNITS)
        prods_t = signal("sb_prods_t", UNITS)
        prods_tc = signal("sb_prods_tc", UNITS)
        pv = signal("sb_pv", UNITS)
        rest_done = signal("sb_rest", UNITS)
        o_done = signal("sb_o", T)
        oT_ps = signal("sb_oT_ps", T)
        oT_done = signal("sb_oT", T)
        out_ps = signal("sb_out_ps", T)
        h_done = signal("sb_h", T)
        every = [moments_done, rstd_done, normed, xT_ps, xT_done, dx_done, proj_ps, proj_done, logits, kept,
                 prods, prods_t, prods_tc, pv, rest_done, o_done, oT_ps, oT_done, out_ps, h_done]

        TAIL = 4

        with nc.Block() as block:
            @block.sync
            def _(sp):
                for s in every:
                    sp.sem_inc(s.sem, s.per)
                for dst, src in other_loads:
                    sp.dma_start(dst, src if len(dst.shape) == 2 else src.rearrange("(c p) n -> p c n", p=P)).then_inc(loaded_ca, 16)
                for d13, s13, d2, s2, s in moe_loads:
                    sp.dma_start(d13, s13.rearrange("(c p) n -> p c n", p=P)).then_inc(s, 16)
                    sp.dma_start(d2, s2.rearrange("(c p) n -> p c n", p=P)).then_inc(s, 16)

            @block.gpsimd
            def _(pool):
                with pool.Fori(0, B) as b:
                    pool.wait_ge(moments_done.sem, moments_done.at(b, 9))
                    pool.tensor_tensor(rstd[:], var_eps[:], half[:, 0:T], ALU.pow).then_inc(rstd_done.sem, 1)
                    for n in range(UNITS):
                        i, hd = n // SB_H, n % SB_H
                        cols = slice(hd * SB_D, (hd + 1) * SB_D)
                        if n == 0:
                            pool.wait_ge(proj_done.sem, proj_done.at(b, 2 * QKP + T))
                        if hd == 0:
                            pool.wait_ge(o_done.sem, o_done.at(b, i + 1 - 2))
                        pool.wait_ge(prods.sem, prods.at(b, n + 1))
                        pool.tensor_tensor(rest[i % 2][:, cols], v[:, i, cols],
                                           prod[n % 3][:, 0:1].to_broadcast([P, SB_D]), ALU.mult).then_inc(rest_done.sem, 1)

            @block.vector
            def _(dve):
                def finish(b, i):
                    dve.wait_ge(pv.sem, pv.at(b, (i + 1) * SB_H))
                    dve.wait_ge(rest_done.sem, rest_done.at(b, (i + 1) * SB_H))
                    dve.wait_ge(oT_ps.sem, oT_ps.at(b, i + 1 - 2))
                    dve.tensor_tensor(o[i % 2][:], ps_o[i % 2][:, 0:D], rest[i % 2][:], ALU.add).then_inc(o_done.sem, 1)

                def add(b, i):
                    dve.wait_ge(out_ps.sem, out_ps.at(b, i + 1))
                    hs = batch_slice(h, b, i)
                    dve.tensor_tensor(hs, ps_a[1][:, 0:D], hs, ALU.add).then_inc(h_done.sem, 1)

                with dve.Fori(0, B) as b:
                    layer_norm(dve, b, h, pause, stats, moments, var_eps, rstd, xn, moments_done, rstd_done, normed,
                               xT_ps, xT_ps.at(b, 0))
                    dve.wait_ge(xT_done.sem, xT_done.at(b, C))
                    dve.wait_ge(proj_ps.sem, proj_ps.at(b, 0))
                    dve.tensor_tensor(dxT[:, :, :], xT[:, :, 0:N], xT[:, :, 1:N + 1], ALU.subtract).then_inc(dx_done.sem, 1)
                    for n in range(UNITS):
                        w = (n // SB_H + 1) * P
                        dve.wait_ge(kept.sem, kept.at(b, n + 1))
                        dve.wait_ge(prods_t.sem, prods_t.at(b, n + 1 - 3))
                        dve.wait_ge(rest_done.sem, rest_done.at(b, n + 1 - 3))
                        dve.tensor_tensor_scan(prod[n % 3][:, 0:w][:, ::-1], keep[n % 2][:, 0:w][:, ::-1],
                                               scan_floor[:, N - w:N][:, ::-1], 0.0, ALU.mult,
                                               ALU.max).then_inc(prods.sem, 1)
                        if n >= SB_H and n % SB_H == TAIL:
                            finish(b, n // SB_H - 1)
                        if n >= SB_H and n % SB_H == TAIL + 4:
                            add(b, n // SB_H - 1)
                    finish(b, T - 1)
                    add(b, T - 1)

            @block.scalar
            def _(act):
                def copy_t(b, n):
                    w = (n // SB_H + 1) * P
                    act.wait_ge(prods_t.sem, prods_t.at(b, n + 1))
                    act.wait_ge(pv.sem, pv.at(b, n + 1 - 2))
                    act.activation(prodT[n % 2][:, 0:w], ps_t[n % 2][:, 0:w], ACT.Copy).then_inc(prods_tc.sem, 1)

                def copy_o(b, i):
                    act.wait_ge(oT_ps.sem, oT_ps.at(b, i + 1))
                    act.wait_ge(out_ps.sem, out_ps.at(b, i + 1 - 2))
                    act.activation(oT[i % 2][:, :, :].rearrange("p c n -> p (c n)"), ps_a[0][:, 0:D],
                                   ACT.Copy).then_inc(oT_done.sem, 1)

                with act.Fori(0, B) as b:
                    for c in range(C):
                        act.wait_ge(xT_ps.sem, xT_ps.at(b, c + 1))
                        if c == 0:
                            act.wait_ge(proj_ps.sem, proj_ps.at(b, 0))
                            act.wait_ge(dx_done.sem, dx_done.at(b, 0))
                        act.activation(xT[:, c, 1:N + 1], ps_a[c][:], ACT.Copy).then_inc(xT_done.sem, 1)
                    for k in range(2 * QKP + 2 * T):
                        act.wait_ge(proj_ps.sem, proj_ps.at(b, k + 1))
                        if k == 0:
                            act.wait_ge(logits.sem, logits.at(b, 0))
                        if k < 2 * QKP:
                            dst = (qT if k < QKP else kT)[:, k % QKP, :]
                            src = ps_a[k % 2][:]
                        else:
                            if k == 2 * QKP:
                                act.wait_ge(pv.sem, pv.at(b, 0))
                                act.wait_ge(rest_done.sem, rest_done.at(b, 0))
                            m = k - 2 * QKP
                            dst = (v if m < T else u)[:, m % T, :]
                            src = ps_a[k % 2][:, 0:D]
                        act.activation(dst, src, ACT.Copy).then_inc(proj_done.sem, 1)
                    for n in range(UNITS + 2):
                        if n < UNITS:
                            w = (n // SB_H + 1) * P
                            act.wait_ge(logits.sem, logits.at(b, n + 1))
                            act.wait_ge(prods.sem, prods.at(b, n + 1 - 2))
                            act.activation(keep[n % 2][:, 0:w], ps_l[n % 2][:, 0:w], ACT.Sigmoid,
                                           scale=-float(SB_D) ** -0.5).then_inc(kept.sem, 1)
                        if n >= 2:
                            copy_t(b, n - 2)
                        if n >= SB_H and n % SB_H == TAIL + 2 and n < UNITS:
                            copy_o(b, n // SB_H - 1)
                    copy_o(b, T - 1)

            @block.tensor
            def _(pe):
                def transposes(b, n):
                    i = n // SB_H
                    pe.wait_ge(prods.sem, prods.at(b, n + 1))
                    pe.wait_ge(prods_tc.sem, prods_tc.at(b, n + 1 - 2))
                    for c in range(i + 1):
                        last = pe.transpose(ps_t[n % 2][:, c * P:(c + 1) * P], prod[n % 3][:, c * P:(c + 1) * P],
                                            ident[:])
                    last.then_inc(prods_t.sem, 1)

                def weigh(b, n):
                    i, hd = n // SB_H, n % SB_H
                    if hd == 0:
                        pe.wait_ge(o_done.sem, o_done.at(b, i + 1 - 2))
                    pe.wait_ge(prods_tc.sem, prods_tc.at(b, n + 1))
                    for c in range(i + 1):
                        last = pe.matmul(ps_o[i % 2][:, hd * SB_D:(hd + 1) * SB_D],
                                         prodT[n % 2][:, c * P:(c + 1) * P], u[:, c, hd * SB_D:(hd + 1) * SB_D],
                                         start=(hd == 0 and c == 0), stop=False, skip_group_check=True)
                    if hd == SB_H - 1:
                        last = pe.matmul(ps_o[i % 2][:, 0:D], ident[:], v[:, i, :], start=False, stop=True,
                                         skip_group_check=True)
                    last.then_inc(pv.sem, 1)

                def turn_o(b, i):
                    pe.wait_ge(o_done.sem, o_done.at(b, i + 1))
                    if i == 0:
                        pe.wait_ge(proj_done.sem, proj_done.at(b, 2 * QKP + 2 * T))
                    pe.wait_ge(oT_done.sem, oT_done.at(b, i))
                    for c in range(C):
                        last = pe.transpose(ps_a[0][:, c * P:(c + 1) * P], o[i % 2][:, c * P:(c + 1) * P], ident[:])
                    last.then_inc(oT_ps.sem, 1)

                def project_o(b, i):
                    pe.wait_ge(oT_done.sem, oT_done.at(b, i + 1))
                    pe.wait_ge(h_done.sem, h_done.at(b, i))
                    for c in range(C):
                        last = pe.matmul(ps_a[1][:, 0:D], oT[i % 2][:, c, :], wo[:, c, :],
                                         start=(c == 0), stop=(c == C - 1))
                    last.then_inc(out_ps.sem, 1)

                pe.wait_ge(loaded_sb, 16 * 4)
                with pe.Fori(0, B) as b:
                    pe.wait_ge(oT_done.sem, oT_done.at(b, 0))
                    pe.wait_ge(h_done.sem, h_done.at(b, 0))
                    turn_x(pe, b, xn, ident, ps_a, normed, xT_ps)
                    for k in range(2 * QKP + 2 * T):
                        if k == 0:
                            pe.wait_ge(xT_done.sem, xT_done.at(b, C))
                        if k == 2 * QKP + T:
                            pe.wait_ge(dx_done.sem, dx_done.at(b, 1))
                        if k >= 2:
                            pe.wait_ge(proj_done.sem, proj_done.at(b, k - 1))
                        for c in range(C):
                            if k < 2 * QKP:
                                m = k % QKP
                                last = pe.matmul(ps_a[k % 2][:], (wq if k < QKP else wk)[:, c, m * P:(m + 1) * P],
                                                 xT[:, c, 1:N + 1], start=(c == 0), stop=(c == C - 1))
                            else:
                                m = (k - 2 * QKP) % T
                                src = xT[:, c, 1 + m * P:1 + (m + 1) * P] if k < 2 * QKP + T else dxT[:, c, m * P:(m + 1) * P]
                                last = pe.matmul(ps_a[k % 2][:, 0:D], src, wv[:, c, :], start=(c == 0), stop=(c == C - 1))
                        last.then_inc(proj_ps.sem, 1)
                    pe.wait_ge(proj_done.sem, proj_done.at(b, 2 * QKP + 2 * T))
                    for n in range(UNITS + 3):
                        if n < UNITS:
                            i, hd = n // SB_H, n % SB_H
                            row, ch = hd % 4 * SB_PAD, hd // 4
                            pe.wait_ge(kept.sem, kept.at(b, n + 1 - 2))
                            pe.matmul(ps_l[n % 2][:, 0:(i + 1) * P], qT[row:row + SB_PAD, ch, i * P:(i + 1) * P],
                                      kT[row:row + SB_PAD, ch, 0:(i + 1) * P], start=True,
                                      stop=True).then_inc(logits.sem, 1)
                        if 2 <= n < UNITS + 2:
                            transposes(b, n - 2)
                        if n >= 3:
                            weigh(b, n - 3)
                        if n >= SB_H and n % SB_H == TAIL + 1 and n < UNITS:
                            turn_o(b, n // SB_H - 1)
                        if n >= SB_H and n % SB_H == TAIL + 3 and n < UNITS:
                            project_o(b, n // SB_H - 1)
                    turn_o(b, T - 1)
                    project_o(b, T - 1)


def layer_norm(dve, b, h, pause, stats, moments, var_eps, rstd, xn, moments_done, rstd_done, normed, xn_read,
               xn_read_at):
    for t in range(T):
        dve.bn_stats(stats[:, t, :], batch_slice(h, b, t)).then_inc(moments_done.sem, 1)
    dve.wait_ge(moments_done.sem, moments_done.at(b, T))
    dve.memset(pause[:], 0.0)
    for t in range(T):
        dve.bn_aggr(moments[:, t, :], stats[:, t, :]).then_inc(moments_done.sem, 1)
    dve.wait_ge(moments_done.sem, moments_done.at(b, 2 * T))
    dve.tensor_scalar(var_eps[:], moments[:, :, 1], EPS_LN, None, ALU.add).then_inc(moments_done.sem, 1)
    dve.wait_ge(rstd_done.sem, rstd_done.at(b, 1))
    dve.wait_ge(xn_read.sem, xn_read_at)
    for t in range(T):
        dve.tensor_scalar(xn[:, t, :], batch_slice(h, b, t), moments[:, t, 0:1], rstd[:, t:t + 1],
                          ALU.subtract, ALU.mult).then_inc(normed.sem, 1)


def turn_x(pe, b, xn, ident, banks, normed, xT_ps):
    for c in range(C):
        for t in range(T):
            if c == 0:
                pe.wait_ge(normed.sem, normed.at(b, t + 1))
            last = pe.transpose(banks[c][:, t * P:(t + 1) * P], xn[:, t, c * P:(c + 1) * P], ident[:])
        last.then_inc(xT_ps.sem, 1)


def experts(nc, bank, h, pause, ident, half, xn, xT, router_w, W13, W2, loaded_moe, loaded_ca):
    CHUNKS = MOE_E * (MOE_F // P)
    FCH = MOE_F // P
    DOWNS = MOE_E * T
    with ExitStack() as ctx:
        def st(name, shape, dt=F32):
            return ctx.enter_context(nc.sbuf_tensor(f"moe_{name}", shape, dt))

        def signal(name, per):
            return Signal(ctx, nc, name, per)

        stats, moments = st("stats", [P, T, 6]), st("moments", [P, T, 2])
        var_eps, rstd = st("var_eps", [P, T]), st("rstd", [P, T])
        numbers_i = st("numbers_i", [P, MOE_E], I32)
        numbers = st("numbers", [P, MOE_E])
        best = st("best", [P, T, MOE_E])
        best_at = st("best_at", [P, T, MOE_E], U32)
        best_f = st("best_f", [P, T, MOE_E])
        gap = st("gap", [P, T])
        share = st("share", [P, 2, T])
        picked = st("picked", [P, 2, T, MOE_E])
        weight = st("weight", [P, T, MOE_E])
        act_gate = [st(f"act_gate{i}", [P, N]) for i in range(2)]
        hidden = [st(f"hidden{i}", [P, FCH, N]) for i in range(2)]

        ps_x, ps_g, ps_d = bank[0:2], bank[2:6], bank[6:8]

        moments_done = signal("moe_moments", 9)
        rstd_done = signal("moe_rstd", 1)
        normed = signal("moe_normed", T)
        xT_ps = signal("moe_xT_ps", C)
        xT_done = signal("moe_xT", C)
        routed = signal("moe_routed", 1)
        route = signal("moe_route", 5 * T + 2)
        shares = signal("moe_shares", 2)
        up_ps = signal("moe_up_ps", CHUNKS)
        gated = signal("moe_gated", CHUNKS)
        hid = signal("moe_hidden", CHUNKS)
        down_ps = signal("moe_down_ps", DOWNS)
        h_done = signal("moe_h", DOWNS)
        numbered = ctx.enter_context(nc.semaphore("moe_numbered"))
        every = [moments_done, rstd_done, normed, xT_ps, xT_done, routed, route, shares, up_ps, gated, hid,
                 down_ps, h_done]

        with nc.Block() as block:
            @block.sync
            def _(sp):
                for s in every:
                    sp.sem_inc(s.sem, s.per)

            @block.gpsimd
            def _(pool):
                pool.iota(numbers_i[:], pattern=[[1, MOE_E]], base=0, channel_multiplier=0).then_inc(numbered, 1)
                pool.wait_ge(numbered, 1)
                pool.tensor_copy(numbers[:], numbers_i[:]).then_inc(numbered, 1)
                with pool.Fori(0, B) as b:
                    pool.wait_ge(moments_done.sem, moments_done.at(b, 9))
                    pool.tensor_tensor(rstd[:], var_eps[:], half[:, 0:T], ALU.pow).then_inc(rstd_done.sem, 1)

            @block.vector
            def _(dve):
                def hide(b, n):
                    e, fc = n // FCH, n % FCH
                    dve.wait_ge(gated.sem, gated.at(b, n + 1))
                    dve.wait_ge(down_ps.sem, down_ps.at(b, (e - 1) * T))
                    dve.tensor_tensor(hidden[e % 2][:, fc, :], ps_g[2 * (n % 2) + 1][:], act_gate[n % 2][:],
                                      ALU.mult).then_inc(hid.sem, 1)

                def add(b, k):
                    e, t = k // T, k % T
                    dve.wait_ge(down_ps.sem, down_ps.at(b, k + 1))
                    dve.wait_ge(h_done.sem, h_done.at(b, k + 1 - T))
                    hs = batch_slice(h, b, t)
                    dve.scalar_tensor_tensor(hs, ps_d[k % 2][:, 0:D], weight[:, t, e:e + 1], hs, ALU.mult,
                                             ALU.add).then_inc(h_done.sem, 1)

                dve.wait_ge(numbered, 2)
                with dve.Fori(0, B) as b:
                    layer_norm(dve, b, h, pause, stats, moments, var_eps, rstd, xn, moments_done, rstd_done, normed,
                               xT_ps, xT_ps.at(b, 0))
                    dve.wait_ge(routed.sem, routed.at(b, 1))
                    dve.memset(pause[:], 0.0)
                    for t in range(T):
                        dve.max(best[:, t, :], ps_x[0][:, t * MOE_E:(t + 1) * MOE_E]).then_inc(route.sem, 1)
                    dve.wait_ge(route.sem, route.at(b, T))
                    dve.tensor_sub(gap[:], best[:, :, 1], best[:, :, 0]).then_inc(route.sem, 1)
                    for t in range(T):
                        dve.max_index(best_at[:, t, :], best[:, t, :],
                                      ps_x[0][:, t * MOE_E:(t + 1) * MOE_E]).then_inc(route.sem, 1)
                    dve.wait_ge(route.sem, route.at(b, 2 * T + 1))
                    dve.tensor_copy(best_f[:, :, :], best_at[:, :, :]).then_inc(route.sem, 1)
                    dve.wait_ge(route.sem, route.at(b, 2 * T + 2))
                    dve.wait_ge(shares.sem, shares.at(b, 2))
                    for t in range(T):
                        for k in range(2):
                            dve.tensor_scalar(picked[:, k, t, :], numbers[:], best_f[:, t, k:k + 1],
                                              share[:, k, t:t + 1], ALU.is_equal, ALU.mult).then_inc(route.sem, 1)
                    dve.wait_ge(route.sem, route.at(b, 4 * T + 2))
                    for t in range(T):
                        dve.tensor_tensor(weight[:, t, :], picked[:, 0, t, :], picked[:, 1, t, :],
                                          ALU.add).then_inc(route.sem, 1)
                    for e in range(MOE_E + 1):
                        for m in range(FCH):
                            if e < MOE_E:
                                hide(b, e * FCH + m)
                            if e >= 1:
                                if e == 1 and m == 0:
                                    dve.wait_ge(route.sem, route.at(b, 5 * T + 2))
                                add(b, (e - 1) * T + m)

            @block.scalar
            def _(act):
                with act.Fori(0, B) as b:
                    for c in range(C):
                        act.wait_ge(xT_ps.sem, xT_ps.at(b, c + 1))
                        act.wait_ge(up_ps.sem, up_ps.at(b, 0))
                        act.activation(xT[:, c, 1:N + 1], ps_x[c][:], ACT.Copy).then_inc(xT_done.sem, 1)
                    act.wait_ge(route.sem, route.at(b, T + 1))
                    act.activation(share[:, 0, :], gap[:], ACT.Sigmoid, scale=-1.0).then_inc(shares.sem, 1)
                    act.activation(share[:, 1, :], gap[:], ACT.Sigmoid).then_inc(shares.sem, 1)
                    for n in range(CHUNKS):
                        act.wait_ge(up_ps.sem, up_ps.at(b, n + 1))
                        act.wait_ge(hid.sem, hid.at(b, n + 1 - 2))
                        act.activation(act_gate[n % 2][:], ps_g[2 * (n % 2)][:], ACT.Silu).then_inc(gated.sem, 1)

            @block.tensor
            def _(pe):
                def up(b, n):
                    e, fc = n // FCH, n % FCH
                    pe.wait_ge(hid.sem, hid.at(b, n + 1 - 2))
                    for part in range(2):
                        for c in range(C):
                            last = pe.matmul(ps_g[2 * (n % 2) + part][:],
                                             W13[:, e, c, part * MOE_F + fc * P:part * MOE_F + (fc + 1) * P],
                                             xT[:, c, 1:N + 1], start=(c == 0), stop=(c == C - 1))
                    last.then_inc(up_ps.sem, 1)

                def down(b, k):
                    e, t = k // T, k % T
                    pe.wait_ge(hid.sem, hid.at(b, (e + 1) * FCH))
                    pe.wait_ge(h_done.sem, h_done.at(b, k + 1 - 2))
                    for fc in range(FCH):
                        last = pe.matmul(ps_d[k % 2][:, 0:D], hidden[e % 2][:, fc, t * P:(t + 1) * P],
                                         W2[:, e, fc, :], start=(fc == 0), stop=(fc == FCH - 1))
                    last.then_inc(down_ps.sem, 1)

                pe.wait_ge(loaded_ca, 16 * 7)
                for e in range(MOE_E):
                    pe.wait_ge(loaded_moe[e], 32)
                with pe.Fori(0, B) as b:
                    pe.wait_ge(xT_done.sem, xT_done.at(b, 0))
                    pe.wait_ge(route.sem, route.at(b, 0))
                    turn_x(pe, b, xn, ident, ps_x, normed, xT_ps)
                    pe.wait_ge(xT_done.sem, xT_done.at(b, C))
                    for t in range(T):
                        for c in range(C):
                            last = pe.matmul(ps_x[0][:, t * MOE_E:(t + 1) * MOE_E],
                                             xT[:, c, 1 + t * P:1 + (t + 1) * P], router_w[:, c, :],
                                             start=(c == 0), stop=(c == C - 1))
                    last.then_inc(routed.sem, 1)
                    for e in range(MOE_E + 1):
                        for m in range(FCH):
                            if e < MOE_E:
                                up(b, e * FCH + m)
                            if e >= 1:
                                down(b, (e - 1) * T + m)


class Attention:

    def __init__(self, ctx, nc, bank, name, keys, masks, gated, ident, ident_bf, window_mask, wo):
        def st(what, shape):
            return ctx.enter_context(nc.sbuf_tensor(f"{name}_{what}", shape, F32))

        def signal(what, per):
            return Signal(ctx, nc, f"{name}_{what}", per)

        self.keys, self.masks = keys, masks
        self.ident, self.ident_bf, self.window_mask, self.wo = ident, ident_bf, window_mask, wo
        self.UNITS = T * CA_H
        self.qT, self.kT = st("qT", [P, INNER // P, N]), st("kT", [P, INNER // P, N])
        self.v = st("v", [P, T, INNER])
        self.neg_max = st("neg_max", [P, T * CA_H])
        self.sums = st("sums", [P, T, CA_H])
        self.scales = st("scales", [P, T, CA_H])
        self.prob = [st(f"prob{i}", [P, N]) for i in range(3)]
        self.probT = [st(f"probT{i}", [P, N]) for i in range(2)]
        self.o = [st(f"o{i}", [P, INNER]) for i in range(2)]
        self.oT = [st(f"oT{i}", [P, INNER // P, P]) for i in range(2)]
        self.ps_a, self.ps_l, self.ps_t, self.ps_o = bank[0:2], bank[2:4], bank[4:6], bank[6:8]
        self.logits = signal("logits", self.UNITS)
        self.maxed = signal("maxed", self.UNITS)
        self.probs = signal("probs", self.UNITS)
        self.probs_t = signal("probs_t", self.UNITS)
        self.probs_tc = signal("probs_tc", self.UNITS)
        self.pv = signal("pv", self.UNITS)
        self.steps = 1 + gated
        self.scaled = signal("scaled", self.steps * T)
        self.o_done = signal("o", T)
        self.oT_ps = signal("oT_ps", T)
        self.oT_done = signal("oT", T)
        self.out_ps = signal("out_ps", T)
        self.h_done = signal("h", T)
        self.every = [self.logits, self.maxed, self.probs, self.probs_t, self.probs_tc, self.pv, self.scaled,
                      self.o_done, self.oT_ps, self.oT_done, self.out_ps, self.h_done]


TAIL = 3


def attend_pe(pe, b, a):
    def transposes(n):
        w = len(a.keys(n // CA_H))
        pe.wait_ge(a.probs.sem, a.probs.at(b, n + 1))
        pe.wait_ge(a.probs_tc.sem, a.probs_tc.at(b, n + 1 - 2))
        for c in range(w):
            last = pe.transpose(a.ps_t[n % 2][:, c * P:(c + 1) * P], a.prob[n % 3][:, c * P:(c + 1) * P],
                                a.ident[:])
        last.then_inc(a.probs_t.sem, 1)

    def weigh(n):
        i, hd = n // CA_H, n % CA_H
        if hd == 0:
            pe.wait_ge(a.o_done.sem, a.o_done.at(b, i + 1 - 2))
        pe.wait_ge(a.probs_tc.sem, a.probs_tc.at(b, n + 1))
        keys = a.keys(i)
        for c, key in enumerate(keys):
            last = pe.matmul(a.ps_o[i % 2][:, hd * CA_D:(hd + 1) * CA_D], a.probT[n % 2][:, c * P:(c + 1) * P],
                             a.v[:, key, hd * CA_D:(hd + 1) * CA_D], start=(c == 0), stop=(c == len(keys) - 1))
        last.then_inc(a.pv.sem, 1)

    def turn_o(i):
        pe.wait_ge(a.o_done.sem, a.o_done.at(b, i + 1))
        pe.wait_ge(a.oT_done.sem, a.oT_done.at(b, i))
        for c in range(INNER // P):
            last = pe.transpose(a.ps_a[0][:, c * P:(c + 1) * P], a.o[i % 2][:, c * P:(c + 1) * P], a.ident[:])
        last.then_inc(a.oT_ps.sem, 1)

    def project_o(i):
        pe.wait_ge(a.oT_done.sem, a.oT_done.at(b, i + 1))
        pe.wait_ge(a.h_done.sem, a.h_done.at(b, i))
        for c in range(INNER // P):
            last = pe.matmul(a.ps_a[1][:, 0:D], a.oT[i % 2][:, c, :], a.wo[:, c, :], start=(c == 0),
                             stop=(c == INNER // P - 1))
        last.then_inc(a.out_ps.sem, 1)

    for n in range(a.UNITS + 3):
        if n < a.UNITS:
            i, hd = n // CA_H, n % CA_H
            keys, m = a.keys(i), a.masks(i)
            w = len(keys) * P
            row, ch = hd % 2 * CA_D, hd // 2
            pe.wait_ge(a.probs.sem, a.probs.at(b, n + 1 - 2))
            q = a.qT[row:row + CA_D, ch, i * P:(i + 1) * P]
            cut, first = w - m * P, keys[0] * P
            if cut:
                pe.matmul(a.ps_l[n % 2][:, 0:cut], q, a.kT[row:row + CA_D, ch, first:first + cut], start=True,
                          stop=True)
            pe.matmul(a.ps_l[n % 2][:, cut:w], a.ident_bf[:],
                      a.window_mask[:, 2 - m:2, :].rearrange("p m k -> p (m k)"), start=True, stop=False)
            pe.matmul(a.ps_l[n % 2][:, cut:w], q, a.kT[row:row + CA_D, ch, first + cut:first + w], start=False,
                      stop=True).then_inc(a.logits.sem, 1)
        if 2 <= n < a.UNITS + 2:
            transposes(n - 2)
        if n >= 3:
            weigh(n - 3)
        if n >= CA_H and n % CA_H == TAIL + 1 and n < a.UNITS:
            turn_o(n // CA_H - 1)
        if n >= CA_H and n % CA_H == TAIL + 3 and n < a.UNITS:
            project_o(n // CA_H - 1)
    turn_o(T - 1)
    project_o(T - 1)


def attend_act(act, b, a):
    def copy_o(i):
        act.wait_ge(a.oT_ps.sem, a.oT_ps.at(b, i + 1))
        act.wait_ge(a.out_ps.sem, a.out_ps.at(b, i + 1 - 2))
        act.activation(a.oT[i % 2][:, :, :].rearrange("p c n -> p (c n)"), a.ps_a[0][:], ACT.Copy).then_inc(a.oT_done.sem, 1)

    for n in range(a.UNITS):
        i, hd = n // CA_H, n % CA_H
        w = len(a.keys(i)) * P
        act.wait_ge(a.maxed.sem, a.maxed.at(b, n + 1))
        act.wait_ge(a.probs_t.sem, a.probs_t.at(b, n + 1 - 3))
        act.activation(a.prob[n % 3][:, 0:w], a.ps_l[n % 2][:, 0:w], ACT.Exp, bias=a.neg_max[:, n:n + 1],
                       accum_out=a.sums[:, i, hd:hd + 1]).then_inc(a.probs.sem, 1)
        if n >= CA_H and n % CA_H == TAIL + 2:
            copy_o(n // CA_H - 1)
    copy_o(T - 1)


def attend_dve(dve, b, a, h, gate):
    def copy_t(n):
        w = len(a.keys(n // CA_H)) * P
        dve.wait_ge(a.probs_t.sem, a.probs_t.at(b, n + 1))
        dve.wait_ge(a.pv.sem, a.pv.at(b, n + 1 - 2))
        dve.tensor_copy(a.probT[n % 2][:, 0:w], a.ps_t[n % 2][:, 0:w]).then_inc(a.probs_tc.sem, 1)

    def finish(i):
        dve.wait_ge(a.pv.sem, a.pv.at(b, (i + 1) * CA_H))
        dve.reciprocal(a.scales[:, i, :], a.sums[:, i, :]).then_inc(a.scaled.sem, 1)
        dve.wait_ge(a.scaled.sem, a.scaled.at(b, a.steps * i + 1))
        if gate is not None:
            dve.tensor_tensor(a.scales[:, i, :], a.scales[:, i, :], gate[:, i, :], ALU.mult).then_inc(a.scaled.sem, 1)
            dve.wait_ge(a.scaled.sem, a.scaled.at(b, a.steps * i + 2))
        dve.wait_ge(a.oT_ps.sem, a.oT_ps.at(b, i + 1 - 2))
        dve.tensor_tensor(a.o[i % 2][:].rearrange("p (h d) -> p h d", h=CA_H),
                          a.ps_o[i % 2][:].rearrange("p (h d) -> p h d", h=CA_H),
                          a.scales[:, i, :].unsqueeze(2).to_broadcast([P, CA_H, CA_D]),
                          ALU.mult).then_inc(a.o_done.sem, 1)

    def add(i):
        dve.wait_ge(a.out_ps.sem, a.out_ps.at(b, i + 1))
        hs = batch_slice(h, b, i)
        dve.tensor_tensor(hs, a.ps_a[1][:, 0:D], hs, ALU.add).then_inc(a.h_done.sem, 1)

    for n in range(a.UNITS + 2):
        if n < a.UNITS:
            w = len(a.keys(n // CA_H)) * P
            dve.wait_ge(a.probs.sem, a.probs.at(b, 0))
            dve.wait_ge(a.logits.sem, a.logits.at(b, n + 1))
            dve.tensor_reduce(a.neg_max[:, n:n + 1], a.ps_l[n % 2][:, 0:w], AX.X, ALU.max,
                              negate=True).then_inc(a.maxed.sem, 1)
        if n >= 2:
            copy_t(n - 2)
        if n >= CA_H and n % CA_H == TAIL and n < a.UNITS:
            finish(n // CA_H - 1)
        if n >= CA_H and n % CA_H == TAIL + 4 and n < a.UNITS:
            add(n // CA_H - 1)
    finish(T - 1)
    add(T - 1)


def causal(nc, bank, h, pause, ident, ident_bf, window_mask, half, xn, xT, ca_w, ca_wo_w, gates_w, rms_col, late_loads,
           loaded_late):
    QC = INNER // P
    PROJ = 2 * QC + T + 1
    with ExitStack() as ctx:
        def st(name, shape, dt=F32):
            return ctx.enter_context(nc.sbuf_tensor(f"ca_{name}", shape, dt))

        def signal(name, per):
            return Signal(ctx, nc, name, per)

        a = Attention(ctx, nc, bank, "ca", lambda i: list(range(i + 1)), lambda i: 1, True, ident, ident_bf,
                      window_mask, ca_wo_w)
        stats, moments = st("stats", [P, T, 6]), st("moments", [P, T, 2])
        var_eps, rstd = st("var_eps", [P, T]), st("rstd", [P, T])
        squares, sum_sq = st("squares", [P, T, D]), st("sum_sq", [P, T])
        mean_sq, rrms = st("mean_sq", [P, T]), st("rrms", [P, T])
        gate_e, gate = st("gate_e", [P, T, CA_H]), st("gate", [P, T, CA_H])

        moments_done = signal("ca_moments", 9)
        rstd_done = signal("ca_rstd", 1)
        normed = signal("ca_normed", T)
        squared = signal("ca_squared", T)
        mean_done = signal("ca_mean_sq", 1)
        rrms_done = signal("ca_rrms", 1)
        rms_normed = signal("ca_rms_normed", T)
        xT_ps = signal("ca_xT_ps", C)
        xT_done = signal("ca_xT", C)
        proj_ps = signal("ca_proj_ps", PROJ)
        proj_done = signal("ca_proj", PROJ)
        gate_done = signal("ca_gate", 2)
        every = [moments_done, rstd_done, normed, squared, mean_done, rrms_done, rms_normed, xT_ps, xT_done,
                 proj_ps, proj_done, gate_done] + a.every

        with nc.Block() as block:
            @block.sync
            def _(sp):
                for s in every:
                    sp.sem_inc(s.sem, s.per)
                for dst, src in late_loads:
                    sp.dma_start(dst, src).then_inc(loaded_late, 16)

            @block.gpsimd
            def _(pool):
                with pool.Fori(0, B) as b:
                    pool.wait_ge(moments_done.sem, moments_done.at(b, 9))
                    pool.tensor_tensor(rstd[:], var_eps[:], half[:, 0:T], ALU.pow).then_inc(rstd_done.sem, 1)
                    pool.wait_ge(mean_done.sem, mean_done.at(b, 1))
                    pool.tensor_tensor(rrms[:], mean_sq[:], half[:, 0:T], ALU.pow).then_inc(rrms_done.sem, 1)

            @block.vector
            def _(dve):
                with dve.Fori(0, B) as b:
                    layer_norm(dve, b, h, pause, stats, moments, var_eps, rstd, xn, moments_done, rstd_done, normed,
                               xT_ps, xT_ps.at(b, 0))
                    dve.wait_ge(squared.sem, squared.at(b, T))
                    dve.tensor_scalar(mean_sq[:], sum_sq[:], 1.0 / D, EPS_RMS, ALU.mult,
                                      ALU.add).then_inc(mean_done.sem, 1)
                    dve.wait_ge(rrms_done.sem, rrms_done.at(b, 1))
                    for t in range(T):
                        dve.tensor_scalar(xn[:, t, :], xn[:, t, :], rrms[:, t:t + 1], None,
                                          ALU.mult).then_inc(rms_normed.sem, 1)
                    dve.wait_ge(proj_done.sem, proj_done.at(b, PROJ))
                    dve.tensor_scalar(gate_e[:, :, :], gate_e[:, :, :], 1.0, None, ALU.add).then_inc(gate_done.sem, 1)
                    dve.wait_ge(gate_done.sem, gate_done.at(b, 1))
                    dve.reciprocal(gate[:, :, :], gate_e[:, :, :]).then_inc(gate_done.sem, 1)
                    dve.wait_ge(gate_done.sem, gate_done.at(b, 2))
                    attend_dve(dve, b, a, h, gate)

            @block.scalar
            def _(act):
                with act.Fori(0, B) as b:
                    for t in range(T):
                        act.wait_ge(normed.sem, normed.at(b, t + 1))
                        if t == 0:
                            act.wait_ge(mean_done.sem, mean_done.at(b, 0))
                        act.activation(squares[:, t, :], xn[:, t, :], ACT.Square,
                                       accum_out=sum_sq[:, t:t + 1]).then_inc(squared.sem, 1)
                    for c in range(C):
                        act.wait_ge(proj_ps.sem, proj_ps.at(b, 0))
                        act.wait_ge(xT_ps.sem, xT_ps.at(b, c + 1))
                        act.activation(xT[:, c, 1:N + 1], a.ps_a[c][:], ACT.Identity,
                                       scale=rms_col[:, c:c + 1]).then_inc(xT_done.sem, 1)
                    for k in range(PROJ):
                        if k == 0:
                            act.wait_ge(a.pv.sem, a.pv.at(b, 0))
                            act.wait_ge(gate_done.sem, gate_done.at(b, 0))
                        act.wait_ge(proj_ps.sem, proj_ps.at(b, k + 1))
                        src = a.ps_a[k % 2][:]
                        if k < QC:
                            ins = act.activation(a.qT[:, k, :], src, ACT.Copy, scale=float(CA_D) ** -0.5)
                        elif k < 2 * QC:
                            ins = act.activation(a.kT[:, k - QC, :], src, ACT.Copy)
                        elif k < 2 * QC + T:
                            ins = act.activation(a.v[:, k - 2 * QC, :], src, ACT.Copy)
                        else:
                            ins = act.activation(gate_e[:, :, :].rearrange("p t h -> p (t h)"),
                                                 a.ps_a[k % 2][:, 0:T * CA_H], ACT.Exp, scale=-1.0)
                        ins.then_inc(proj_done.sem, 1)
                    attend_act(act, b, a)

            @block.tensor
            def _(pe):
                with pe.Fori(0, B) as b:
                    pe.wait_ge(a.oT_done.sem, a.oT_done.at(b, 0))
                    pe.wait_ge(a.h_done.sem, a.h_done.at(b, 0))
                    turn_x(pe, b, xn, ident, a.ps_a, rms_normed, xT_ps)
                    for k in range(PROJ):
                        if k == 0:
                            pe.wait_ge(xT_done.sem, xT_done.at(b, C))
                        if k >= 2:
                            pe.wait_ge(proj_done.sem, proj_done.at(b, k - 1))
                        if k < 2 * QC:
                            for c in range(C):
                                last = pe.matmul(a.ps_a[k % 2][:], ca_w[:, c, k * P:(k + 1) * P],
                                                 xT[:, c, 1:N + 1], start=(c == 0), stop=(c == C - 1))
                        elif k < 2 * QC + T:
                            t = k - 2 * QC
                            for c in range(C):
                                last = pe.matmul(a.ps_a[k % 2][:], xT[:, c, 1 + t * P:1 + (t + 1) * P],
                                                 ca_w[:, c, 2 * INNER:], start=(c == 0), stop=(c == C - 1))
                        else:
                            for t in range(T):
                                for c in range(C):
                                    last = pe.matmul(a.ps_a[k % 2][:, t * CA_H:(t + 1) * CA_H],
                                                     xT[:, c, 1 + t * P:1 + (t + 1) * P], gates_w[:, c, :],
                                                     start=(c == 0), stop=(c == C - 1))
                        last.then_inc(proj_ps.sem, 1)
                    pe.wait_ge(proj_done.sem, proj_done.at(b, PROJ))
                    attend_pe(pe, b, a)


LATE_SHAPES = {
    "wqkv": [DEPTH, C, 3 * INNER],
    "wo": [DEPTH, INNER // P, D],
    "w1": [DEPTH, C, 2 * HID],
    "w2": [DEPTH, FC, D],
    "ln_g": [DEPTH, C],
    "ln_b": [DEPTH, C],
    "b1": [DEPTH, 2, FC],
    "trig": [T, 4 * CA_D],
    "qk_scale": [DEPTH, 4 * CA_D],
    "spare": [FC * N],
}


def late_views(big):
    views, at = {}, 0
    for name, shape in LATE_SHAPES.items():
        size = int(np.prod(shape))
        flat = big[:, at:at + size]
        letters = "abc"[:len(shape)]
        views[name] = flat.rearrange(f"p ({' '.join(letters)}) -> p {' '.join(letters)}",
                                     **{x: n for x, n in zip(letters[:-1], shape[:-1])})
        at += size
    return views, at


def late_loads(views, b2_row, wqkv, ffn_wo, w1, w2f, trig, qk_scale, ln_g, ln_b, b1, b2):
    loads = []
    full = (FC - 1) * P
    for l in range(DEPTH):
        loads += [(views["wqkv"][:, l], wqkv[l].rearrange("(c p) n -> p c n", p=P)),
                  (views["wo"][:, l], ffn_wo[l].rearrange("(c p) n -> p c n", p=P)),
                  (views["w1"][:, l], w1[l].rearrange("(c p) n -> p c n", p=P)),
                  (views["w2"][:, l, 0:FC - 1], w2f[l, 0:full, :].rearrange("(c p) n -> p c n", p=P)),
                  (views["w2"][0:HID - full, l, FC - 1], w2f[l, full:HID, :])]
    loads += [(views["ln_g"], ln_g.rearrange("p (l c) -> p l c", c=C)),
              (views["ln_b"], ln_b.rearrange("p (l c) -> p l c", c=C)),
              (views["b1"], b1), (views["trig"], trig), (views["qk_scale"], qk_scale), (b2_row[:, :], b2)]
    return loads


def local_layers(nc, bank, h, pause, ident, ident_bf, window_mask, half, one_row, xn, xT, w, b2_row, depth,
                 loaded_late, n_late):
    HD2 = CA_D // 2
    with ExitStack() as ctx:
        def st(name, shape, dt=F32):
            return ctx.enter_context(nc.sbuf_tensor(f"local_{name}", shape, dt))

        def signal(name, per):
            return Signal(ctx, nc, f"local_{name}", per)

        a = Attention(ctx, nc, bank, "local", lambda i: list(range(max(i - 1, 0), i + 1)),
                      lambda i: min(i + 1, 2), False, ident, ident_bf, window_mask, None)
        straight = [w["early_a"][:, i * 2 * INNER:(i + 1) * 2 * INNER] for i in range(2)]
        table = w["early_b"][:, 0:T * 4 * CA_D].rearrange("p (t n) -> p t n", t=T)
        squares = [w["spare"][:, i * 2 * INNER:(i + 1) * 2 * INNER] for i in range(2)]
        crossed = [w["spare"][:, 4 * INNER:6 * INNER], w["early_a"][:, 4 * INNER:6 * INNER]]
        norm_sq, rnorm = st("norm_sq", [P, T, 16]), st("rnorm", [P, T, 16])
        shifted = st("shifted", [P, T, P])
        stats, moments = st("stats", [P, T, 12]), st("moments", [P, T, 2])
        var_eps, rstd = st("var_eps", [P, T]), st("rstd", [P, T])
        act_gate = [a.prob[0], a.prob[1]]
        hidden = w["spare"].rearrange("p (c n) -> p c n", c=FC)

        table_done = ctx.enter_context(nc.semaphore("local_table"))
        staged = signal("staged", 1)
        xT_ps = signal("xT_ps", C)
        xT_done = signal("xT", C)
        qkv_ps = signal("qkv_ps", 3 * T)
        squared = signal("squared", 2 * T)
        v_done = signal("v", T)
        rotary = signal("rotary", 4 * T)
        norms = signal("norms", 2 * T)
        rnorm_done = signal("rnorm", T)
        rotated = signal("rotated", 2 * T)
        qkT_ps = signal("qkT_ps", T)
        qkT_done = signal("qkT", 2 * T)
        shift_done = signal("shift", 32)
        moments_done = signal("moments", 3 * T + 1)
        rstd_done = signal("rstd", 1)
        normed = signal("normed", 2 * T)
        nT_ps = signal("nT_ps", C)
        nT_done = signal("nT", C)
        up_ps = signal("up_ps", FC)
        gated = signal("gated", FC)
        hid = signal("hidden", FC)
        down_ps = signal("down_ps", T)
        h_done = signal("h2", T)
        every = [staged, xT_ps, xT_done, qkv_ps, squared, v_done, rotary, norms, rnorm_done, rotated,
                 qkT_ps, qkT_done, shift_done, moments_done, rstd_done, normed, nT_ps, nT_done, up_ps, gated,
                 hid, down_ps, h_done] + a.every
        ps_a = a.ps_a

        for layer in range(depth):
            wqkv, w1, w2 = w["wqkv"][:, layer], w["w1"][:, layer], w["w2"][:, layer]
            a.wo = w["wo"][:, layer]
            with nc.Block() as block:
                @block.sync
                def _(sp):
                    if layer == 0:
                        for s in every:
                            sp.sem_inc(s.sem, s.per)
                    with sp.Fori(0, B) as b:
                        sp.wait_ge(a.h_done.sem, a.h_done.at(b, T))
                        sp.wait_ge(normed.sem, normed.at(b, 0))
                        sp.dma_start(shifted[1:P, :, :],
                                     h[0:P - 1, bass.ds(b * T, T), P:2 * P]).then_inc(shift_done.sem, 16)
                        sp.dma_start(shifted[0:1, 1:T, :],
                                     h[P - 1:P, bass.ds(b * T, T - 1), P:2 * P]).then_inc(shift_done.sem, 16)

                @block.gpsimd
                def _(pool):
                    with pool.Fori(0, B) as b:
                        for t in range(T):
                            pool.wait_ge(norms.sem, norms.at(b, 2 * t + 2))
                            pool.tensor_tensor(rnorm[:, t, :], norm_sq[:, t, :], half[:], ALU.pow).then_inc(rnorm_done.sem, 1)
                            pool.wait_ge(rotary.sem, rotary.at(b, 4 * t + 4))
                            pool.wait_ge(qkT_ps.sem, qkT_ps.at(b, t + 1 - 2))
                            pool.tensor_tensor(straight[t % 2], straight[t % 2], crossed[t % 2],
                                               ALU.add).then_inc(rotated.sem, 1)
                            pool.wait_ge(rnorm_done.sem, rnorm_done.at(b, t + 1))
                            pool.wait_ge(rotated.sem, rotated.at(b, 2 * t + 1))
                            heads = straight[t % 2].rearrange("p (h d) -> p h d", d=CA_D)
                            pool.tensor_tensor(heads, heads, rnorm[:, t, :].unsqueeze(2).to_broadcast([P, 2 * CA_H, CA_D]),
                                               ALU.mult).then_inc(rotated.sem, 1)
                        pool.wait_ge(moments_done.sem, moments_done.at(b, 3 * T + 1))
                        pool.tensor_tensor(rstd[:], var_eps[:], half[:, 0:T], ALU.pow).then_inc(rstd_done.sem, 1)

                @block.vector
                def _(dve):
                    if layer == 0:
                        dve.memset(shifted[0:1, 0, :], 0.0)
                    dve.wait_ge(loaded_late, 16 * n_late)
                    dve.tensor_tensor(table[:, :, :], w["trig"],
                                      w["qk_scale"][:, layer, :].unsqueeze(1).to_broadcast([P, T, 4 * CA_D]),
                                      ALU.mult).then_inc(table_done, 1)
                    dve.wait_ge(table_done, layer + 1)
                    with dve.Fori(0, B) as b:
                        dve.wait_ge(nT_ps.sem, nT_ps.at(b, 0))
                        dve.tensor_scalar(xn[:, :, :], h[:, bass.ds(b * T, T), :], 1.0, None,
                                          ALU.mult).then_inc(staged.sem, 1)
                        dve.wait_ge(down_ps.sem, down_ps.at(b, 0))
                        for t in range(T):
                            dve.wait_ge(rotated.sem, rotated.at(b, 2 * (t + 1 - 2)))
                            dve.wait_ge(qkT_ps.sem, qkT_ps.at(b, t + 1 - 2))
                            for k in range(2):
                                dve.wait_ge(squared.sem, squared.at(b, 2 * t + k + 1))
                                ps = bank[2 + 2 * k + t % 2][:]
                                cos = table[:, t, 2 * k * CA_D:(2 * k + 1) * CA_D]
                                sin = table[:, t, (2 * k + 1) * CA_D:(2 * k + 2) * CA_D]
                                cols = slice(k * INNER, (k + 1) * INNER)
                                dve.tensor_tensor(straight[t % 2][:, cols].rearrange("p (h d) -> p h d", d=CA_D),
                                                  ps.rearrange("p (h d) -> p h d", d=CA_D),
                                                  cos.unsqueeze(1).to_broadcast([P, CA_H, CA_D]),
                                                  ALU.mult).then_inc(rotary.sem, 1)
                                for s in range(2):
                                    ins = dve.tensor_tensor(
                                        crossed[t % 2][:, cols].rearrange("p (h s d) -> p h s d", s=2, d=HD2)[:, :, s, :],
                                        ps.rearrange("p (h s d) -> p h s d", s=2, d=HD2)[:, :, 1 - s, :],
                                        sin[:, s * HD2:(s + 1) * HD2].unsqueeze(1).to_broadcast([P, CA_H, HD2]),
                                        ALU.mult)
                                ins.then_inc(rotary.sem, 1)
                            dve.tensor_reduce(norm_sq[:, t, :], squares[t % 2].rearrange("p (h d) -> p h d", d=CA_D),
                                              AX.X, ALU.add).then_inc(norms.sem, 1)
                            dve.wait_ge(norms.sem, norms.at(b, 2 * t + 1))
                            dve.tensor_scalar(norm_sq[:, t, :], norm_sq[:, t, :], 1e-24, None,
                                              ALU.max).then_inc(norms.sem, 1)
                        attend_dve(dve, b, a, h, None)
                        dve.wait_ge(a.h_done.sem, a.h_done.at(b, T))
                        dve.memset(pause[:], 0.0)
                        for t in range(T):
                            dve.bn_stats(stats[:, t, 0:6], batch_slice(h, b, t)[:, 0:P]).then_inc(moments_done.sem, 1)
                        dve.wait_ge(shift_done.sem, shift_done.at(b, 32))
                        for t in range(T):
                            dve.bn_stats(stats[:, t, 6:12], shifted[:, t, :]).then_inc(moments_done.sem, 1)
                        dve.wait_ge(moments_done.sem, moments_done.at(b, 2 * T))
                        dve.memset(pause[:], 0.0)
                        for t in range(T):
                            dve.bn_aggr(moments[:, t, :], stats[:, t, :]).then_inc(moments_done.sem, 1)
                        dve.wait_ge(moments_done.sem, moments_done.at(b, 3 * T))
                        dve.tensor_scalar(var_eps[:], moments[:, :, 1], EPS_LN, None, ALU.add).then_inc(moments_done.sem, 1)
                        dve.wait_ge(xT_ps.sem, xT_ps.at(b, C))
                        dve.wait_ge(rstd_done.sem, rstd_done.at(b, 1))
                        for t in range(T):
                            for c, src in enumerate([batch_slice(h, b, t)[:, 0:P], shifted[:, t, :]]):
                                dve.tensor_scalar(xn[:, t, c * P:(c + 1) * P], src, moments[:, t, 0:1],
                                                  rstd[:, t:t + 1], ALU.subtract, ALU.mult).then_inc(normed.sem, 1)
                        for n in range(FC):
                            dve.wait_ge(gated.sem, gated.at(b, n + 1))
                            dve.wait_ge(down_ps.sem, down_ps.at(b, 0))
                            dve.scalar_tensor_tensor(hidden[0:FW[n], n, :], bank[2 + n % 2][0:FW[n], :],
                                                     w["b1"][0:FW[n], layer, 0, n:n + 1], act_gate[n % 2][0:FW[n], :],
                                                     ALU.add, ALU.mult).then_inc(hid.sem, 1)
                        for t in range(T):
                            dve.wait_ge(down_ps.sem, down_ps.at(b, t + 1))
                            hs = batch_slice(h, b, t)
                            dve.tensor_tensor(hs, bank[6 + t % 2][:, 0:D], hs, ALU.add).then_inc(h_done.sem, 1)

                @block.scalar
                def _(act):
                    def copy_qk(b, t):
                        act.wait_ge(qkT_ps.sem, qkT_ps.at(b, t + 1))
                        for k, dst in enumerate([a.qT, a.kT]):
                            act.activation(dst[:, :, t * P:(t + 1) * P],
                                           ps_a[k][:].rearrange("p (c n) -> p c n", c=INNER // P),
                                           ACT.Copy).then_inc(qkT_done.sem, 1)

                    with act.Fori(0, B) as b:
                        for c in range(C):
                            act.wait_ge(up_ps.sem, up_ps.at(b, 0))
                            act.wait_ge(xT_ps.sem, xT_ps.at(b, c + 1))
                            act.activation(xT[:, c, 1:N + 1], ps_a[c][:], ACT.Copy).then_inc(xT_done.sem, 1)
                        act.wait_ge(down_ps.sem, down_ps.at(b, 0))
                        for t in range(T):
                            act.wait_ge(norms.sem, norms.at(b, 2 * (t + 1 - 2)))
                            for k in range(2):
                                act.wait_ge(qkv_ps.sem, qkv_ps.at(b, 3 * t + k + 1))
                                act.activation(squares[t % 2][:, k * INNER:(k + 1) * INNER], bank[2 + 2 * k + t % 2][:],
                                               ACT.Square).then_inc(squared.sem, 1)
                            act.wait_ge(qkv_ps.sem, qkv_ps.at(b, 3 * t + 3))
                            act.activation(a.v[:, t, :], bank[6 + t % 2][:], ACT.Copy).then_inc(v_done.sem, 1)
                            if t >= 1:
                                copy_qk(b, t - 1)
                        copy_qk(b, T - 1)
                        attend_act(act, b, a)
                        for c in range(C):
                            act.wait_ge(nT_ps.sem, nT_ps.at(b, c + 1))
                            act.activation(xT[:, c, 1:N + 1], ps_a[c][:], ACT.Identity, bias=w["ln_b"][:, layer, c:c + 1],
                                           scale=w["ln_g"][:, layer, c:c + 1]).then_inc(nT_done.sem, 1)
                        for n in range(FC):
                            act.wait_ge(up_ps.sem, up_ps.at(b, n + 1))
                            act.wait_ge(hid.sem, hid.at(b, n + 1 - 2))
                            act.activation(act_gate[n % 2][0:FW[n], :], bank[4 + n % 2][0:FW[n], :], ACT.Gelu,
                                           bias=w["b1"][0:FW[n], layer, 1, n:n + 1]).then_inc(gated.sem, 1)

                @block.tensor
                def _(pe):
                    def turn_qk(b, t):
                        pe.wait_ge(rotated.sem, rotated.at(b, 2 * t + 2))
                        if t == 0:
                            pe.wait_ge(xT_done.sem, xT_done.at(b, C))
                        pe.wait_ge(qkT_done.sem, qkT_done.at(b, 2 * t))
                        for k in range(2):
                            for c in range(INNER // P):
                                at = k * INNER + c * P
                                last = pe.transpose(ps_a[k][:, c * P:(c + 1) * P], straight[t % 2][:, at:at + P], ident[:])
                        last.then_inc(qkT_ps.sem, 1)

                    pe.wait_ge(loaded_late, 16 * n_late)
                    with pe.Fori(0, B) as b:
                        pe.wait_ge(nT_done.sem, nT_done.at(b, 0))
                        turn_staged(pe, b, xn, ident, ps_a, staged, xT_ps)
                        pe.wait_ge(xT_done.sem, xT_done.at(b, C))
                        pe.wait_ge(hid.sem, hid.at(b, 0))
                        pe.wait_ge(h_done.sem, h_done.at(b, 0))
                        for t in range(T):
                            for k in range(3):
                                if k < 2:
                                    pe.wait_ge(rotary.sem, rotary.at(b, 4 * (t + 1 - 2)))
                                    pe.wait_ge(squared.sem, squared.at(b, 2 * (t + 1 - 2)))
                                else:
                                    pe.wait_ge(v_done.sem, v_done.at(b, t + 1 - 2))
                                for c in range(C):
                                    last = pe.matmul(bank[2 + 2 * k + t % 2][:], xT[:, c, 1 - c + t * P:1 - c + (t + 1) * P],
                                                     wqkv[:, c, k * INNER:(k + 1) * INNER], start=(c == 0),
                                                     stop=(c == C - 1))
                                last.then_inc(qkv_ps.sem, 1)
                            if t >= 1:
                                turn_qk(b, t - 1)
                        turn_qk(b, T - 1)
                        pe.wait_ge(qkT_done.sem, qkT_done.at(b, 2 * T))
                        pe.wait_ge(rotary.sem, rotary.at(b, 4 * T))
                        pe.wait_ge(v_done.sem, v_done.at(b, T))
                        attend_pe(pe, b, a)
                        pe.wait_ge(a.h_done.sem, a.h_done.at(b, T))
                        for c in range(C):
                            for t in range(T):
                                pe.wait_ge(normed.sem, normed.at(b, 2 * t + c + 1))
                                last = pe.transpose(ps_a[c][:, t * P:(t + 1) * P], xn[:, t, c * P:(c + 1) * P], ident[:])
                            last.then_inc(nT_ps.sem, 1)
                        pe.wait_ge(nT_done.sem, nT_done.at(b, C))
                        for n in range(FC):
                            pe.wait_ge(hid.sem, hid.at(b, n + 1 - 2))
                            for part in range(2):
                                for c in range(C):
                                    at = part * HID + n * P
                                    last = pe.matmul(bank[2 + 2 * part + n % 2][0:FW[n], :], w1[:, c, at:at + FW[n]],
                                                     xT[:, c, 1:N + 1], start=(c == 0), stop=(c == C - 1))
                            last.then_inc(up_ps.sem, 1)
                        for t in range(T):
                            if t >= 2:
                                pe.wait_ge(h_done.sem, h_done.at(b, t + 1 - 2))
                            pe.matmul(bank[6 + t % 2][:, 0:D], one_row[:], b2_row[:, layer * D:(layer + 1) * D],
                                      start=True, stop=False)
                            for n in range(FC):
                                if t == 0:
                                    pe.wait_ge(hid.sem, hid.at(b, n + 1))
                                last = pe.matmul(bank[6 + t % 2][:, 0:D], hidden[0:FW[n], n, t * P:(t + 1) * P],
                                                 w2[0:FW[n], n, :], start=False, stop=(n == FC - 1))
                            last.then_inc(down_ps.sem, 1)
            for s in every:
                s.passed += B


def turn_staged(pe, b, xn, ident, banks, staged, xT_ps):
    pe.wait_ge(staged.sem, staged.at(b, 1))
    for c in range(C):
        for t in range(T):
            last = pe.transpose(banks[c][:, t * P:(t + 1) * P], xn[:, t, c * P:(c + 1) * P], ident[:])
        last.then_inc(xT_ps.sem, 1)


def rotary_tables():
    f = np.float32
    half_idx = np.arange(0, CA_D, 2, dtype=f)
    inv_freq = f(1.0) / f(10000.0) ** (half_idx / f(CA_D))
    t = np.arange(N, dtype=f)
    freqs = t[:, None] * inv_freq[None, :]
    freqs = np.concatenate([freqs, freqs], axis=-1)
    base = (half_idx + f(0.4 * CA_D)) / f(1.4 * CA_D)
    power = (t - f(N // 2)) / f(64.0)
    scale = base[None, :] ** power[:, None]
    scale = np.concatenate([scale, scale], axis=-1)
    sign = np.where(np.arange(CA_D) < CA_D // 2, f(-1.0), f(1.0))
    cos, sin = np.cos(freqs), np.sin(freqs) * sign
    tables = np.stack([f(8.0) * cos * scale, f(8.0) * sin * scale, cos / scale, sin / scale], axis=1)
    return np.ascontiguousarray(tables.astype(f).reshape(T, P, 4 * CA_D).transpose(1, 0, 2))


def kernel(x, L0_tok_emb0, L0_tok_emb1, L0_tok_emb2, L0_tok_emb3, L0_tok_proj0, L0_tok_proj1, L0_tok_proj2,
           L0_tok_proj3, L0_attn_Wq, L0_attn_Wk, L0_attn_Wv, L0_attn_Wo, L0_ffn_moe_router, L0_ffn_moe_w13,
           L0_ffn_moe_w2, L1_attn_wq, L1_attn_wk, L1_attn_wv, L1_attn_wo, L1_attn_w_lr, L1_attn_w_target,
           L1_attn_w_gates, L1_attn_rms_w, L1_ffn_wqkv, L1_ffn_q_scale, L1_ffn_k_scale, L1_ffn_wo, L1_ffn_ln_g,
           L1_ffn_ln_b, L1_ffn_w1, L1_ffn_b1, L1_ffn_w2, L1_ffn_b2, stages=5):
    import concourse.bacc as bacc
    from concourse.bass_utils import run_bass_kernel_spmd

    tables = [np.asarray(t) for t in (L0_tok_emb0, L0_tok_emb1, L0_tok_emb2, L0_tok_emb3)]
    projs = [np.asarray(t) for t in (L0_tok_proj0, L0_tok_proj1, L0_tok_proj2, L0_tok_proj3)]
    emb = np.zeros((CUTOFFS[-1], D), tables[0].dtype)
    for k, t in enumerate(tables):
        emb[CUTOFFS[k]:CUTOFFS[k + 1], 0:EMB_W[k]] = t
    proj = np.zeros((3 * P, D), projs[0].dtype)
    for k, t in enumerate(projs):
        proj[EMB_AT[k]:EMB_AT[k] + EMB_W[k]] = t.T

    def padded(w):
        got = np.zeros((D, SB_H, SB_PAD), w.dtype)
        got[:, :, 0:SB_D] = np.asarray(w).T.reshape(D, SB_H, SB_D)
        return got.reshape(D, SB_H * SB_PAD)

    def heads_last(w):
        return np.ascontiguousarray(np.asarray(w).transpose(1, 0, 2).reshape(D, INNER))

    def columns(w):
        return np.ascontiguousarray(np.asarray(w).reshape(-1, P).T)

    q_s, k_s = np.asarray(L1_ffn_q_scale), np.asarray(L1_ffn_k_scale)
    qk_scale = np.stack([q_s, np.roll(q_s, CA_D // 2, axis=1), k_s, np.roll(k_s, CA_D // 2, axis=1)], axis=1)
    qk_scale = np.ascontiguousarray(np.broadcast_to(qk_scale.reshape(1, DEPTH, 4 * CA_D), (P, DEPTH, 4 * CA_D)))
    b1 = np.zeros((DEPTH, 2, FC * P), q_s.dtype)
    b1[:, :, 0:HID] = np.asarray(L1_ffn_b1).reshape(DEPTH, 2, HID)
    b1 = np.ascontiguousarray(b1.reshape(DEPTH, 2, FC, P).transpose(3, 0, 1, 2))

    arrays = {
        "ids": np.ascontiguousarray(np.asarray(x).reshape(NT, P).T),
        "emb": emb,
        "proj": proj.reshape(3, P, D),
        "sb_wq": padded(np.asarray(L0_attn_Wq)), "sb_wk": padded(np.asarray(L0_attn_Wk)),
        "sb_wv": np.ascontiguousarray(np.asarray(L0_attn_Wv).T),
        "sb_wo": np.ascontiguousarray(np.asarray(L0_attn_Wo).T),
        "router": np.asarray(L0_ffn_moe_router), "w13": np.asarray(L0_ffn_moe_w13), "w2": np.asarray(L0_ffn_moe_w2),
        "ca_wq": heads_last(L1_attn_wq), "ca_wk": heads_last(L1_attn_wk), "ca_wv": heads_last(L1_attn_wv),
        "ca_wo": np.asarray(L1_attn_wo).reshape(INNER, D), "w_gates": np.asarray(L1_attn_w_gates),
        "rms_w": columns(L1_attn_rms_w),
        "trig": rotary_tables(),
        "wqkv": np.asarray(L1_ffn_wqkv), "qk_scale": qk_scale,
        "ffn_wo": np.asarray(L1_ffn_wo), "ln_g": columns(L1_ffn_ln_g), "ln_b": columns(L1_ffn_ln_b),
        "w1": np.asarray(L1_ffn_w1), "b1": b1, "w2f": np.asarray(L1_ffn_w2),
        "b2": np.asarray(L1_ffn_b2).reshape(1, DEPTH * D),
    }
    nc = bacc.Bacc("TRN2", target_bir_lowering=False, num_devices=1)
    args = [nc.dram_tensor(k, a.shape, mybir.dt.from_np(a.dtype), kind="ExternalInput").ap() for k, a in arrays.items()]
    out = nc.dram_tensor("out", (B * N, D), F32, kind="ExternalOutput").ap()
    program(nc, *args, out, stages=stages)
    r = run_bass_kernel_spmd(nc, [arrays], core_ids=[0])
    return r.results[0]["out"].reshape(B, N, D)
```

```python
import concourse.bass as bass
from concourse import mybir
from contextlib import ExitStack
import numpy as np

F32 = mybir.dt.float32
BF16 = mybir.dt.bfloat16
I32 = mybir.dt.int32
U32 = mybir.dt.uint32
ALU = mybir.AluOpType
ACT = mybir.ActivationFunctionType
AX = mybir.AxisListType

P = 128
B, N, D = 4, 512, 256
T = N // P
NT = B * T
C = D // P
EPS_LN = 1e-5
EPS_RMS = float(np.finfo(np.float32).eps)
MASKED = -1e30

CUTOFFS = [0, 5000, 15000, 25000, 32000]
EMB_W = [256, 64, 16, 4]
EMB_AT = [0, 256, 320, 336]
EMB_K = 340
EMB_CHUNKS = [128, 128, 84]

SB_H, SB_D, SB_PAD = 16, 16, 32
MOE_E, MOE_F = 8, 512
MOE_TILES = (2 * B * N + MOE_E * (P - 1)) // P
MOE_TILES += MOE_TILES % 2
CA_H, CA_D = 8, 64
INNER = CA_H * CA_D
DEPTH = 2
HID = 682
FC = 6
FW = [128, 128, 128, 128, 128, 42]


class Signal:

    def __init__(self, ctx, nc, name, per):
        self.sem = ctx.enter_context(nc.semaphore(name))
        self.per = per
        self.passed = 0

    def at(self, i, n):
        assert -self.per < n <= self.per, (n, self.per)
        return i * self.per + ((self.passed + 1) * self.per + n)


def batch_slice(tensor, b, t):
    return tensor[:, bass.ds(b * T + t, 1), :].rearrange("p a n -> p (a n)")


def program(nc, ids, emb, proj, sb_wq, sb_wk, sb_wv, sb_wv2, sb_wo2, kinds, router, w13, w2, ca_wq, ca_wk, ca_wv, ca_wo,
            w_gates, rms_w, trig, wqkv, qk_scale, ffn_wo, ln_g, ln_b, w1, b1, w2f, b2, xs, ys, out,
            stages=5):
    with ExitStack() as ctx:
        def sb(name, shape, dt=F32, where=ctx):
            return where.enter_context(nc.sbuf_tensor(name, shape, dt))

        bank = [ctx.enter_context(nc.psum_tensor(f"bank{i}", [P, 512], F32)) for i in range(8)]

        h = sb("h", [P, NT, D])
        ident = sb("ident", [P, P])
        ident_bf = sb("ident_bf", [P, P], BF16)
        scan_floor = sb("scan_floor", [P, N])
        window_mask = sb("window_mask", [P, 2, P], BF16)
        half = sb("half", [P, 16])
        one_row = sb("one_row", [1, P])
        pause = sb("pause", [P, 1])
        xn = sb("xn", [P, T, D])
        xT = sb("xT", [P, C, N + 1])
        proj_w = sb("proj_w", [P, 3, D])
        sb_w = sb("sb_w", [P, 3 * C * SB_H * SB_PAD + SB_H * SB_PAD // P * D + C * D])
        row_kind = sb("row_kind", [P, 2])
        ca_all = sb("ca_all", [P, C * 3 * INNER + INNER // P * D])
        ca_w = ca_all[:, 0:C * 3 * INNER].rearrange("p (c n) -> p c n", c=C)
        ca_wo_w = ca_all[:, C * 3 * INNER:].rearrange("p (c n) -> p c n", c=INNER // P)
        gates_w = sb("gates_w", [P, C, CA_H])
        router_w = sb("router_w", [P, C, MOE_E])
        rms_col = sb("rms_col", [P, C])
        b2_row = sb("b2_row", [1, DEPTH * D])
        big = sb("big", [P, MOE_E * (C * 2 * MOE_F + MOE_F // P * D)])

        def sem(name):
            return ctx.enter_context(nc.semaphore(name))

        loaded_sb = sem("loaded_sb")
        loaded_ca = sem("loaded_ca")

        SBW = C * SB_H * SB_PAD
        at = [0, SBW, 2 * SBW, 3 * SBW, 3 * SBW + SB_H * SB_PAD // P * D, 3 * SBW + SB_H * SB_PAD // P * D + C * D]
        sb_loads = [(sb_w[:, at[k]:at[k + 1]].rearrange("p (c n) -> p c n", n=w.shape[1]),
                     w.rearrange("(c p) n -> p c n", p=P))
                    for k, w in enumerate([sb_wq, sb_wk, sb_wv2, sb_wo2, sb_wv])] + [(row_kind[:, :], kinds)]
        consts_and_embedding(nc, sb, bank, ids, emb, proj, proj_w, h, ident, ident_bf, scan_floor,
                             window_mask, half, one_row, xT, sb_loads, loaded_sb)
        if stages >= 1:
            xn_all = ca_all[:, 0:NT * D].rearrange("p (t n) -> p t n", t=NT)
            stick_breaking(nc, bank, h, half, ident, scan_floor, xn_all, xn, xT, sb_w, big, row_kind, loaded_sb, xs)
        if stages >= 2:
            xn_all = sb_w[:, 0:NT * D].rearrange("p (t n) -> p t n", t=NT)
            share, slot = sb("moe_share", [P, 2, NT]), sb("moe_slot", [P, 2, NT], I32)
            experts(nc, bank, h, half, share, slot, ident, xT, xn_all, router_w, big, xs, ys, router, w13, w2,
                    [(ca_w[:, :, 0:512], ca_wq), (ca_w[:, :, 512:1024], ca_wk), (ca_w[:, :, 1024:1536], ca_wv),
                     (ca_wo_w, ca_wo), (gates_w[:, :, :], w_gates), (rms_col[:, :], rms_w)],
                    loaded_ca)
        if stages >= 3:
            loaded_late = sem("loaded_late")
            late, _ = late_views(big)
            late["early_a"] = sb_w[:, :]
            late["early_b"] = ca_all[:, 0:C * 3 * INNER]
            loads = late_loads(late, b2_row, wqkv, ffn_wo, w1, w2f, trig, qk_scale, ln_g, ln_b, b1, b2)
            at = LATE_SIZE - FC * N
            xn_all = big[:, at:at + NT * D].rearrange("p (t n) -> p t n", t=NT)
            causal(nc, bank, h, half, share, slot, ys, big, ident, ident_bf, window_mask, xn_all, xn, xT, ca_w, ca_wo_w, gates_w, rms_col,
                   sb_w, loads if stages > 3 else [], loaded_late, loaded_ca)
        kept = []
        if stages >= 4:
            kept = [late["early_b"][:, (b + 1) * T * D:(b + 2) * T * D] for b in range(2)]
            kept += [big[:, LATE_SIZE + b * T * D:LATE_SIZE + (b + 1) * T * D] for b in range(2)]
            local_layers(nc, bank, h, pause, ident, ident_bf, window_mask, half, one_row, xn, xT, late, b2_row, kept,
                         min(DEPTH, stages - 3), loaded_late, len(loads))
        store(nc, h, kept, out)


class Normalizer:

    def __init__(self, ctx, nc, name, rms=False):
        def st(what, shape):
            return ctx.enter_context(nc.sbuf_tensor(f"{name}_{what}", shape, F32))

        self.factor, self.offset = (1.0 + EPS_RMS, EPS_LN * EPS_RMS) if rms else (1.0, EPS_LN)
        self.stats, self.moments = st("stats", [P, NT, 6]), st("moments", [P, NT, 2])
        self.square, self.scale = st("square", [P, NT]), st("scale", [P, NT])
        self.steps = ctx.enter_context(nc.semaphore(f"{name}_steps"))
        self.scale_done = ctx.enter_context(nc.semaphore(f"{name}_scale"))
        self.normed = ctx.enter_context(nc.semaphore(f"{name}_normed"))

    def on_dve(self, dve, b, h, out):
        tiles, steps = range(b * T, (b + 1) * T), b * (2 * T + 1)
        mine = slice(b * T, (b + 1) * T)
        for t in tiles:
            dve.bn_stats(self.stats[:, t, :], h[:, t, :]).then_inc(self.steps, 1)
        dve.wait_ge(self.steps, steps + T)
        for t in tiles:
            dve.bn_aggr(self.moments[:, t, :], self.stats[:, t, :]).then_inc(self.steps, 1)
        dve.wait_ge(self.steps, steps + 2 * T)
        dve.tensor_scalar(self.square[:, mine], self.moments[:, mine, 1], self.factor, self.offset, ALU.mult,
                          ALU.add).then_inc(self.steps, 1)
        dve.wait_ge(self.scale_done, b + 1)
        for t in tiles:
            dve.tensor_scalar(out[:, t, :], h[:, t, :], self.moments[:, t, 0:1], self.scale[:, t:t + 1],
                              ALU.subtract, ALU.mult).then_inc(self.normed, 1)

    def on_pool(self, pool, half):
        for b in range(B):
            mine = slice(b * T, (b + 1) * T)
            pool.wait_ge(self.steps, (b + 1) * (2 * T + 1))
            pool.tensor_tensor(self.scale[:, mine], self.square[:, mine], half[:, mine],
                               ALU.pow).then_inc(self.scale_done, 1)


def store(nc, h, kept, out):
    with ExitStack() as ctx:
        stored = ctx.enter_context(nc.semaphore("stored"))
        summed = ctx.enter_context(nc.semaphore("final_summed"))
        with nc.Block() as block:
            @block.vector
            def _(dve):
                for b in range(B if kept else 0):
                    hb = h[:, b * T:(b + 1) * T, :].rearrange("p t d -> p (t d)")
                    dve.tensor_tensor(hb, hb, kept[b], ALU.add).then_inc(summed, 1)

            @block.sync
            def _(sp):
                for b in range(B):
                    if kept:
                        sp.wait_ge(summed, b + 1)
                    sp.dma_start(out[b * N:(b + 1) * N, :].rearrange("(t p) d -> p t d", p=P),
                                 h[:, b * T:(b + 1) * T, :]).then_inc(stored, 16)
                sp.wait_ge(stored, 16 * B)


def consts_and_embedding(nc, sb, bank, ids, emb, proj, proj_w, h, ident, ident_bf, scan_floor,
                         window_mask, half, one_row, xT, weights, loaded_sb):
    with ExitStack() as ctx:
        def st(name, shape, dt=F32):
            return ctx.enter_context(nc.sbuf_tensor(name, shape, dt))

        def sem(name):
            return ctx.enter_context(nc.semaphore(name))

        ids_sb = st("ids_sb", [P, NT], I32)
        ids_f = st("ids_f", [P, NT])
        row = st("row", [P, NT])
        row_i = st("row_i", [P, NT], U32)
        at_least = st("at_least", [P, 5, NT])
        in_table = st("in_table", [P, 4, NT])
        gathered = st("gathered", [P, NT, D])
        feat = [st(f"feat{k}", [P, EMB_K]) for k in range(2)]
        featT = [st(f"featT{k}", [P, 3, P]) for k in range(2)]

        ids_in, proj_in = sem("ids_in"), sem("proj_in")
        rows_in = [sem(f"rows_in{t}") for t in range(NT)]
        made = sem("made")
        index = sem("index")
        masked = sem("masked")
        turned = sem("turned")
        turned_sb = sem("turned_sb")
        summed = sem("summed")
        kept = sem("kept")

        with nc.Block() as block:
            @block.sync
            def _(sp):
                sp.dma_start(ids_sb[:, :], ids).then_inc(ids_in, 16)
                sp.dma_start(proj_w[:, :, :], proj.rearrange("c p n -> p c n")).then_inc(proj_in, 16)
                for dst, src in weights:
                    sp.dma_start(dst, src).then_inc(loaded_sb, 16)

            @block.gpsimd
            def _(pool):
                pool.wait_ge(index, 12)
                for t in range(NT):
                    pool.indirect_dma_start(
                        gathered[:, t, :], None, emb,
                        bass.IndirectOffsetOnAxis(ap=row_i[:, t:t + 1], axis=0)).then_inc(rows_in[t], 16)
                pool.memset(ident_bf[:], 0.0).then_inc(made, 1)
                pool.memset(scan_floor[:], 0.0).then_inc(made, 1)
                pool.memset(window_mask[:], 0.0).then_inc(made, 1)
                pool.memset(half[:], -0.5).then_inc(made, 1)
                pool.memset(one_row[:], 1.0).then_inc(made, 1)
                pool.memset(xT[:, :, 0:1], 0.0).then_inc(made, 1)
                pool.wait_ge(made, 6)
                pool.affine_select(out=ident_bf[:], in_=ident_bf[:], compare_op=ALU.not_equal, fill=1.0,
                                   base=0, pattern=[[-1, P]], channel_multiplier=1).then_inc(made, 1)
                own_key = scan_floor[:, N - P:N]
                pool.affine_select(out=own_key, in_=own_key, compare_op=ALU.not_equal, fill=1.0,
                                   base=0, pattern=[[-1, P]], channel_multiplier=1).then_inc(made, 1)
                before, own = window_mask[:, 0, :], window_mask[:, 1, :]
                pool.affine_select(out=before, in_=before, compare_op=ALU.is_ge, fill=MASKED,
                                   base=0, pattern=[[1, P]], channel_multiplier=-1).then_inc(made, 1)
                pool.affine_select(out=own, in_=own, compare_op=ALU.is_ge, fill=MASKED,
                                   base=0, pattern=[[-1, P]], channel_multiplier=1).then_inc(made, 1)

            @block.vector
            def _(dve):
                dve.memset(ident[:], 0.0).then_inc(index, 1)
                dve.wait_ge(ids_in, 16)
                dve.tensor_copy(ids_f[:], ids_sb[:]).then_inc(index, 1)
                dve.wait_ge(index, 2)
                dve.tensor_scalar(row[:], ids_f[:], 0.0, float(CUTOFFS[-1] - 1), ALU.max, ALU.min).then_inc(index, 1)
                for k in range(5):
                    dve.tensor_scalar(at_least[:, k, :], ids_f[:], float(CUTOFFS[k]), None,
                                      ALU.is_ge).then_inc(index, 1)
                dve.wait_ge(index, 8)
                for k in range(3):
                    dve.tensor_sub(in_table[:, k, :], at_least[:, k, :], at_least[:, k + 1, :]).then_inc(index, 1)
                dve.tensor_copy(row_i[:], row[:]).then_inc(index, 1)
                dve.tensor_sub(in_table[:, 3, :], at_least[:, 3, :], at_least[:, 4, :]).then_inc(index, 1)
                dve.wait_ge(index, 13)
                for t in range(NT):
                    dve.wait_ge(rows_in[t], 16)
                    if t >= 2:
                        dve.wait_ge(turned, t - 1)
                    for k in range(4):
                        last = dve.tensor_scalar(feat[t % 2][:, EMB_AT[k]:EMB_AT[k] + EMB_W[k]],
                                                 gathered[:, t, 0:EMB_W[k]], in_table[:, k, t:t + 1], None,
                                                 ALU.mult)
                    last.then_inc(masked, 1)
                    if t >= 1:
                        dve.wait_ge(summed, t)
                        dve.tensor_scalar(h[:, t - 1, :], bank[2 + (t - 1) % 2][:, 0:D], float(D) ** 0.5, None,
                                          ALU.mult).then_inc(kept, 1)
                dve.wait_ge(summed, NT)
                dve.tensor_scalar(h[:, NT - 1, :], bank[2 + (NT - 1) % 2][:, 0:D], float(D) ** 0.5, None,
                                  ALU.mult).then_inc(kept, 1)

            @block.scalar
            def _(act):
                act.wait_ge(made, 10)
                act.wait_ge(index, 1)
                act.activation(ident[:], ident_bf[:], ACT.Copy).then_inc(made, 1)
                for t in range(NT):
                    act.wait_ge(turned, t + 1)
                    if t >= 2:
                        act.wait_ge(summed, t - 1)
                    act.activation(featT[t % 2][:, 0:2, :].rearrange("p c n -> p (c n)"),
                                   bank[t % 2][:, 0:2 * P], ACT.Copy)
                    act.activation(featT[t % 2][0:EMB_CHUNKS[2], 2, :],
                                   bank[t % 2][0:EMB_CHUNKS[2], 2 * P:3 * P], ACT.Copy).then_inc(turned_sb, 1)

            @block.tensor
            def _(pe):
                pe.wait_ge(made, 11)
                pe.wait_ge(proj_in, 16)

                def project(t):
                    pe.wait_ge(turned_sb, t + 1)
                    if t >= 2:
                        pe.wait_ge(kept, t - 1)
                    for c, w in enumerate(EMB_CHUNKS):
                        last = pe.matmul(bank[2 + t % 2][:, 0:D], featT[t % 2][0:w, c, :], proj_w[0:w, c, :],
                                         start=(c == 0), stop=(c == 2))
                    last.then_inc(summed, 1)

                for t in range(NT):
                    pe.wait_ge(masked, t + 1)
                    if t >= 2:
                        pe.wait_ge(turned_sb, t - 1)
                    for c, w in enumerate(EMB_CHUNKS):
                        last = pe.transpose(bank[t % 2][0:w, c * P:(c + 1) * P],
                                            feat[t % 2][:, c * P:c * P + w], ident[:])
                    last.then_inc(turned, 1)
                    if t >= 1:
                        project(t - 1)
                project(NT - 1)


def stage_batches(sp, first, xn, xn_all, normed, staged, xT_ps):
    if first:
        sp.wait_ge(normed, T)
        sp.dma_start(xn[:, :, :], xn_all[:, 0:T, :]).then_inc(staged.sem, 16)
    else:
        with sp.Fori(1, B) as b:
            sp.wait_ge(normed, b * T + T)
            sp.wait_ge(xT_ps.sem, xT_ps.at(b, 0))
            sp.dma_start(xn[:, :, :], xn_all[:, bass.ds(b * T, T), :]).then_inc(staged.sem, 16)


def stick_breaking(nc, bank, h, half, ident, scan_floor, xn_all, xn, xT, sb_w, big, row_kind, loaded_sb, xs):
    UNITS = T * SB_H
    G = SB_H * SB_PAD // P
    PER = P // SB_PAD
    PROJ = 3 * G + T
    wq, wk, wv2 = (sb_w[:, k * C * 512:(k + 1) * C * 512].rearrange("p (c n) -> p c n", c=C) for k in range(3))
    wo2 = sb_w[:, 3 * C * 512:3 * C * 512 + G * D].rearrange("p (c n) -> p c n", c=G)
    wv = sb_w[:, 3 * C * 512 + G * D:].rearrange("p (c n) -> p c n", c=C)
    with ExitStack() as ctx:
        taken = [0]

        def st(name, shape):
            size = int(np.prod(shape[1:]))
            flat = big[:, taken[0]:taken[0] + size]
            taken[0] += size
            names = "abc"[:len(shape) - 1]
            return flat.rearrange(f"p ({' '.join(names)}) -> p {' '.join(names)}",
                                  **{x: n for x, n in zip(names[:-1], shape[1:-1])}) if len(names) > 1 else flat

        def signal(name, per):
            return Signal(ctx, nc, name, per)

        qT, kT = st("qT", [P, G, N]), st("kT", [P, G, N])
        alone = [st(f"alone{i}", [P, G, PER * P]) for i in range(2)]
        dxT = st("dxT", [P, C, N])
        u = st("u", [P, T, SB_H * SB_PAD])
        v_add, v_mul = st("v_add", [P, G, N]), st("v_mul", [P, G, N])
        keep = [st(f"keep{i}", [P, N]) for i in range(2)]
        prod = [st(f"prod{i}", [P, N]) for i in range(3)]
        prodT = [st(f"prodT{i}", [P, N]) for i in range(2)]
        summed = st("summed", [P, G * P])
        oT = [st(f"oT{i}", [P, G * P]) for i in range(2)]

        ps_a, ps_l, ps_t, ps_o = bank[0:2], bank[2:4], bank[4:6], bank[6:8]

        u_cleared = ctx.enter_context(nc.semaphore("sb_u_cleared"))
        alone_cleared = ctx.enter_context(nc.semaphore("sb_alone_cleared"))
        zero_made = ctx.enter_context(nc.semaphore("sb_zero_made"))
        xs_cleared = ctx.enter_context(nc.semaphore("sb_xs_cleared"))
        zero = st("zero", [P, D])
        norm = Normalizer(ctx, nc, "sb_norm")
        staged = signal("sb_staged", 16)
        xT_ps = signal("sb_xT_ps", C)
        xT_done = signal("sb_xT", C)
        dx_done = signal("sb_dx", 1)
        proj_ps = signal("sb_proj_ps", PROJ)
        proj_done = signal("sb_proj", PROJ)
        alone_done = signal("sb_alone", T)
        logits = signal("sb_logits", UNITS)
        kept = signal("sb_keep", UNITS)
        prods = signal("sb_prods", UNITS)
        prods_t = signal("sb_prods_t", UNITS)
        prods_tc = signal("sb_prods_tc", UNITS)
        pv = signal("sb_pv", UNITS)
        sum_done = signal("sb_sum", T)
        oT_done = signal("sb_oT", T)
        out_ps = signal("sb_out_ps", T)
        h_done = signal("sb_h", T)
        every = [staged, xT_ps, xT_done, dx_done, proj_ps, proj_done, alone_done,
                 logits, kept, prods, prods_t, prods_tc, pv, sum_done, oT_done, out_ps, h_done]

        FINISH, PROJECT, ADD = 5, 7, 8

        with nc.Block() as block:
            @block.sync
            def _(sp):
                for s in every:
                    sp.sem_inc(s.sem, s.per)
                stage_batches(sp, True, xn, xn_all, norm.normed, staged, xT_ps)
                stage_batches(sp, False, xn, xn_all, norm.normed, staged, xT_ps)
                sp.wait_ge(zero_made, 1)
                sp.dma_start(xs.rearrange("(j p) n -> p j n", p=P),
                             zero.unsqueeze(1).to_broadcast([P, MOE_TILES, D])).then_inc(xs_cleared, 16)
                sp.wait_ge(xs_cleared, 16)

            @block.gpsimd
            def _(pool):
                norm.on_pool(pool, half)
                pool.memset(u, 0.0).then_inc(u_cleared, 1)
                pool.wait_ge(u_cleared, 1)
                ones = u[0:1, 0, :].rearrange("p (h e) -> p h e", e=SB_PAD)[:, :, SB_D:]
                pool.memset(ones, 1.0).then_inc(u_cleared, 1)

            @block.vector
            def _(dve):
                def isolate(b, i):
                    if i == 0:
                        dve.wait_ge(proj_done.sem, proj_done.at(b, G))
                    dve.wait_ge(logits.sem, logits.at(b, (i + 1 - 2) * SB_H))
                    for r in range(PER):
                        rows = slice(r * SB_PAD, (r + 1) * SB_PAD)
                        last = dve.tensor_copy(alone[i % 2][rows, :, r * P:(r + 1) * P],
                                               qT[rows, :, i * P:(i + 1) * P])
                    last.then_inc(alone_done.sem, 1)

                def finish(b, i):
                    dve.wait_ge(pv.sem, pv.at(b, (i + 1) * SB_H))
                    dve.wait_ge(oT_done.sem, oT_done.at(b, i))
                    if i == 0:
                        dve.wait_ge(proj_done.sem, proj_done.at(b, 3 * G))
                    blk = slice(i * P, (i + 1) * P)
                    dve.tensor_tensor(summed.rearrange("p (c n) -> p c n", c=G),
                                      ps_o[i % 2][:].rearrange("p (c n) -> p c n", c=G), v_add[:, :, blk],
                                      ALU.add).then_inc(sum_done.sem, 1)
                    dve.wait_ge(out_ps.sem, out_ps.at(b, i + 1 - 2))
                    dve.wait_ge(sum_done.sem, sum_done.at(b, i + 1))
                    dve.tensor_tensor(oT[i % 2].rearrange("p (c n) -> p c n", c=G),
                                      summed.rearrange("p (c n) -> p c n", c=G), v_mul[:, :, blk],
                                      ALU.mult).then_inc(oT_done.sem, 1)

                def add(b, i):
                    dve.wait_ge(out_ps.sem, out_ps.at(b, i + 1))
                    hs = batch_slice(h, b, i)
                    dve.tensor_tensor(hs, ps_a[i % 2][:, 0:D], hs, ALU.add).then_inc(h_done.sem, 1)

                for b in range(B):
                    norm.on_dve(dve, b, h, xn_all)
                dve.memset(zero, 0.0).then_inc(zero_made, 1)
                for i in range(2):
                    dve.memset(alone[i], 0.0).then_inc(alone_cleared, 1)
                dve.wait_ge(alone_cleared, 2)
                with dve.Fori(0, B) as b:
                    dve.wait_ge(proj_ps.sem, proj_ps.at(b, 0))
                    dve.wait_ge(xT_done.sem, xT_done.at(b, C))
                    dve.tensor_tensor(dxT, xT[:, :, 0:N], xT[:, :, 1:N + 1], ALU.subtract).then_inc(dx_done.sem, 1)
                    isolate(b, 0)
                    for n in range(UNITS):
                        i, hd = n // SB_H, n % SB_H
                        w = (i + 1) * P
                        dve.wait_ge(kept.sem, kept.at(b, n + 1))
                        dve.wait_ge(prods_t.sem, prods_t.at(b, n + 1 - 3))
                        dve.tensor_tensor_scan(prod[n % 3][:, 0:w][:, ::-1], keep[n % 2][:, 0:w][:, ::-1],
                                               scan_floor[:, N - w:N][:, ::-1], 0.0, ALU.mult,
                                               ALU.max).then_inc(prods.sem, 1)
                        if hd == 10 and i + 1 < T:
                            isolate(b, i + 1)
                        if i >= 1 and hd == FINISH:
                            finish(b, i - 1)
                        if i >= 1 and hd == ADD:
                            add(b, i - 1)
                    finish(b, T - 1)
                    add(b, T - 1)

            @block.scalar
            def _(act):
                def copy_t(b, n):
                    w = (n // SB_H + 1) * P
                    act.wait_ge(prods_t.sem, prods_t.at(b, n + 1))
                    act.wait_ge(pv.sem, pv.at(b, n + 1 - 2))
                    act.activation(prodT[n % 2][:, 0:w], ps_t[n % 2][:, 0:w], ACT.Copy).then_inc(prods_tc.sem, 1)

                act.wait_ge(u_cleared, 2)
                act.wait_ge(loaded_sb, 16 * 6)
                with act.Fori(0, B) as b:
                    for c in range(C):
                        act.wait_ge(xT_ps.sem, xT_ps.at(b, c + 1))
                        if c == 0:
                            act.wait_ge(proj_ps.sem, proj_ps.at(b, 0))
                            act.wait_ge(dx_done.sem, dx_done.at(b, 0))
                        act.activation(xT[:, c, 1:N + 1], ps_a[c][:], ACT.Copy).then_inc(xT_done.sem, 1)
                    for k in range(PROJ):
                        act.wait_ge(proj_ps.sem, proj_ps.at(b, k + 1))
                        src = ps_a[k % 2][:]
                        g = k % G
                        if k == 0:
                            act.wait_ge(logits.sem, logits.at(b, 0))
                            act.wait_ge(alone_done.sem, alone_done.at(b, 0))
                            act.wait_ge(oT_done.sem, oT_done.at(b, 0))
                            act.wait_ge(pv.sem, pv.at(b, 0))
                        if k < 2 * G:
                            ins = act.activation((qT if k < G else kT)[:, g, :], src, ACT.Copy)
                        elif k < 3 * G:
                            act.activation(v_add[:, g, :], src, ACT.Copy, scale=row_kind[:, 0:1])
                            ins = act.activation(v_mul[:, g, :], src, ACT.Identity, bias=row_kind[:, 0:1],
                                                 scale=row_kind[:, 1:2])
                        else:
                            ins = act.activation(
                                u[:, k - 3 * G, :].rearrange("p (h e) -> p h e", e=SB_PAD)[:, :, 0:SB_D],
                                ps_a[k % 2][:, 0:D].rearrange("p (h e) -> p h e", e=SB_D), ACT.Copy)
                        ins.then_inc(proj_done.sem, 1)
                    for n in range(UNITS + 2):
                        if n < UNITS:
                            w = (n // SB_H + 1) * P
                            act.wait_ge(logits.sem, logits.at(b, n + 1))
                            act.wait_ge(prods.sem, prods.at(b, n + 1 - 2))
                            act.activation(keep[n % 2][:, 0:w], ps_l[n % 2][:, 0:w], ACT.Sigmoid,
                                           scale=-float(SB_D) ** -0.5).then_inc(kept.sem, 1)
                        if n >= 2:
                            copy_t(b, n - 2)

            @block.tensor
            def _(pe):
                def transposes(b, n):
                    i = n // SB_H
                    pe.wait_ge(prods.sem, prods.at(b, n + 1))
                    pe.wait_ge(prods_tc.sem, prods_tc.at(b, n + 1 - 2))
                    for c in range(i + 1):
                        last = pe.transpose(ps_t[n % 2][:, c * P:(c + 1) * P], prod[n % 3][:, c * P:(c + 1) * P],
                                            ident[:])
                    last.then_inc(prods_t.sem, 1)

                def weigh(b, n):
                    i, hd = n // SB_H, n % SB_H
                    row, g = hd % PER * SB_PAD, hd // PER
                    if hd == 0:
                        pe.wait_ge(sum_done.sem, sum_done.at(b, i + 1 - 2))
                    pe.wait_ge(prods_tc.sem, prods_tc.at(b, n + 1))
                    for c in range(i + 1):
                        last = pe.matmul(ps_o[i % 2][row:row + SB_PAD, g * P:(g + 1) * P],
                                         u[:, c, hd * SB_PAD:(hd + 1) * SB_PAD], prodT[n % 2][:, c * P:(c + 1) * P],
                                         start=(c == 0), stop=(c == i))
                    last.then_inc(pv.sem, 1)

                def project_o(b, i):
                    pe.wait_ge(oT_done.sem, oT_done.at(b, i + 1))
                    pe.wait_ge(h_done.sem, h_done.at(b, i + 1 - 2))
                    for g in range(G):
                        last = pe.matmul(ps_a[i % 2][:, 0:D], oT[i % 2][:, g * P:(g + 1) * P], wo2[:, g, :],
                                         start=(g == 0), stop=(g == G - 1))
                    last.then_inc(out_ps.sem, 1)

                with pe.Fori(0, B) as b:
                    pe.wait_ge(h_done.sem, h_done.at(b, 0))
                    turn_staged(pe, b, xn, ident, ps_a, staged, xT_ps)
                    for k in range(PROJ):
                        if k == 0:
                            pe.wait_ge(xT_done.sem, xT_done.at(b, C))
                            pe.wait_ge(loaded_sb, 16 * 6)
                        if k == 3 * G:
                            pe.wait_ge(dx_done.sem, dx_done.at(b, 1))
                        if k >= 2:
                            pe.wait_ge(proj_done.sem, proj_done.at(b, k - 1))
                        for c in range(C):
                            g = k % G
                            if k < 3 * G:
                                last = pe.matmul(ps_a[k % 2][:], (wq, wk, wv2)[k // G][:, c, g * P:(g + 1) * P],
                                                 xT[:, c, 1:N + 1], start=(c == 0), stop=(c == C - 1))
                            else:
                                t = k - 3 * G
                                last = pe.matmul(ps_a[k % 2][:, 0:D], dxT[:, c, t * P:(t + 1) * P], wv[:, c, :],
                                                 start=(c == 0), stop=(c == C - 1))
                        last.then_inc(proj_ps.sem, 1)
                    for n in range(UNITS + 4):
                        if n < UNITS:
                            i, hd = n // SB_H, n % SB_H
                            if hd == 0:
                                pe.wait_ge(alone_done.sem, alone_done.at(b, i + 1))
                                pe.wait_ge(proj_done.sem, proj_done.at(b, 2 * G))
                            pe.wait_ge(kept.sem, kept.at(b, n + 1 - 2))
                            at = hd % PER * P
                            pe.matmul(ps_l[n % 2][:, 0:(i + 1) * P], alone[i % 2][:, hd // PER, at:at + P],
                                      kT[:, hd // PER, 0:(i + 1) * P], start=True, stop=True).then_inc(logits.sem, 1)
                        if 2 <= n < UNITS + 2:
                            transposes(b, n - 2)
                        if n == 4:
                            pe.wait_ge(proj_done.sem, proj_done.at(b, PROJ))
                        if n >= 4:
                            weigh(b, n - 4)
                        if n >= SB_H and n % SB_H == PROJECT and n < UNITS:
                            project_o(b, n // SB_H - 1)
                    project_o(b, T - 1)


def experts(nc, bank, h, half, share, slot, ident, xT, xn_all, router_w, big, xs, ys, router, w13, w2, next_loads, loaded_ca):
    PAIRS = MOE_TILES // 2
    W13 = big[:, 0:MOE_E * C * 2 * MOE_F].rearrange("p (e c f) -> p e c f", e=MOE_E, c=C)
    W2 = big[:, MOE_E * C * 2 * MOE_F:].rearrange("p (e c f) -> p e c f", e=MOE_E, c=MOE_F // P)
    FCH = MOE_F // P
    LEVELS = NT
    xs_tiles = xs.rearrange("(j p) n -> p j n", p=P)
    ys_tiles = ys.rearrange("(j p) n -> p j n", p=P)
    with ExitStack() as ctx:
        def st(name, shape, dt=F32):
            return ctx.enter_context(nc.sbuf_tensor(f"moe_{name}", shape, dt))

        def signal(name, per):
            return Signal(ctx, nc, f"moe_{name}", per)

        def sem(name):
            return ctx.enter_context(nc.semaphore(f"moe_{name}"))

        numbers_i = st("numbers_i", [P, MOE_TILES], I32)
        numbers = st("numbers", [P, MOE_TILES])
        levels = st("levels", [P, LEVELS])
        ones = st("ones", [P, P])
        below = st("below", [P, P])
        going_on = st("going_on", [P, MOE_E, NT])
        best = st("best", [P, NT, MOE_E])
        best_at = st("best_at", [P, NT, MOE_E], U32)
        best_f = st("best_f", [P, NT, MOE_E])
        gap = st("gap", [P, NT])
        chosen = [st(f"chosen{k}", [P, MOE_E, NT]) for k in range(2)]
        either = st("either", [P, MOE_E, NT])
        total = st("total", [P, MOE_E, NT])
        upto = st("upto", [P, MOE_E, NT])
        level_on = st("level_on", [P, MOE_E, LEVELS])
        filled = st("filled", [P, MOE_E])
        end = st("end", [P, MOE_E])
        first = st("first", [P, MOE_E])
        slot_e = st("slot_e", [P, MOE_E, NT])
        slot_f = st("slot_f", [P, 2, NT])
        passed = st("passed", [1, MOE_TILES, MOE_E])
        tile_f = st("tile_f", [1, MOE_TILES])
        tile_e = st("tile_e", [1, MOE_TILES], I32)
        x_in = st("x_in", [P, 2, D])
        x_inT = [st(f"x_inT{u}", [P, C * P]) for u in range(2)]
        act_gate = [st(f"act_gate{u}", [P, MOE_F]) for u in range(2)]
        hidden = [st(f"hidden{u}", [P, MOE_F]) for u in range(2)]
        hiddenT = [st(f"hiddenT{u}", [P, MOE_F]) for u in range(2)]
        y_out = st("y_out", [P, 2, D])

        norm = Normalizer(ctx, nc, "moe_norm")
        loaded_router, loaded_w = sem("loaded_router"), sem("loaded_w")
        xT_ps = sem("xT_ps")
        xT_done = sem("xT")
        routed = sem("routed")
        consts = sem("consts")
        route = sem("route")
        shares = sem("shares")
        counted = sem("counted")
        scattered = sem("scattered")
        x_loaded = signal("x_loaded", 16)
        x_ps = signal("x_ps", 2)
        x_done = signal("x", 2)
        gate_ps = signal("gate_ps", 2)
        up_ps = signal("up_ps", 2)
        gated = signal("gated", 2)
        hid = signal("hid", 2)
        hidT_ps = signal("hidT_ps", 2)
        hidT_done = signal("hidT", 2)
        down_ps = signal("down_ps", 2)
        y_done = signal("y", 2)
        stored = signal("stored", 16)
        every = [x_loaded, x_ps, x_done, gate_ps, up_ps, gated, hid, hidT_ps, hidT_done, down_ps, y_done, stored]

        R_BEST = NT
        R_GAP = R_BEST + 1
        R_INDEX = R_GAP + NT
        R_FLOAT = R_INDEX + 2
        R_CHOSEN = R_FLOAT + 2
        R_EITHER = R_CHOSEN + 1
        R_TOTAL = R_EITHER + 1
        R_UPTO = R_TOTAL + 1
        R_LEVELS = R_UPTO + 1
        R_FILLED = R_LEVELS + 1
        R_END = R_FILLED + 1
        R_FIRST = R_END + 2
        R_RANK = R_FIRST + 1
        R_SLOT_E = R_RANK + 1
        R_PICKED = R_SLOT_E + 2
        R_SLOT_F = R_PICKED + 2
        R_SLOT = R_SLOT_F + 1
        R_PASSED = R_SLOT + 1
        R_TILE_F = R_PASSED + 1
        R_CAPPED = R_TILE_F + 1
        R_TILE_E = R_CAPPED + 1

        with nc.Block() as block:
            @block.sync
            def _(sp):
                for s in every:
                    sp.sem_inc(s.sem, s.per)
                sp.dma_start(router_w[:, :, :], router.rearrange("(c p) n -> p c n", p=P)).then_inc(loaded_router, 16)
                for e in range(MOE_E):
                    sp.dma_start(W13[:, e], w13[e].rearrange("(c p) n -> p c n", p=P)).then_inc(loaded_w, 16)
                    sp.dma_start(W2[:, e], w2[e].rearrange("(c p) n -> p c n", p=P)).then_inc(loaded_w, 16)
                for dst, src in next_loads:
                    sp.dma_start(dst, src if len(src.shape) == 2 and src.shape[0] == P
                                 else src.rearrange("(c p) n -> p c n", p=P)).then_inc(loaded_ca, 16)
                sp.wait_ge(scattered, 16 * 2 * NT)
                with sp.Fori(0, PAIRS) as j:
                    sp.wait_ge(x_ps.sem, x_ps.at(j, 0))
                    sp.dma_start(x_in[:, :, :], xs_tiles[:, bass.ds(2 * j, 2), :]).then_inc(x_loaded.sem, 16)

            @block.gpsimd
            def _(pool):
                norm.on_pool(pool, half)
                pool.iota(numbers_i[:], pattern=[[1, MOE_TILES]], base=0, channel_multiplier=0).then_inc(consts, 1)
                pool.memset(ones[:], 1.0).then_inc(consts, 1)
                pool.memset(below[:], 1.0).then_inc(consts, 1)
                pool.memset(going_on[:, :, :], 1.0).then_inc(consts, 1)
                pool.wait_ge(consts, 4)
                pool.tensor_copy(numbers[:], numbers_i[:]).then_inc(consts, 1)
                pool.affine_select(out=below[:], in_=below[:], compare_op=ALU.is_ge, fill=0.0, base=-1,
                                   pattern=[[1, P]], channel_multiplier=-1).then_inc(consts, 1)
                pool.memset(going_on[:, :, 0:1], 0.0).then_inc(consts, 1)
                pool.wait_ge(route, R_SLOT)
                for t in range(NT):
                    for k in range(2):
                        pool.indirect_dma_start(xs, bass.IndirectOffsetOnAxis(ap=slot[:, k, t:t + 1], axis=0),
                                                xn_all[:, t, :], None).then_inc(scattered, 16)
                pool.wait_ge(stored.sem, stored.at(PAIRS - 1, 16))

            @block.vector
            def _(dve):
                def logits(t):
                    at = t % T * MOE_E
                    return bank[4 + t // T][:, at:at + MOE_E]

                for b in range(B):
                    norm.on_dve(dve, b, h, xn_all)
                for t in range(NT):
                    dve.wait_ge(routed, t // T + 1)
                    dve.max(best[:, t, :], logits(t)).then_inc(route, 1)
                dve.wait_ge(route, R_BEST)
                dve.tensor_sub(gap[:], best[:, :, 1], best[:, :, 0]).then_inc(route, 1)
                for t in range(NT):
                    dve.max_index(best_at[:, t, :], best[:, t, :], logits(t)).then_inc(route, 1)
                dve.wait_ge(route, R_INDEX)
                dve.tensor_copy(best_f[:, :, :], best_at[:, :, :]).then_inc(route, 1)
                dve.wait_ge(consts, 7)
                dve.tensor_scalar(levels[:], numbers[:, 0:LEVELS], float(P), None, ALU.mult).then_inc(route, 1)
                dve.wait_ge(route, R_FLOAT)
                for k in range(2):
                    dve.tensor_tensor(chosen[k][:, :, :],
                                      numbers[:, 0:MOE_E].unsqueeze(2).to_broadcast([P, MOE_E, NT]),
                                      best_f[:, :, k].unsqueeze(1).to_broadcast([P, MOE_E, NT]),
                                      ALU.is_equal).then_inc(route, 1)
                dve.wait_ge(route, R_CHOSEN)
                dve.tensor_tensor(either[:, :, :], chosen[0][:, :, :], chosen[1][:, :, :], ALU.add).then_inc(route, 1)
                dve.wait_ge(counted, 1)
                dve.tensor_copy(total[:, :, :].rearrange("p e t -> p (e t)"), bank[3][:, 128:256]).then_inc(route, 1)
                dve.wait_ge(route, R_TOTAL)
                dve.tensor_tensor_scan(upto[:, :, :].rearrange("p e t -> p (e t)"),
                                       going_on[:, :, :].rearrange("p e t -> p (e t)"),
                                       total[:, :, :].rearrange("p e t -> p (e t)"), 0.0, ALU.mult,
                                       ALU.add).then_inc(route, 1)
                dve.wait_ge(route, R_UPTO)
                dve.tensor_tensor(level_on[:, :, :],
                                  upto[:, :, NT - 1].unsqueeze(2).to_broadcast([P, MOE_E, LEVELS]),
                                  levels[:].unsqueeze(1).to_broadcast([P, MOE_E, LEVELS]),
                                  ALU.is_gt).then_inc(route, 1)
                dve.wait_ge(route, R_LEVELS)
                dve.tensor_reduce(filled[:], level_on[:, :, :], AX.X, ALU.add).then_inc(route, 1)
                dve.wait_ge(route, R_FILLED)
                dve.tensor_tensor_scan(end[:], ones[:, 0:MOE_E], filled[:], 0.0, ALU.mult, ALU.add).then_inc(route, 1)
                dve.wait_ge(route, R_END)
                dve.tensor_tensor(first[:], end[:], filled[:], ALU.subtract).then_inc(route, 1)
                dve.tensor_tensor(slot_e[:, :, :], upto[:, :, :], total[:, :, :], ALU.subtract).then_inc(route, 1)
                dve.wait_ge(route, R_FIRST)
                dve.tensor_tensor(slot_e[:, :, :], bank[3][:, 0:128].rearrange("p (e t) -> p e t", e=MOE_E),
                                  slot_e[:, :, :], ALU.add).then_inc(route, 1)
                dve.wait_ge(route, R_RANK)
                dve.scalar_tensor_tensor(slot_e[:, :, :], first[:].unsqueeze(2).to_broadcast([P, MOE_E, NT]),
                                         float(P), slot_e[:, :, :], ALU.mult, ALU.add).then_inc(route, 1)
                dve.wait_ge(route, R_SLOT_E)
                for k in range(2):
                    dve.tensor_tensor(chosen[k][:, :, :], chosen[k][:, :, :], slot_e[:, :, :],
                                      ALU.mult).then_inc(route, 1)
                dve.wait_ge(route, R_PICKED)
                for k in range(2):
                    dve.tensor_reduce(slot_f[:, k, :], chosen[k][:, :, :].rearrange("p e t -> p t e"), AX.X,
                                      ALU.add).then_inc(route, 1)
                dve.wait_ge(route, R_SLOT_F)
                dve.tensor_copy(slot[:, :, :], slot_f[:, :, :]).then_inc(route, 1)
                dve.tensor_tensor(passed[:, :, :], end[0:1, :].unsqueeze(1).to_broadcast([1, MOE_TILES, MOE_E]),
                                  numbers[0:1, :].unsqueeze(2).to_broadcast([1, MOE_TILES, MOE_E]),
                                  ALU.is_le).then_inc(route, 1)
                dve.wait_ge(route, R_PASSED)
                dve.tensor_reduce(tile_f[:], passed[:, :, :], AX.X, ALU.add).then_inc(route, 1)
                dve.wait_ge(route, R_TILE_F)
                dve.tensor_scalar(tile_f[:], tile_f[:], float(MOE_E - 1), None, ALU.min).then_inc(route, 1)
                dve.wait_ge(route, R_CAPPED)
                dve.tensor_copy(tile_e[:], tile_f[:]).then_inc(route, 1)

                with dve.Fori(0, PAIRS) as j:
                    def hide(u):
                        dve.wait_ge(gated.sem, gated.at(j, u + 1))
                        dve.wait_ge(up_ps.sem, up_ps.at(j, u + 1))
                        dve.wait_ge(hidT_ps.sem, hidT_ps.at(j, u + 1 - 2))
                        dve.tensor_tensor(hidden[u][:], bank[3 + 2 * u][:], act_gate[u][:],
                                          ALU.mult).then_inc(hid.sem, 1)

                    def copy_y(u):
                        dve.wait_ge(down_ps.sem, down_ps.at(j, u + 1))
                        dve.wait_ge(stored.sem, stored.at(j, 0))
                        dve.tensor_copy(y_out[:, u, :], bank[u][:, 0:D]).then_inc(y_done.sem, 1)

                    def copy_x(u):
                        dve.wait_ge(x_ps.sem, x_ps.at(j, u + 1))
                        dve.wait_ge(up_ps.sem, up_ps.at(j, u + 1 - 2))
                        dve.tensor_copy(x_inT[u][:], bank[u][:, 0:D]).then_inc(x_done.sem, 1)

                    def copy_hidden(u):
                        dve.wait_ge(hidT_ps.sem, hidT_ps.at(j, u + 1))
                        dve.wait_ge(down_ps.sem, down_ps.at(j, u + 1 - 2))
                        dve.tensor_copy(hiddenT[u][:], bank[6 + u][:]).then_inc(hidT_done.sem, 1)

                    copy_x(0)
                    copy_x(1)
                    hide(0)
                    copy_hidden(0)
                    hide(1)
                    copy_y(0)
                    copy_hidden(1)
                    copy_y(1)


            @block.scalar
            def _(act):
                for b in range(B):
                    for c in range(C):
                        act.wait_ge(xT_ps, b * C + c + 1)
                        if b >= 1:
                            act.wait_ge(routed, b)
                        act.activation(xT[:, c, 1:N + 1], bank[b % 2 * C + c][:], ACT.Copy).then_inc(xT_done, 1)
                act.wait_ge(route, R_GAP)
                act.activation(share[:, 0, :], gap[:], ACT.Sigmoid, scale=-1.0).then_inc(shares, 1)
                act.activation(share[:, 1, :], gap[:], ACT.Sigmoid).then_inc(shares, 1)
                with act.Fori(0, PAIRS) as j:
                    for u in range(2):
                        act.wait_ge(gate_ps.sem, gate_ps.at(j, u + 1))
                        act.wait_ge(hid.sem, hid.at(j, u + 1 - 2))
                        act.activation(act_gate[u][:], bank[2 + 2 * u][:], ACT.Silu).then_inc(gated.sem, 1)
                    act.wait_ge(y_done.sem, y_done.at(j, 2))
                    act.dma_start(ys_tiles[:, bass.ds(2 * j, 2), :], y_out[:, :, :]).then_inc(stored.sem, 16)

            @block.tensor
            def _(pe):
                def turn(b):
                    pe.wait_ge(norm.normed, (b + 1) * T)
                    for c in range(C):
                        if b >= 2:
                            pe.wait_ge(xT_done, (b - 2) * C + c + 1)
                        for t in range(T):
                            last = pe.transpose(bank[b % 2 * C + c][:, t * P:(t + 1) * P],
                                                xn_all[:, b * T + t, c * P:(c + 1) * P], ident[:])
                        last.then_inc(xT_ps, 1)

                turn(0)
                pe.wait_ge(loaded_router, 16)
                for b in range(B):
                    if b + 1 < B:
                        turn(b + 1)
                    pe.wait_ge(xT_done, (b + 1) * C)
                    for t in range(T):
                        for c in range(C):
                            last = pe.matmul(bank[4 + b][:, t * MOE_E:(t + 1) * MOE_E],
                                             xT[:, c, 1 + t * P:1 + (t + 1) * P], router_w[:, c, :],
                                             start=(c == 0), stop=(c == C - 1))
                    last.then_inc(routed, 1)

                pe.wait_ge(consts, 7)
                pe.wait_ge(route, R_EITHER)
                chose = either[:, :, :].rearrange("p e t -> p (e t)")
                pe.matmul(bank[3][:, 0:128], below[:], chose, start=True, stop=True)
                pe.matmul(bank[3][:, 128:256], ones[:], chose, start=True, stop=True).then_inc(counted, 1)
                pe.wait_ge(loaded_w, 16 * 2 * MOE_E)
                pe.wait_ge(route, R_TILE_E)
                with pe.Fori(0, PAIRS) as j:
                    def turn_in(u):
                        pe.wait_ge(x_loaded.sem, x_loaded.at(j, 16))
                        pe.wait_ge(y_done.sem, y_done.at(j, u + 1 - 2))
                        for c in range(C):
                            last = pe.transpose(bank[u][:, c * P:(c + 1) * P], x_in[:, u, c * P:(c + 1) * P], ident[:])
                        last.then_inc(x_ps.sem, 1)

                    def widen(u, part, expert, done):
                        for c in range(C):
                            w = W13[:, bass.ds(expert, 1), c, part * MOE_F:(part + 1) * MOE_F]
                            last = pe.matmul(bank[2 + 2 * u + part][:], x_inT[u][:, c * P:(c + 1) * P],
                                             w.rearrange("p e f -> p (e f)"), start=(c == 0), stop=(c == C - 1))
                        last.then_inc(done.sem, 1)

                    def turn_hidden(u):
                        pe.wait_ge(hid.sem, hid.at(j, u + 1))
                        pe.wait_ge(hidT_done.sem, hidT_done.at(j, u + 1 - 2))
                        for c in range(FCH):
                            last = pe.transpose(bank[6 + u][:, c * P:(c + 1) * P], hidden[u][:, c * P:(c + 1) * P],
                                                ident[:])
                        last.then_inc(hidT_ps.sem, 1)

                    def narrow(u, expert):
                        pe.wait_ge(hidT_done.sem, hidT_done.at(j, u + 1))
                        for c in range(FCH):
                            last = pe.matmul(bank[u][:, 0:D], hiddenT[u][:, c * P:(c + 1) * P],
                                             W2[:, bass.ds(expert, 1), c, :].rearrange("p e f -> p (e f)"),
                                             start=(c == 0), stop=(c == FCH - 1))
                        last.then_inc(down_ps.sem, 1)

                    expert = [pe.value_load(tile_e[0:1, bass.ds(2 * j + u, 1)], min_val=0, max_val=MOE_E - 1)
                              for u in range(2)]
                    turn_in(0)
                    turn_in(1)
                    for u in range(2):
                        pe.wait_ge(x_done.sem, x_done.at(j, u + 1))
                        pe.wait_ge(gated.sem, gated.at(j, u + 1 - 2))
                        widen(u, 0, expert[u], gate_ps)
                        if u == 1:
                            turn_hidden(0)
                        pe.wait_ge(hid.sem, hid.at(j, u + 1 - 2))
                        widen(u, 1, expert[u], up_ps)
                    narrow(0, expert[0])
                    turn_hidden(1)
                    narrow(1, expert[1])


class Attention:

    def __init__(self, ctx, nc, bank, name, keys, masks, ident, ident_bf, window_mask, wo, q_odd):
        def st(what, shape):
            return ctx.enter_context(nc.sbuf_tensor(f"{name}_{what}", shape, F32))

        def signal(what, per):
            return Signal(ctx, nc, f"{name}_{what}", per)

        self.keys, self.masks = keys, masks
        self.ident, self.ident_bf, self.window_mask, self.wo = ident, ident_bf, window_mask, wo
        self.UNITS = T * CA_H
        self.q = [st("q_even", [P, INNER // P, N])[:, :, :], q_odd.rearrange("p (c n) -> p c n", n=N)]
        self.q_cleared = ctx.enter_context(nc.semaphore(f"{name}_q_cleared"))
        self.kT = st("kT", [P, INNER // P, N])
        self.v = st("v", [P, T, INNER])
        self.neg_max = st("neg_max", [P, self.UNITS])
        self.sums = st("sums", [P, self.UNITS])
        self.inv = st("inv", [P, self.UNITS])
        self.prob = [st(f"prob{i}", [P, N]) for i in range(4)]
        self.probT = [st(f"probT{i}", [P, N]) for i in range(2)]
        self.oT_all = st("oT", [P, 2, INNER // P, P])
        self.oT = [self.oT_all[:, i] for i in range(2)]
        self.ps_a, self.ps_l, self.ps_t, self.ps_o = bank[0:2], bank[2:4], bank[4:6], bank[6:8]
        self.logits = signal("logits", self.UNITS)
        self.maxed = signal("maxed", self.UNITS)
        self.probs = signal("probs", self.UNITS)
        self.inverted = signal("inverted", self.UNITS)
        self.scaled = signal("scaled", self.UNITS)
        self.probs_t = signal("probs_t", self.UNITS)
        self.probs_tc = signal("probs_tc", self.UNITS)
        self.pv = signal("pv", self.UNITS)
        self.oT_done = signal("oT", T)
        self.out_ps = signal("out_ps", T)
        self.h_done = signal("h", T)
        self.every = [self.logits, self.maxed, self.probs, self.inverted, self.scaled, self.probs_t,
                      self.probs_tc, self.pv, self.oT_done, self.out_ps, self.h_done]


def clear_q(pool, a):
    for parity in range(2):
        pool.memset(a.q[parity], 0.0).then_inc(a.q_cleared, 1)


def copy_q(act, a, chunks, tokens, src, scale=1.0):
    for parity in range(2):
        own = slice(parity * CA_D, (parity + 1) * CA_D)
        last = act.activation(a.q[parity][own, chunks, tokens], src[own], ACT.Copy, scale=scale)
    return last


TAIL = 5


def attend_pe(pe, b, a, between=()):
    def others(n):
        for at, step in between:
            if at == n:
                step()

    def transposes(n):
        w = len(a.keys(n // CA_H))
        pe.wait_ge(a.scaled.sem, a.scaled.at(b, n + 1))
        pe.wait_ge(a.probs_tc.sem, a.probs_tc.at(b, n + 1 - 2))
        for c in range(w):
            last = pe.transpose(a.ps_t[n % 2][:, c * P:(c + 1) * P], a.prob[n % 4][:, c * P:(c + 1) * P],
                                a.ident[:])
        last.then_inc(a.probs_t.sem, 1)

    def weigh(n):
        i, hd = n // CA_H, n % CA_H
        row, ch = hd % 2 * CA_D, hd // 2
        if hd == 0:
            pe.wait_ge(a.oT_done.sem, a.oT_done.at(b, i + 1 - 2))
        pe.wait_ge(a.probs_tc.sem, a.probs_tc.at(b, n + 1))
        keys = a.keys(i)
        for c, key in enumerate(keys):
            last = pe.matmul(a.ps_o[i % 2][row:row + CA_D, ch * P:(ch + 1) * P],
                             a.v[:, key, hd * CA_D:(hd + 1) * CA_D], a.probT[n % 2][:, c * P:(c + 1) * P],
                             start=(c == 0), stop=(c == len(keys) - 1))
        last.then_inc(a.pv.sem, 1)

    def project_o(i):
        pe.wait_ge(a.oT_done.sem, a.oT_done.at(b, i + 1))
        pe.wait_ge(a.h_done.sem, a.h_done.at(b, i + 1 - 2))
        for c in range(INNER // P):
            last = pe.matmul(a.ps_a[i % 2][:, 0:D], a.oT[i % 2][:, c, :], a.wo[:, c, :], start=(c == 0),
                             stop=(c == INNER // P - 1))
        last.then_inc(a.out_ps.sem, 1)

    for n in range(a.UNITS + 4):
        if n < a.UNITS:
            others(n)
            i, hd = n // CA_H, n % CA_H
            keys, m = a.keys(i), a.masks(i)
            w = len(keys) * P
            ch = hd // 2
            pe.wait_ge(a.probs.sem, a.probs.at(b, n + 1 - 2))
            q = a.q[hd % 2][:, ch, i * P:(i + 1) * P]
            cut, first = w - m * P, keys[0] * P
            if cut:
                pe.matmul(a.ps_l[n % 2][:, 0:cut], q, a.kT[:, ch, first:first + cut], start=True,
                          stop=True)
            pe.matmul(a.ps_l[n % 2][:, cut:w], a.ident_bf[:],
                      a.window_mask[:, 2 - m:2, :].rearrange("p m k -> p (m k)"), start=True, stop=False)
            pe.matmul(a.ps_l[n % 2][:, cut:w], q, a.kT[:, ch, first + cut:first + w], start=False,
                      stop=True).then_inc(a.logits.sem, 1)
        if 2 <= n < a.UNITS + 2:
            transposes(n - 2)
        if 4 <= n:
            weigh(n - 4)
        if n >= CA_H and n % CA_H == TAIL and n < a.UNITS:
            project_o(n // CA_H - 1)
    others(a.UNITS)
    project_o(T - 1)


def attend_act(act, b, a, between=()):
    def copy_t(n):
        w = len(a.keys(n // CA_H)) * P
        act.wait_ge(a.probs_t.sem, a.probs_t.at(b, n + 1))
        act.wait_ge(a.pv.sem, a.pv.at(b, n + 1 - 2))
        act.activation(a.probT[n % 2][:, 0:w], a.ps_t[n % 2][:, 0:w], ACT.Copy).then_inc(a.probs_tc.sem, 1)

    def copy_o(i):
        act.wait_ge(a.pv.sem, a.pv.at(b, (i + 1) * CA_H))
        act.wait_ge(a.out_ps.sem, a.out_ps.at(b, i + 1 - 2))
        act.activation(a.oT[i % 2].rearrange("p c n -> p (c n)"), a.ps_o[i % 2][:],
                       ACT.Copy).then_inc(a.oT_done.sem, 1)

    for n in range(a.UNITS + 3):
        for at, step in between:
            if at == n:
                step()
        if n < a.UNITS:
            w = len(a.keys(n // CA_H)) * P
            act.wait_ge(a.maxed.sem, a.maxed.at(b, n + 1))
            act.wait_ge(a.probs_t.sem, a.probs_t.at(b, n + 1 - 4))
            act.activation(a.prob[n % 4][:, 0:w], a.ps_l[n % 2][:, 0:w], ACT.Exp, bias=a.neg_max[:, n:n + 1],
                           accum_out=a.sums[:, n:n + 1]).then_inc(a.probs.sem, 1)
        if n >= 3:
            copy_t(n - 3)
        if n >= CA_H and n % CA_H == TAIL - 1 and n < a.UNITS:
            copy_o(n // CA_H - 1)
    copy_o(T - 1)


def attend_dve(dve, b, a, h, gate, between=()):
    def scale(n):
        i, hd = n // CA_H, n % CA_H
        w = len(a.keys(i)) * P
        dve.wait_ge(a.probs.sem, a.probs.at(b, n + 1))
        dve.reciprocal(a.inv[:, n:n + 1], a.sums[:, n:n + 1]).then_inc(a.inverted.sem, 1)
        dve.wait_ge(a.inverted.sem, a.inverted.at(b, n + 1))
        prob = a.prob[n % 4][:, 0:w]
        if gate is None:
            dve.tensor_scalar(prob, prob, a.inv[:, n:n + 1], None, ALU.mult).then_inc(a.scaled.sem, 1)
        else:
            dve.tensor_scalar(prob, prob, a.inv[:, n:n + 1], gate[:, i, hd:hd + 1], ALU.mult,
                              ALU.mult).then_inc(a.scaled.sem, 1)

    def add(i):
        dve.wait_ge(a.out_ps.sem, a.out_ps.at(b, i + 1))
        hs = batch_slice(h, b, i)
        dve.tensor_tensor(hs, a.ps_a[i % 2][:, 0:D], hs, ALU.add).then_inc(a.h_done.sem, 1)

    for n in range(a.UNITS + 1):
        for at, step in between:
            if at == n:
                step()
        if n < a.UNITS:
            w = len(a.keys(n // CA_H)) * P
            dve.wait_ge(a.logits.sem, a.logits.at(b, n + 1))
            dve.tensor_reduce(a.neg_max[:, n:n + 1], a.ps_l[n % 2][:, 0:w], AX.X, ALU.max,
                              negate=True).then_inc(a.maxed.sem, 1)
        if n >= 1:
            scale(n - 1)
        if n >= CA_H and n % CA_H == TAIL + 2 and n < a.UNITS:
            add(n // CA_H - 1)
    add(T - 1)


def causal(nc, bank, h, half, share, slot, ys, big, ident, ident_bf, window_mask, xn_all, xn, xT, ca_w, ca_wo_w, gates_w, rms_col, early_w,
           late_loads, loaded_late, loaded_ca):
    QC = INNER // P
    PROJ = 2 * QC + T + 1
    with ExitStack() as ctx:
        def st(name, shape, dt=F32):
            return ctx.enter_context(nc.sbuf_tensor(f"ca_{name}", shape, dt))

        def signal(name, per):
            return Signal(ctx, nc, name, per)

        a = Attention(ctx, nc, bank, "ca", lambda i: list(range(i + 1)), lambda i: 1, ident, ident_bf,
                      window_mask, ca_wo_w, early_w[:, 2 * D * T + N:2 * D * T + N + INNER // P * N])
        gate_e, gate = st("gate_e", [P, T, CA_H]), st("gate", [P, T, CA_H])

        norm = Normalizer(ctx, nc, "ca_norm", rms=True)
        y_in = big[:, 0:2 * NT * D].rearrange("p (k t n) -> p k t n", k=2, t=NT)
        gathered = [ctx.enter_context(nc.semaphore(f"ca_gathered{b}")) for b in range(B)]
        combined = ctx.enter_context(nc.semaphore("ca_combined"))
        staged = signal("ca_staged", 16)
        xT_ps = signal("ca_xT_ps", C)
        xT_done = signal("ca_xT", C)
        proj_ps = signal("ca_proj_ps", PROJ)
        proj_done = signal("ca_proj", PROJ)
        gate_done = signal("ca_gate", 2)
        every = [staged, xT_ps, xT_done, proj_ps, proj_done, gate_done] + a.every

        with nc.Block() as block:
            @block.sync
            def _(sp):
                for s in every:
                    sp.sem_inc(s.sem, s.per)
                stage_batches(sp, True, xn, xn_all, norm.normed, staged, xT_ps)
                sp.wait_ge(combined, 2 * NT)
                for dst, src in late_loads:
                    sp.dma_start(dst, src).then_inc(loaded_late, 16)
                stage_batches(sp, False, xn, xn_all, norm.normed, staged, xT_ps)

            @block.gpsimd
            def _(pool):
                clear_q(pool, a)
                for t in range(NT):
                    for k in range(2):
                        pool.indirect_dma_start(y_in[:, k, t, :], None, ys,
                                                bass.IndirectOffsetOnAxis(ap=slot[:, k, t:t + 1],
                                                                          axis=0)).then_inc(gathered[t // T], 16)
                norm.on_pool(pool, half)

            @block.vector
            def _(dve):
                for b in range(B):
                    dve.wait_ge(gathered[b], 16 * 2 * T)
                    for k in range(2):
                        if k == 1:
                            dve.wait_ge(combined, (2 * b + 1) * T)
                        for t in range(b * T, (b + 1) * T):
                            dve.scalar_tensor_tensor(h[:, t, :], y_in[:, k, t, :], share[:, k, t:t + 1], h[:, t, :],
                                                     ALU.mult, ALU.add).then_inc(combined, 1)
                    dve.wait_ge(combined, 2 * T * (b + 1))
                    norm.on_dve(dve, b, h, xn_all)
                with dve.Fori(0, B) as b:
                    dve.wait_ge(proj_done.sem, proj_done.at(b, PROJ))
                    dve.tensor_scalar(gate_e[:, :, :], gate_e[:, :, :], 1.0, None, ALU.add).then_inc(gate_done.sem, 1)
                    dve.wait_ge(gate_done.sem, gate_done.at(b, 1))
                    dve.reciprocal(gate[:, :, :], gate_e[:, :, :]).then_inc(gate_done.sem, 1)
                    dve.wait_ge(gate_done.sem, gate_done.at(b, 2))
                    attend_dve(dve, b, a, h, gate)

            @block.scalar
            def _(act):
                act.wait_ge(a.q_cleared, 2)
                act.wait_ge(loaded_ca, 16 * 6)
                with act.Fori(0, B) as b:
                    for c in range(C):
                        act.wait_ge(proj_ps.sem, proj_ps.at(b, 0))
                        act.wait_ge(xT_ps.sem, xT_ps.at(b, c + 1))
                        act.activation(xT[:, c, 1:N + 1], a.ps_a[c][:], ACT.Identity,
                                       scale=rms_col[:, c:c + 1]).then_inc(xT_done.sem, 1)
                    for k in range(PROJ):
                        if k == 0:
                            act.wait_ge(a.pv.sem, a.pv.at(b, 0))
                            act.wait_ge(gate_done.sem, gate_done.at(b, 0))
                        act.wait_ge(proj_ps.sem, proj_ps.at(b, k + 1))
                        src = a.ps_a[k % 2][:]
                        if k < QC:
                            ins = copy_q(act, a, k, slice(0, N), src, float(CA_D) ** -0.5)
                        elif k < 2 * QC:
                            ins = act.activation(a.kT[:, k - QC, :], src, ACT.Copy)
                        elif k < 2 * QC + T:
                            ins = act.activation(a.v[:, k - 2 * QC, :], src, ACT.Copy)
                        else:
                            ins = act.activation(gate_e[:, :, :].rearrange("p t h -> p (t h)"),
                                                 a.ps_a[k % 2][:, 0:T * CA_H], ACT.Exp, scale=-1.0)
                        ins.then_inc(proj_done.sem, 1)
                    attend_act(act, b, a)

            @block.tensor
            def _(pe):
                pe.wait_ge(loaded_ca, 16 * 6)
                with pe.Fori(0, B) as b:
                    pe.wait_ge(a.oT_done.sem, a.oT_done.at(b, 0))
                    pe.wait_ge(a.h_done.sem, a.h_done.at(b, 0))
                    turn_staged(pe, b, xn, ident, a.ps_a, staged, xT_ps)
                    for k in range(PROJ):
                        if k == 0:
                            pe.wait_ge(xT_done.sem, xT_done.at(b, C))
                        if k >= 2:
                            pe.wait_ge(proj_done.sem, proj_done.at(b, k - 1))
                        if k < 2 * QC:
                            for c in range(C):
                                last = pe.matmul(a.ps_a[k % 2][:], ca_w[:, c, k * P:(k + 1) * P],
                                                 xT[:, c, 1:N + 1], start=(c == 0), stop=(c == C - 1))
                        elif k < 2 * QC + T:
                            t = k - 2 * QC
                            for c in range(C):
                                last = pe.matmul(a.ps_a[k % 2][:], xT[:, c, 1 + t * P:1 + (t + 1) * P],
                                                 ca_w[:, c, 2 * INNER:], start=(c == 0), stop=(c == C - 1))
                        else:
                            for t in range(T):
                                for c in range(C):
                                    last = pe.matmul(a.ps_a[k % 2][:, t * CA_H:(t + 1) * CA_H],
                                                     xT[:, c, 1 + t * P:1 + (t + 1) * P], gates_w[:, c, :],
                                                     start=(c == 0), stop=(c == C - 1))
                        last.then_inc(proj_ps.sem, 1)
                    pe.wait_ge(proj_done.sem, proj_done.at(b, PROJ))
                    attend_pe(pe, b, a)


LATE_SHAPES = {
    "wqkv": [DEPTH, C, 3 * INNER],
    "wo": [DEPTH, INNER // P, D],
    "w1": [DEPTH, C, 2 * HID],
    "w2": [DEPTH, FC, D],
    "ln_g": [DEPTH, C],
    "ln_b": [DEPTH, C],
    "b1": [DEPTH, 2, FC],
    "trig": [T, 4 * CA_D],
    "qk_scale": [DEPTH, 4 * CA_D],
    "spare": [FC * N],
}
LATE_SIZE = sum(int(np.prod(x)) for x in LATE_SHAPES.values())


def late_views(big):
    views, at = {}, 0
    for name, shape in LATE_SHAPES.items():
        size = int(np.prod(shape))
        flat = big[:, at:at + size]
        letters = "abc"[:len(shape)]
        views[name] = flat.rearrange(f"p ({' '.join(letters)}) -> p {' '.join(letters)}",
                                     **{x: n for x, n in zip(letters[:-1], shape[:-1])})
        at += size
    return views, at


def late_loads(views, b2_row, wqkv, ffn_wo, w1, w2f, trig, qk_scale, ln_g, ln_b, b1, b2):
    loads = []
    full = (FC - 1) * P
    for l in range(DEPTH):
        loads += [(views["wqkv"][:, l], wqkv[l].rearrange("(c p) n -> p c n", p=P)),
                  (views["wo"][:, l], ffn_wo[l].rearrange("(c p) n -> p c n", p=P)),
                  (views["w1"][:, l], w1[l].rearrange("(c p) n -> p c n", p=P)),
                  (views["w2"][:, l, 0:FC - 1], w2f[l, 0:full, :].rearrange("(c p) n -> p c n", p=P)),
                  (views["w2"][0:HID - full, l, FC - 1], w2f[l, full:HID, :])]
    loads += [(views["ln_g"], ln_g.rearrange("p (l c) -> p l c", c=C)),
              (views["ln_b"], ln_b.rearrange("p (l c) -> p l c", c=C)),
              (views["b1"], b1), (views["trig"], trig), (views["qk_scale"], qk_scale), (b2_row[:, :], b2)]
    return loads


def local_layers(nc, bank, h, pause, ident, ident_bf, window_mask, half, one_row, xn, xT, w, b2_row, kept, depth,
                 loaded_late, n_late):
    HD2 = CA_D // 2
    TH, NH = T // 2, N // 2
    LN_STEPS = 3 * TH + 1
    DOWN_AFTER = [FC + 2, FC + 3]
    TURN_N = 5
    TURN_AT, COPY_AT, SCALE_AT, NORM_AT = 6, 7, 3, 3 * CA_H + 3
    with ExitStack() as ctx:
        def st(name, shape, dt=F32):
            return ctx.enter_context(nc.sbuf_tensor(f"local_{name}", shape, dt))

        def signal(name, per):
            return Signal(ctx, nc, f"local_{name}", per)

        a = Attention(ctx, nc, bank, "local", lambda i: list(range(max(i - 1, 0), i + 1)),
                      lambda i: min(i + 1, 2), ident, ident_bf, window_mask, None,
                      w["early_a"][:, 2 * D * T + N:2 * D * T + N + INNER // P * N])
        straight = [w["early_a"][:, i * 2 * INNER:(i + 1) * 2 * INNER] for i in range(2)]
        table = w["early_b"][:, 0:T * 4 * CA_D].rearrange("p (t n) -> p t n", t=T)
        squares = [w["spare"][:, i * 2 * INNER:(i + 1) * 2 * INNER] for i in range(2)]
        crossed = [w["spare"][:, 4 * INNER:6 * INNER],
                   a.oT_all[:, :, :, :].rearrange("p i c n -> p (i c n)")]
        norm_sq, rnorm = st("norm_sq", [P, T, 16]), st("rnorm", [P, T, 16])
        shifted = st("shifted", [P, T, P])
        stats, moments = st("stats", [P, T, 12]), st("moments", [P, T, 2])
        var_eps, rstd = st("var_eps", [P, T]), st("rstd", [P, T])
        act_gate = [a.prob[0], a.prob[1]]
        hidden = w["spare"].rearrange("p (c n) -> p c n", c=FC)

        norm = Normalizer(ctx, nc, "enter_norm")
        copied = ctx.enter_context(nc.semaphore("enter_kept"))
        table_done = ctx.enter_context(nc.semaphore("local_table"))
        staged = signal("staged", 16)
        xT_ps = signal("xT_ps", C)
        xT_done = signal("xT", C)
        qkv_ps = signal("qkv_ps", 3 * T)
        squared = signal("squared", 2 * T)
        v_done = signal("v", T)
        rotary = signal("rotary", 4 * T)
        norms = signal("norms", 2 * T)
        rnorm_done = signal("rnorm", T)
        rotated = signal("rotated", 2 * T)
        q_scaled = signal("q_scaled", T)
        qkT_ps = signal("qkT_ps", T)
        qkT_done = signal("qkT", 2 * T)
        shift_done = [signal(f"shift{half}", 32) for half in range(2)]
        moments_done = signal("moments", 2 * LN_STEPS)
        rstd_done = signal("rstd", 2)
        normed = signal("normed", 2 * T)
        nT_ps = signal("nT_ps", 2)
        nT_done = signal("nT", 2 * C)
        up_ps = signal("up_ps", 2 * FC)
        gated = signal("gated", 2 * FC)
        hid = signal("hidden", 2 * FC)
        down_ps = signal("down_ps", T)
        h_done = signal("h2", T)
        every = [staged, xT_ps, xT_done, qkv_ps, squared, v_done, rotary, norms, rnorm_done, rotated,
                 q_scaled, qkT_ps, qkT_done, *shift_done, moments_done, rstd_done, normed, nT_ps, nT_done, up_ps, gated,
                 hid, down_ps, h_done] + a.every
        ps_a = a.ps_a

        for layer in range(depth):
            wqkv, w1, w2 = w["wqkv"][:, layer], w["w1"][:, layer], w["w2"][:, layer]
            a.wo = w["wo"][:, layer]
            with nc.Block() as block:
                @block.sync
                def _(sp):
                    if layer == 0:
                        for s in every:
                            sp.sem_inc(s.sem, s.per)
                    with sp.Fori(0, B) as b:
                        if layer == 0:
                            sp.wait_ge(norm.normed, b * T + T)
                        sp.wait_ge(nT_ps.sem, nT_ps.at(b, 0))
                        sp.dma_start(xn[:, :, :], h[:, bass.ds(b * T, T), :]).then_inc(staged.sem, 16)
                        for u in range(2):
                            t0 = u * TH
                            sp.wait_ge(a.h_done.sem, a.h_done.at(b, t0 + TH))
                            sp.dma_start(shifted[1:P, t0:t0 + TH, :],
                                         h[0:P - 1, t0:NT, P:2 * P][:, bass.ds(b * T, TH), :]).then_inc(shift_done[u].sem, 16)
                            t1 = max(t0, 1)
                            sp.dma_start(shifted[0:1, t1:t0 + TH, :],
                                         h[P - 1:P, t1 - 1:NT, P:2 * P][:, bass.ds(b * T, t0 + TH - t1), :]).then_inc(shift_done[u].sem, 16)

                @block.gpsimd
                def _(pool):
                    if layer == 0:
                        norm.on_pool(pool, half)
                        clear_q(pool, a)
                    with pool.Fori(0, B) as b:
                        for t in range(T):
                            pool.wait_ge(rotary.sem, rotary.at(b, 4 * t + 4))
                            pool.wait_ge(qkT_ps.sem, qkT_ps.at(b, t + 1 - 2))
                            pool.tensor_tensor(straight[t % 2], straight[t % 2], crossed[t % 2],
                                               ALU.add).then_inc(rotated.sem, 1)
                            pool.wait_ge(norms.sem, norms.at(b, 2 * t + 2))
                            pool.tensor_tensor(rnorm[:, t, :], norm_sq[:, t, :], half[:], ALU.pow).then_inc(rnorm_done.sem, 1)
                            pool.wait_ge(rnorm_done.sem, rnorm_done.at(b, t + 1))
                            pool.wait_ge(rotated.sem, rotated.at(b, 2 * t + 1))
                            keys = straight[t % 2][:, INNER:].rearrange("p (h d) -> p h d", d=CA_D)
                            pool.tensor_tensor(keys, keys, rnorm[:, t, CA_H:].unsqueeze(2).to_broadcast([P, CA_H, CA_D]),
                                               ALU.mult).then_inc(rotated.sem, 1)
                        for u in range(2):
                            pool.wait_ge(moments_done.sem, moments_done.at(b, (u + 1) * LN_STEPS))
                            mine = slice(u * TH, (u + 1) * TH)
                            pool.tensor_tensor(rstd[:, mine], var_eps[:, mine], half[:, 0:TH],
                                               ALU.pow).then_inc(rstd_done.sem, 1)

                @block.vector
                def _(dve):
                    def add_down(b, t):
                        dve.wait_ge(down_ps.sem, down_ps.at(b, t + 1))
                        hs = batch_slice(h, b, t)
                        dve.tensor_tensor(hs, bank[6 + t % 2][:, 0:D], hs, ALU.add).then_inc(h_done.sem, 1)

                    if layer == 0:
                        dve.memset(shifted[0:1, 0, :], 0.0)
                        for b in range(B):
                            dve.wait_ge(copied, b + 1)
                            norm.on_dve(dve, b, h, h)
                    dve.wait_ge(loaded_late, 16 * n_late)
                    dve.tensor_tensor(table[:, :, :], w["trig"],
                                      w["qk_scale"][:, layer, :].unsqueeze(1).to_broadcast([P, T, 4 * CA_D]),
                                      ALU.mult).then_inc(table_done, 1)
                    dve.wait_ge(table_done, layer + 1)
                    with dve.Fori(0, B) as b:
                        def scale_q(t):
                            dve.wait_ge(rnorm_done.sem, rnorm_done.at(b, t + 1))
                            dve.wait_ge(rotated.sem, rotated.at(b, 2 * t + 1))
                            queries = straight[t % 2][:, 0:INNER].rearrange("p (h d) -> p h d", d=CA_D)
                            dve.tensor_tensor(queries, queries,
                                              rnorm[:, t, 0:CA_H].unsqueeze(2).to_broadcast([P, CA_H, CA_D]),
                                              ALU.mult).then_inc(q_scaled.sem, 1)

                        def own_half(u):
                            tiles = range(u * TH, (u + 1) * TH)
                            dve.wait_ge(a.h_done.sem, a.h_done.at(b, (u + 1) * TH))
                            dve.memset(pause[:], 0.0)
                            for t in tiles:
                                dve.bn_stats(stats[:, t, 0:6], batch_slice(h, b, t)[:, 0:P]).then_inc(moments_done.sem, 1)

                        def shifted_half(u):
                            tiles = range(u * TH, (u + 1) * TH)
                            dve.wait_ge(shift_done[u].sem, shift_done[u].at(b, 32))
                            for t in tiles:
                                dve.bn_stats(stats[:, t, 6:12], shifted[:, t, :]).then_inc(moments_done.sem, 1)
                            dve.wait_ge(moments_done.sem, moments_done.at(b, u * LN_STEPS + 2 * TH))
                            dve.memset(pause[:], 0.0)
                            for t in tiles:
                                dve.bn_aggr(moments[:, t, :], stats[:, t, :]).then_inc(moments_done.sem, 1)
                            dve.wait_ge(moments_done.sem, moments_done.at(b, u * LN_STEPS + 3 * TH))
                            mine = slice(u * TH, (u + 1) * TH)
                            dve.tensor_scalar(var_eps[:, mine], moments[:, mine, 1], EPS_LN, None,
                                              ALU.add).then_inc(moments_done.sem, 1)

                        def center(u):
                            dve.wait_ge(xT_ps.sem, xT_ps.at(b, C))
                            dve.wait_ge(rstd_done.sem, rstd_done.at(b, u + 1))
                            for t in range(u * TH, (u + 1) * TH):
                                for c, src in enumerate([batch_slice(h, b, t)[:, 0:P], shifted[:, t, :]]):
                                    dve.tensor_scalar(xn[:, t, c * P:(c + 1) * P], src, moments[:, t, 0:1],
                                                      rstd[:, t:t + 1], ALU.subtract, ALU.mult).then_inc(normed.sem, 1)

                        dve.wait_ge(down_ps.sem, down_ps.at(b, 0))
                        dve.wait_ge(a.out_ps.sem, a.out_ps.at(b, 0))
                        for t in range(T):
                            dve.wait_ge(rotated.sem, rotated.at(b, 2 * (t + 1 - 2)))
                            dve.wait_ge(qkT_ps.sem, qkT_ps.at(b, t + 1 - 2))
                            for k in range(2):
                                dve.wait_ge(squared.sem, squared.at(b, 2 * t + k + 1))
                                ps = bank[2 + 2 * k + t % 2][:]
                                cos = table[:, t, 2 * k * CA_D:(2 * k + 1) * CA_D]
                                sin = table[:, t, (2 * k + 1) * CA_D:(2 * k + 2) * CA_D]
                                cols = slice(k * INNER, (k + 1) * INNER)
                                dve.tensor_tensor(straight[t % 2][:, cols].rearrange("p (h d) -> p h d", d=CA_D),
                                                  ps.rearrange("p (h d) -> p h d", d=CA_D),
                                                  cos.unsqueeze(1).to_broadcast([P, CA_H, CA_D]),
                                                  ALU.mult).then_inc(rotary.sem, 1)
                                for s in range(2):
                                    ins = dve.tensor_tensor(
                                        crossed[t % 2][:, cols].rearrange("p (h s d) -> p h s d", s=2, d=HD2)[:, :, s, :],
                                        ps.rearrange("p (h s d) -> p h s d", s=2, d=HD2)[:, :, 1 - s, :],
                                        sin[:, s * HD2:(s + 1) * HD2].unsqueeze(1).to_broadcast([P, CA_H, HD2]),
                                        ALU.mult)
                                ins.then_inc(rotary.sem, 1)
                                if k == 0 and t >= 1:
                                    scale_q(t - 1)
                            dve.tensor_reduce(norm_sq[:, t, :], squares[t % 2].rearrange("p (h d) -> p h d", d=CA_D),
                                              AX.X, ALU.add).then_inc(norms.sem, 1)
                            dve.wait_ge(norms.sem, norms.at(b, 2 * t + 1))
                            dve.tensor_scalar(norm_sq[:, t, :], norm_sq[:, t, :], 1e-24, None,
                                              ALU.max).then_inc(norms.sem, 1)
                        attend_dve(dve, b, a, h, None, [(SCALE_AT, lambda: scale_q(T - 1)),
                                                        (NORM_AT, lambda: own_half(0)),
                                                        (NORM_AT, lambda: shifted_half(0)),
                                                        (NORM_AT + 2, lambda: center(0))])
                        own_half(1)
                        for u in range(2 * FC):
                            n, cols = u % FC, slice(u // FC * NH, (u // FC + 1) * NH)
                            if u == 1:
                                shifted_half(1)
                            if u == 3:
                                center(1)
                            dve.wait_ge(gated.sem, gated.at(b, u + 1))
                            dve.scalar_tensor_tensor(hidden[0:FW[n], n, cols], bank[2 + u % 2][0:FW[n], 0:NH],
                                                     w["b1"][0:FW[n], layer, 0, n:n + 1],
                                                     act_gate[u % 2][0:FW[n], 0:NH],
                                                     ALU.add, ALU.mult).then_inc(hid.sem, 1)
                            if u in DOWN_AFTER:
                                add_down(b, DOWN_AFTER.index(u))
                        for t in range(TH, T):
                            add_down(b, t)

                @block.scalar
                def _(act):
                    def copy_qk(b, t):
                        act.wait_ge(qkT_ps.sem, qkT_ps.at(b, t + 1))
                        tokens = slice(t * P, (t + 1) * P)
                        qT, kT = (ps_a[k][:].rearrange("p (c n) -> p c n", c=INNER // P) for k in range(2))
                        copy_q(act, a, slice(0, INNER // P), tokens, qT).then_inc(qkT_done.sem, 1)
                        act.activation(a.kT[:, :, tokens], kT, ACT.Copy).then_inc(qkT_done.sem, 1)

                    if layer == 0:
                        for b in range(B):
                            act.activation(kept[b], h[:, b * T:(b + 1) * T, :].rearrange("p t d -> p (t d)"),
                                           ACT.Copy).then_inc(copied, 1)
                    act.wait_ge(a.q_cleared, 2)
                    with act.Fori(0, B) as b:
                        for c in range(C):
                            act.wait_ge(up_ps.sem, up_ps.at(b, 0))
                            act.wait_ge(xT_ps.sem, xT_ps.at(b, c + 1))
                            act.activation(xT[:, c, 1:N + 1], ps_a[c][:], ACT.Copy).then_inc(xT_done.sem, 1)
                        act.wait_ge(down_ps.sem, down_ps.at(b, 0))
                        for t in range(T):
                            act.wait_ge(norms.sem, norms.at(b, 2 * (t + 1 - 2)))
                            for k in range(2):
                                act.wait_ge(qkv_ps.sem, qkv_ps.at(b, 3 * t + k + 1))
                                act.activation(squares[t % 2][:, k * INNER:(k + 1) * INNER], bank[2 + 2 * k + t % 2][:],
                                               ACT.Square).then_inc(squared.sem, 1)
                            act.wait_ge(qkv_ps.sem, qkv_ps.at(b, 3 * t + 3))
                            act.activation(a.v[:, t, :], bank[6 + t % 2][:], ACT.Copy).then_inc(v_done.sem, 1)
                            if t >= 1:
                                copy_qk(b, t - 1)
                        def copy_n(half):
                            act.wait_ge(nT_ps.sem, nT_ps.at(b, half + 1))
                            for c in range(C):
                                act.activation(xT[:, c, 1 + half * NH:1 + (half + 1) * NH],
                                               ps_a[half][:, c * NH:(c + 1) * NH], ACT.Identity,
                                               bias=w["ln_b"][:, layer, c:c + 1],
                                               scale=w["ln_g"][:, layer, c:c + 1]).then_inc(nT_done.sem, 1)

                        attend_act(act, b, a, [(COPY_AT, lambda: copy_qk(b, T - 1))])
                        copy_n(0)
                        for u in range(2 * FC):
                            n = u % FC
                            if u == TURN_N:
                                copy_n(1)
                            act.wait_ge(up_ps.sem, up_ps.at(b, u + 1))
                            act.wait_ge(hid.sem, hid.at(b, u + 1 - 2))
                            act.activation(act_gate[u % 2][0:FW[n], 0:NH], bank[4 + u % 2][0:FW[n], 0:NH], ACT.Gelu,
                                           bias=w["b1"][0:FW[n], layer, 1, n:n + 1]).then_inc(gated.sem, 1)

                @block.tensor
                def _(pe):
                    def turn_qk(b, t):
                        pe.wait_ge(rotated.sem, rotated.at(b, 2 * t + 2))
                        pe.wait_ge(q_scaled.sem, q_scaled.at(b, t + 1))
                        if t == 0:
                            pe.wait_ge(xT_done.sem, xT_done.at(b, C))
                        pe.wait_ge(qkT_done.sem, qkT_done.at(b, 2 * t))
                        for k in range(2):
                            for c in range(INNER // P):
                                at = k * INNER + c * P
                                last = pe.transpose(ps_a[k][:, c * P:(c + 1) * P], straight[t % 2][:, at:at + P], ident[:])
                        last.then_inc(qkT_ps.sem, 1)

                    pe.wait_ge(loaded_late, 16 * n_late)
                    with pe.Fori(0, B) as b:
                        pe.wait_ge(nT_done.sem, nT_done.at(b, 0))
                        turn_staged(pe, b, xn, ident, ps_a, staged, xT_ps)
                        pe.wait_ge(xT_done.sem, xT_done.at(b, C))
                        pe.wait_ge(hid.sem, hid.at(b, 0))
                        pe.wait_ge(h_done.sem, h_done.at(b, 0))
                        for t in range(T):
                            for k in range(3):
                                if k < 2:
                                    pe.wait_ge(rotary.sem, rotary.at(b, 4 * (t + 1 - 2)))
                                    pe.wait_ge(squared.sem, squared.at(b, 2 * (t + 1 - 2)))
                                else:
                                    pe.wait_ge(v_done.sem, v_done.at(b, t + 1 - 2))
                                for c in range(C):
                                    last = pe.matmul(bank[2 + 2 * k + t % 2][:], xT[:, c, 1 - c + t * P:1 - c + (t + 1) * P],
                                                     wqkv[:, c, k * INNER:(k + 1) * INNER], start=(c == 0),
                                                     stop=(c == C - 1))
                                last.then_inc(qkv_ps.sem, 1)
                            if t >= 1:
                                turn_qk(b, t - 1)
                        pe.wait_ge(rotary.sem, rotary.at(b, 4 * T))
                        pe.wait_ge(v_done.sem, v_done.at(b, T))

                        def turn_n(half):
                            for c in range(C):
                                for t in range(half * TH, (half + 1) * TH):
                                    pe.wait_ge(normed.sem, normed.at(b, 2 * t + c + 1))
                                    at = c * NH + (t - half * TH) * P
                                    last = pe.transpose(ps_a[half][:, at:at + P], xn[:, t, c * P:(c + 1) * P], ident[:])
                            last.then_inc(nT_ps.sem, 1)

                        def up(u):
                            half, n = u // FC, u % FC
                            pe.wait_ge(hid.sem, hid.at(b, u + 1 - 2))
                            if n == 0:
                                pe.wait_ge(nT_done.sem, nT_done.at(b, (half + 1) * C))
                            for part in range(2):
                                for c in range(C):
                                    at = part * HID + n * P
                                    last = pe.matmul(bank[2 + 2 * part + u % 2][0:FW[n], 0:NH], w1[:, c, at:at + FW[n]],
                                                     xT[:, c, 1 + half * NH:1 + (half + 1) * NH],
                                                     start=(c == 0), stop=(c == C - 1))
                            last.then_inc(up_ps.sem, 1)

                        def down(t):
                            if t >= 2:
                                pe.wait_ge(h_done.sem, h_done.at(b, t + 1 - 2))
                            pe.matmul(bank[6 + t % 2][:, 0:D], one_row[:], b2_row[:, layer * D:(layer + 1) * D],
                                      start=True, stop=False)
                            for n in range(FC):
                                pe.wait_ge(hid.sem, hid.at(b, t // TH * FC + n + 1))
                                last = pe.matmul(bank[6 + t % 2][:, 0:D], hidden[0:FW[n], n, t * P:(t + 1) * P],
                                                 w2[0:FW[n], n, :], start=False, stop=(n == FC - 1))
                            last.then_inc(down_ps.sem, 1)

                        pe.wait_ge(qkT_done.sem, qkT_done.at(b, 2 * (T - 1)))
                        attend_pe(pe, b, a, [(TURN_AT, lambda: turn_qk(b, T - 1)),
                                             ((T - 1) * CA_H, lambda: pe.wait_ge(qkT_done.sem, qkT_done.at(b, 2 * T))),
                                             (a.UNITS, lambda: turn_n(0))])
                        for u in range(2 * FC):
                            if u == TURN_N:
                                pe.wait_ge(a.h_done.sem, a.h_done.at(b, T))
                                turn_n(1)
                            up(u)
                            if u in DOWN_AFTER:
                                down(DOWN_AFTER.index(u))
                        for t in range(TH, T):
                            down(t)
            for s in every:
                s.passed += B


def turn_staged(pe, b, xn, ident, banks, staged, xT_ps):
    pe.wait_ge(staged.sem, staged.at(b, staged.per))
    for c in range(C):
        for t in range(T):
            last = pe.transpose(banks[c][:, t * P:(t + 1) * P], xn[:, t, c * P:(c + 1) * P], ident[:])
        last.then_inc(xT_ps.sem, 1)


def rotary_tables():
    f = np.float32
    half_idx = np.arange(0, CA_D, 2, dtype=f)
    inv_freq = f(1.0) / f(10000.0) ** (half_idx / f(CA_D))
    t = np.arange(N, dtype=f)
    freqs = t[:, None] * inv_freq[None, :]
    freqs = np.concatenate([freqs, freqs], axis=-1)
    base = (half_idx + f(0.4 * CA_D)) / f(1.4 * CA_D)
    power = (t - f(N // 2)) / f(64.0)
    scale = base[None, :] ** power[:, None]
    scale = np.concatenate([scale, scale], axis=-1)
    sign = np.where(np.arange(CA_D) < CA_D // 2, f(-1.0), f(1.0))
    cos, sin = np.cos(freqs), np.sin(freqs) * sign
    tables = np.stack([f(8.0) * cos * scale, f(8.0) * sin * scale, cos / scale, sin / scale], axis=1)
    return np.ascontiguousarray(tables.astype(f).reshape(T, P, 4 * CA_D).transpose(1, 0, 2))


def kernel(x, L0_tok_emb0, L0_tok_emb1, L0_tok_emb2, L0_tok_emb3, L0_tok_proj0, L0_tok_proj1, L0_tok_proj2,
           L0_tok_proj3, L0_attn_Wq, L0_attn_Wk, L0_attn_Wv, L0_attn_Wo, L0_ffn_moe_router, L0_ffn_moe_w13,
           L0_ffn_moe_w2, L1_attn_wq, L1_attn_wk, L1_attn_wv, L1_attn_wo, L1_attn_w_lr, L1_attn_w_target,
           L1_attn_w_gates, L1_attn_rms_w, L1_ffn_wqkv, L1_ffn_q_scale, L1_ffn_k_scale, L1_ffn_wo, L1_ffn_ln_g,
           L1_ffn_ln_b, L1_ffn_w1, L1_ffn_b1, L1_ffn_w2, L1_ffn_b2, stages=5):
    import concourse.bacc as bacc
    from concourse.bass_utils import run_bass_kernel_spmd

    tables = [np.asarray(t) for t in (L0_tok_emb0, L0_tok_emb1, L0_tok_emb2, L0_tok_emb3)]
    projs = [np.asarray(t) for t in (L0_tok_proj0, L0_tok_proj1, L0_tok_proj2, L0_tok_proj3)]
    emb = np.zeros((CUTOFFS[-1], D), tables[0].dtype)
    for k, t in enumerate(tables):
        emb[CUTOFFS[k]:CUTOFFS[k + 1], 0:EMB_W[k]] = t
    proj = np.zeros((3 * P, D), projs[0].dtype)
    for k, t in enumerate(projs):
        proj[EMB_AT[k]:EMB_AT[k] + EMB_W[k]] = t.T

    def padded(w, twice=False):
        got = np.zeros((D, SB_H, SB_PAD), w.dtype)
        got[:, :, 0:SB_D] = w.T.reshape(D, SB_H, SB_D)
        if twice:
            got[:, :, SB_D:] = got[:, :, 0:SB_D]
        return got.reshape(D, SB_H * SB_PAD)

    def twice_rows(w):
        one = w.T.reshape(SB_H, 1, SB_D, D)
        return np.ascontiguousarray(np.broadcast_to(one, (SB_H, 2, SB_D, D)).reshape(SB_H * SB_PAD, D))

    low = (np.arange(P) % SB_PAD < SB_D).astype(np.float32)
    kinds = np.stack([low, 1 - low], axis=1)

    def heads_last(w):
        return np.ascontiguousarray(np.asarray(w).transpose(1, 0, 2).reshape(D, INNER))

    def columns(w):
        return np.ascontiguousarray(np.asarray(w).reshape(-1, P).T)

    q_s, k_s = np.asarray(L1_ffn_q_scale), np.asarray(L1_ffn_k_scale)
    qk_scale = np.stack([q_s, np.roll(q_s, CA_D // 2, axis=1), k_s, np.roll(k_s, CA_D // 2, axis=1)], axis=1)
    qk_scale = np.ascontiguousarray(np.broadcast_to(qk_scale.reshape(1, DEPTH, 4 * CA_D), (P, DEPTH, 4 * CA_D)))
    b1 = np.zeros((DEPTH, 2, FC * P), q_s.dtype)
    b1[:, :, 0:HID] = np.asarray(L1_ffn_b1).reshape(DEPTH, 2, HID)
    b1 = np.ascontiguousarray(b1.reshape(DEPTH, 2, FC, P).transpose(3, 0, 1, 2))

    arrays = {
        "ids": np.ascontiguousarray(np.asarray(x).reshape(NT, P).T),
        "emb": emb,
        "proj": proj.reshape(3, P, D),
        "sb_wq": padded(np.asarray(L0_attn_Wq)), "sb_wk": padded(np.asarray(L0_attn_Wk)),
        "sb_wv": np.ascontiguousarray(np.asarray(L0_attn_Wv).T),
        "sb_wv2": padded(np.asarray(L0_attn_Wv), twice=True),
        "sb_wo2": twice_rows(np.asarray(L0_attn_Wo)), "kinds": kinds,
        "router": np.asarray(L0_ffn_moe_router), "w13": np.asarray(L0_ffn_moe_w13), "w2": np.asarray(L0_ffn_moe_w2),
        "ca_wq": heads_last(L1_attn_wq), "ca_wk": heads_last(L1_attn_wk), "ca_wv": heads_last(L1_attn_wv),
        "ca_wo": np.asarray(L1_attn_wo).reshape(INNER, D), "w_gates": np.asarray(L1_attn_w_gates),
        "rms_w": columns(L1_attn_rms_w),
        "trig": rotary_tables(),
        "wqkv": np.asarray(L1_ffn_wqkv), "qk_scale": qk_scale,
        "ffn_wo": np.asarray(L1_ffn_wo), "ln_g": columns(L1_ffn_ln_g), "ln_b": columns(L1_ffn_ln_b),
        "w1": np.asarray(L1_ffn_w1), "b1": b1, "w2f": np.asarray(L1_ffn_w2),
        "b2": np.asarray(L1_ffn_b2).reshape(1, DEPTH * D),
    }
    nc = bacc.Bacc("TRN2", target_bir_lowering=False, num_devices=1)
    args = [nc.dram_tensor(k, a.shape, mybir.dt.from_np(a.dtype), kind="ExternalInput").ap() for k, a in arrays.items()]
    out = nc.dram_tensor("out", (B * N, D), F32, kind="ExternalOutput").ap()
    slots = [nc.dram_tensor(name, (MOE_TILES * P, D), F32, kind="Internal").ap() for name in ("moe_in", "moe_out")]
    program(nc, *args, *slots, out, stages=stages)
    r = run_bass_kernel_spmd(nc, [arrays], core_ids=[0])
    return r.results[0]["out"].reshape(B, N, D)
```

```python
import concourse.bass as bass
from concourse import mybir
from contextlib import ExitStack
import numpy as np

F32 = mybir.dt.float32
BF16 = mybir.dt.bfloat16
I32 = mybir.dt.int32
U32 = mybir.dt.uint32
ALU = mybir.AluOpType
ACT = mybir.ActivationFunctionType
AX = mybir.AxisListType

P = 128
B, N, D = 4, 512, 256
T = N // P
NT = B * T
C = D // P
EPS_LN = 1e-5
EPS_RMS = float(np.finfo(np.float32).eps)
MASKED = -1e30

CUTOFFS = [0, 5000, 15000, 25000, 32000]
EMB_W = [256, 64, 16, 4]
EMB_AT = [0, 256, 320, 336]
EMB_K = 340
EMB_CHUNKS = [128, 128, 84]

SB_H, SB_D, SB_PAD = 16, 16, 32
MOE_E, MOE_F = 8, 512
MOE_TILES = (2 * B * N + MOE_E * (P - 1)) // P
MOE_STEP = 4
MOE_TILES = -(-MOE_TILES // MOE_STEP) * MOE_STEP
CA_H, CA_D = 8, 64
INNER = CA_H * CA_D
EARLY_SIZE = 2 * 2 * INNER + INNER // P * N
DEPTH = 2
HID = 682
FC = 6
FW = [128, 128, 128, 128, 128, 42]


class Signal:

    def __init__(self, ctx, nc, name, per):
        self.sem = ctx.enter_context(nc.semaphore(name))
        self.per = per
        self.passed = 0

    def at(self, i, n):
        assert -self.per < n <= self.per, (n, self.per)
        return i * self.per + ((self.passed + 1) * self.per + n)


def batch_slice(tensor, b, t):
    return tensor[:, bass.ds(b * T + t, 1), :].rearrange("p a n -> p (a n)")


def program(nc, ids, emb, proj, sb_wq, sb_wk, sb_wv, sb_wv2, sb_wo2, kinds, router, w13, w2, ca_wq, ca_wk, ca_wv, ca_wo,
            w_gates, rms_w, trig, wqkv, qk_scale, ffn_wo, ln_g, ln_b, w1, b1, w2f, b2, xs, ys, out):
    with ExitStack() as ctx:
        def sb(name, shape, dt=F32):
            return ctx.enter_context(nc.sbuf_tensor(name, shape, dt))

        bank = [ctx.enter_context(nc.psum_tensor(f"bank{i}", [P, 512], F32)) for i in range(8)]

        h = sb("h", [P, NT, D])
        ident = sb("ident", [P, P])
        ident_bf = sb("ident_bf", [P, P], BF16)
        scan_floor = sb("scan_floor", [P, N])
        window_mask = sb("window_mask", [P, 2, P], BF16)
        half = sb("half", [P, 16])
        one_row = sb("one_row", [1, P])
        pause = sb("pause", [P, 1])
        xn = sb("xn", [P, T, D])
        xT = sb("xT", [P, C, N + 1])
        proj_w = sb("proj_w", [P, 3, D])
        sb_w = sb("sb_w", [P, EARLY_SIZE])
        row_kind = sb("row_kind", [P, 2 + P // SB_D])
        ca_all = sb("ca_all", [P, C * 3 * INNER + INNER // P * D])
        ca_w = ca_all[:, 0:C * 3 * INNER].rearrange("p (c n) -> p c n", c=C)
        ca_wo_w = ca_all[:, C * 3 * INNER:].rearrange("p (c n) -> p c n", c=INNER // P)
        gates_w = sb("gates_w", [P, C, CA_H])
        router_w = sb("router_w", [P, C, MOE_E])
        rms_col = sb("rms_col", [P, C])
        b2_row = sb("b2_row", [1, DEPTH * D])
        big = sb("big", [P, MOE_E * (C * 2 * MOE_F + MOE_F // P * D)])

        def sem(name):
            return ctx.enter_context(nc.semaphore(name))

        loaded_sb = sem("loaded_sb")
        loaded_ca = sem("loaded_ca")

        sb_loads = [(view, w.rearrange("(c p) n -> p c n", p=P))
                    for view, w in zip(sb_views(sb_w), [sb_wq, sb_wk, sb_wv2, sb_wo2, sb_wv])] + [(row_kind[:, :], kinds)]
        xn_all = ca_all[:, 0:NT * D].rearrange("p (t n) -> p t n", t=NT)
        sb_norm = Normalizer(ctx, nc, "sb_norm")
        consts_and_embedding(nc, sb, bank, ids, emb, proj, proj_w, h, ident, ident_bf, scan_floor,
                             window_mask, half, one_row, xT, xn_all, sb_norm, sb_loads, loaded_sb)
        stick_breaking(nc, bank, h, pause, half, sb_norm, ident, scan_floor, xn_all, xn, xT, sb_w, big, row_kind,
                       loaded_sb, xs)
        share, slot = sb("moe_share", [P, 2, NT]), sb("moe_slot", [P, 2, NT], I32)
        experts(nc, bank, share, slot, ident, xT, xn_all, router_w, big, xs, ys, router, w13, w2,
                [(ca_w[:, :, 0:512], ca_wq), (ca_w[:, :, 512:1024], ca_wk), (ca_w[:, :, 1024:1536], ca_wv),
                 (ca_wo_w, ca_wo), (gates_w[:, :, :], w_gates), (rms_col[:, :], rms_w)],
                loaded_ca)
        loaded_late = sem("loaded_late")
        late = late_views(big)
        late["early_a"] = sb_w[:, :]
        late["early_b"] = ca_all[:, 0:C * 3 * INNER]
        loads = late_loads(late, b2_row, wqkv, ffn_wo, w1, w2f, trig, qk_scale, ln_g, ln_b, b1, b2)
        at = LATE_SIZE - FC * N
        xn_late = big[:, at:at + NT * D].rearrange("p (t n) -> p t n", t=NT)
        causal(nc, bank, h, half, share, slot, ys, big, ident, ident_bf, window_mask, xn_late, xn, xT, ca_w, ca_wo_w,
               gates_w, rms_col, sb_w, loads, loaded_late, loaded_ca)
        kept = [late["early_b"][:, (b + 1) * T * D:(b + 2) * T * D] for b in range(2)]
        kept += [big[:, LATE_SIZE + b * T * D:LATE_SIZE + (b + 1) * T * D] for b in range(2)]
        local_layers(nc, bank, h, pause, ident, ident_bf, window_mask, half, one_row, xn, xT, late, b2_row, kept,
                     loaded_late, len(loads))
        store(nc, h, kept, out)


def store(nc, h, kept, out):
    with ExitStack() as ctx:
        stored = ctx.enter_context(nc.semaphore("stored"))
        summed = ctx.enter_context(nc.semaphore("final_summed"))
        with nc.Block() as block:
            @block.vector
            def _(dve):
                for b in range(B if kept else 0):
                    hb = h[:, b * T:(b + 1) * T, :].rearrange("p t d -> p (t d)")
                    dve.tensor_tensor(hb, hb, kept[b], ALU.add).then_inc(summed, 1)

            @block.sync
            def _(sp):
                for b in range(B):
                    if kept:
                        sp.wait_ge(summed, b + 1)
                    sp.dma_start(out[b * N:(b + 1) * N, :].rearrange("(t p) d -> p t d", p=P),
                                 h[:, b * T:(b + 1) * T, :]).then_inc(stored, 16)
                sp.wait_ge(stored, 16 * B)


class Normalizer:

    def __init__(self, ctx, nc, name, rms=False):
        def st(what, shape):
            return ctx.enter_context(nc.sbuf_tensor(f"{name}_{what}", shape, F32))

        self.factor, self.offset = (1.0 + EPS_RMS, EPS_LN * EPS_RMS) if rms else (1.0, EPS_LN)
        self.stats, self.moments = st("stats", [P, NT, 6]), st("moments", [P, NT, 2])
        self.square, self.scale = st("square", [P, NT]), st("scale", [P, NT])
        self.steps = ctx.enter_context(nc.semaphore(f"{name}_steps"))
        self.scale_done = ctx.enter_context(nc.semaphore(f"{name}_scale"))
        self.normed = ctx.enter_context(nc.semaphore(f"{name}_normed"))

    def on_dve(self, dve, b, h, out):
        tiles, steps = range(b * T, (b + 1) * T), b * (2 * T + 1)
        mine = slice(b * T, (b + 1) * T)
        for t in tiles:
            dve.bn_stats(self.stats[:, t, :], h[:, t, :]).then_inc(self.steps, 1)
        dve.wait_ge(self.steps, steps + T)
        for t in tiles:
            dve.bn_aggr(self.moments[:, t, :], self.stats[:, t, :]).then_inc(self.steps, 1)
        dve.wait_ge(self.steps, steps + 2 * T)
        dve.tensor_scalar(self.square[:, mine], self.moments[:, mine, 1], self.factor, self.offset, ALU.mult,
                          ALU.add).then_inc(self.steps, 1)
        dve.wait_ge(self.scale_done, b + 1)
        for t in tiles:
            dve.tensor_scalar(out[:, t, :], h[:, t, :], self.moments[:, t, 0:1], self.scale[:, t:t + 1],
                              ALU.subtract, ALU.mult).then_inc(self.normed, 1)

    def on_pool(self, pool, half, batches=range(B)):
        for b in batches:
            mine = slice(b * T, (b + 1) * T)
            pool.wait_ge(self.steps, (b + 1) * (2 * T + 1))
            pool.tensor_tensor(self.scale[:, mine], self.square[:, mine], half[:, mine],
                               ALU.pow).then_inc(self.scale_done, 1)


def consts_and_embedding(nc, sb, bank, ids, emb, proj, proj_w, h, ident, ident_bf, scan_floor,
                         window_mask, half, one_row, xT, xn_all, norm, weights, loaded_sb):
    with ExitStack() as ctx:
        def st(name, shape, dt=F32):
            return ctx.enter_context(nc.sbuf_tensor(name, shape, dt))

        def sem(name):
            return ctx.enter_context(nc.semaphore(name))

        ids_sb = st("ids_sb", [P, NT], I32)
        ids_f = st("ids_f", [P, NT])
        row = st("row", [P, NT])
        row_i = st("row_i", [P, NT], U32)
        at_least = st("at_least", [P, 5, NT])
        in_table = st("in_table", [P, 4, NT])
        gathered = st("gathered", [P, NT, D])
        feat = [st(f"feat{k}", [P, EMB_K]) for k in range(2)]
        featT = [st(f"featT{k}", [P, 3, P]) for k in range(2)]

        ids_in, proj_in = sem("ids_in"), sem("proj_in")
        rows_in = [sem(f"rows_in{t}") for t in range(NT)]
        made = sem("made")
        index = sem("index")
        masked = sem("masked")
        turned = sem("turned")
        turned_sb = sem("turned_sb")
        summed = sem("summed")
        kept = sem("kept")
        NORM_AFTER = T - 1

        with nc.Block() as block:
            @block.sync
            def _(sp):
                sp.dma_start(ids_sb[:, :], ids).then_inc(ids_in, 16)
                sp.dma_start(proj_w[:, :, :], proj.rearrange("c p n -> p c n")).then_inc(proj_in, 16)
                for dst, src in weights:
                    sp.dma_start(dst, src).then_inc(loaded_sb, 16)

            @block.gpsimd
            def _(pool):
                pool.wait_ge(index, 12)
                for t in range(NT):
                    pool.indirect_dma_start(
                        gathered[:, t, :], None, emb,
                        bass.IndirectOffsetOnAxis(ap=row_i[:, t:t + 1], axis=0)).then_inc(rows_in[t], 16)
                pool.memset(ident_bf[:], 0.0).then_inc(made, 1)
                pool.memset(scan_floor[:], 0.0).then_inc(made, 1)
                pool.memset(window_mask[:], 0.0).then_inc(made, 1)
                pool.memset(half[:], -0.5).then_inc(made, 1)
                pool.memset(one_row[:], 1.0).then_inc(made, 1)
                pool.memset(xT[:, :, 0:1], 0.0).then_inc(made, 1)
                pool.wait_ge(made, 6)
                pool.affine_select(out=ident_bf[:], in_=ident_bf[:], compare_op=ALU.not_equal, fill=1.0,
                                   base=0, pattern=[[-1, P]], channel_multiplier=1).then_inc(made, 1)
                own_key = scan_floor[:, N - P:N]
                pool.affine_select(out=own_key, in_=own_key, compare_op=ALU.not_equal, fill=1.0,
                                   base=0, pattern=[[-1, P]], channel_multiplier=1).then_inc(made, 1)
                before, own = window_mask[:, 0, :], window_mask[:, 1, :]
                pool.affine_select(out=before, in_=before, compare_op=ALU.is_ge, fill=MASKED,
                                   base=0, pattern=[[1, P]], channel_multiplier=-1).then_inc(made, 1)
                pool.affine_select(out=own, in_=own, compare_op=ALU.is_ge, fill=MASKED,
                                   base=0, pattern=[[-1, P]], channel_multiplier=1).then_inc(made, 1)
                pool.wait_ge(made, 10)
                norm.on_pool(pool, half, range(B - 1))

            @block.vector
            def _(dve):
                dve.memset(ident[:], 0.0).then_inc(index, 1)
                dve.wait_ge(ids_in, 16)
                dve.tensor_copy(ids_f[:], ids_sb[:]).then_inc(index, 1)
                dve.wait_ge(index, 2)
                dve.tensor_scalar(row[:], ids_f[:], 0.0, float(CUTOFFS[-1] - 1), ALU.max, ALU.min).then_inc(index, 1)
                for k in range(5):
                    dve.tensor_scalar(at_least[:, k, :], ids_f[:], float(CUTOFFS[k]), None,
                                      ALU.is_ge).then_inc(index, 1)
                dve.wait_ge(index, 8)
                for k in range(3):
                    dve.tensor_sub(in_table[:, k, :], at_least[:, k, :], at_least[:, k + 1, :]).then_inc(index, 1)
                dve.tensor_copy(row_i[:], row[:]).then_inc(index, 1)
                dve.tensor_sub(in_table[:, 3, :], at_least[:, 3, :], at_least[:, 4, :]).then_inc(index, 1)
                dve.wait_ge(index, 13)
                for t in range(NT):
                    dve.wait_ge(rows_in[t], 16)
                    if t >= 2:
                        dve.wait_ge(turned, t - 1)
                    for k in range(4):
                        last = dve.tensor_scalar(feat[t % 2][:, EMB_AT[k]:EMB_AT[k] + EMB_W[k]],
                                                 gathered[:, t, 0:EMB_W[k]], in_table[:, k, t:t + 1], None,
                                                 ALU.mult)
                    last.then_inc(masked, 1)
                    if t % T == NORM_AFTER and t > T:
                        dve.wait_ge(kept, t // T * T)
                        norm.on_dve(dve, t // T - 1, h, xn_all)

            @block.scalar
            def _(act):
                act.wait_ge(made, 10)
                act.wait_ge(index, 1)
                act.activation(ident[:], ident_bf[:], ACT.Copy).then_inc(made, 1)

                def keep(t):
                    act.wait_ge(summed, t + 1)
                    act.activation(h[:, t, :], bank[2 + t % 2][:, 0:D], ACT.Copy, scale=float(D) ** 0.5).then_inc(kept, 1)

                for t in range(NT):
                    act.wait_ge(turned, t + 1)
                    if t >= 2:
                        act.wait_ge(summed, t - 1)
                    act.activation(featT[t % 2][:, 0:2, :].rearrange("p c n -> p (c n)"),
                                   bank[t % 2][:, 0:2 * P], ACT.Copy)
                    act.activation(featT[t % 2][0:EMB_CHUNKS[2], 2, :],
                                   bank[t % 2][0:EMB_CHUNKS[2], 2 * P:3 * P], ACT.Copy).then_inc(turned_sb, 1)
                    if t >= 1:
                        keep(t - 1)
                keep(NT - 1)

            @block.tensor
            def _(pe):
                pe.wait_ge(made, 11)
                pe.wait_ge(proj_in, 16)

                def project(t):
                    pe.wait_ge(turned_sb, t + 1)
                    if t >= 2:
                        pe.wait_ge(kept, t - 1)
                    for c, w in enumerate(EMB_CHUNKS):
                        last = pe.matmul(bank[2 + t % 2][:, 0:D], featT[t % 2][0:w, c, :], proj_w[0:w, c, :],
                                         start=(c == 0), stop=(c == 2))
                    last.then_inc(summed, 1)

                for t in range(NT):
                    pe.wait_ge(masked, t + 1)
                    if t >= 2:
                        pe.wait_ge(turned_sb, t - 1)
                    for c, w in enumerate(EMB_CHUNKS):
                        last = pe.transpose(bank[t % 2][0:w, c * P:(c + 1) * P],
                                            feat[t % 2][:, c * P:c * P + w], ident[:])
                    last.then_inc(turned, 1)
                    if t >= 1:
                        project(t - 1)
                project(NT - 1)


def sb_views(sb_w):
    views, at = [], 0
    for chunks, width in [(C, D), (C, D), (C, SB_H * SB_PAD), (SB_H * SB_PAD // P, D), (C, D)]:
        views.append(sb_w[:, at:at + chunks * width].rearrange("p (c n) -> p c n", c=chunks))
        at += chunks * width
    return views


def stage_batches(sp, first, xn, xn_all, normed, staged, xT_ps):
    if first:
        sp.wait_ge(normed, T)
        sp.dma_start(xn[:, :, :], xn_all[:, 0:T, :]).then_inc(staged.sem, 16)
    else:
        with sp.Fori(1, B) as b:
            sp.wait_ge(normed, b * T + T)
            sp.wait_ge(xT_ps.sem, xT_ps.at(b, 0))
            sp.dma_start(xn[:, :, :], xn_all[:, bass.ds(b * T, T), :]).then_inc(staged.sem, 16)
        end_staging(sp, staged)


def end_staging(sp, staged):
    sp.wait_ge(staged.sem, staged.at(B - 1, 16))
    sp.sem_inc(staged.sem, 16)


def stick_breaking(nc, bank, h, pause, half, norm, ident, scan_floor, xn_all, xn, xT, sb_w, big, row_kind,
                   loaded_sb, xs):
    UNITS = T * SB_H
    G = SB_H * SB_PAD // P
    QG = D // P
    PER = P // SB_D
    PROJ = 2 * QG + G + T
    wq, wk, wv2, wo2, wv = sb_views(sb_w)
    with ExitStack() as ctx:
        taken = [0]

        def st(name, shape):
            size = int(np.prod(shape[1:]))
            flat = big[:, taken[0]:taken[0] + size]
            taken[0] += size
            names = "abc"[:len(shape) - 1]
            return flat.rearrange(f"p ({' '.join(names)}) -> p {' '.join(names)}",
                                  **{x: n for x, n in zip(names[:-1], shape[1:-1])}) if len(names) > 1 else flat

        def signal(name, per):
            return Signal(ctx, nc, name, per)

        qT, kT = st("qT", [P, QG, N]), st("kT", [P, QG, N])
        alone = [st(f"alone{i}", [P, QG, PER * P]) for i in range(2)]
        dxT = st("dxT", [P, C, N])
        u = st("u", [P, T, SB_H * SB_PAD])
        v_add, v_mul = st("v_add", [P, G, N]), st("v_mul", [P, G, N])
        keep = [st(f"keep{i}", [P, N]) for i in range(2)]
        prod = [st(f"prod{i}", [P, N]) for i in range(3)]
        prodT = [st(f"prodT{i}", [P, N]) for i in range(2)]
        summed = st("summed", [P, G * P])
        oT = [st(f"oT{i}", [P, G * P]) for i in range(2)]

        ps_a, ps_l, ps_t, ps_o = bank[0:2], bank[2:4], bank[4:6], bank[6:8]
        ps_out = [ps_a[i % 2] for i in range(T - 1)] + [ps_l[0]]

        stats, moments = st("stats", [P, T, 6]), st("moments", [P, T, 2])
        var_eps, rstd = st("var_eps", [P, T]), st("rstd", [P, T])
        moments_done = signal("sb_moments", 2 * T + 1)
        rstd_done = signal("sb_rstd", 1)
        u_cleared = ctx.enter_context(nc.semaphore("sb_u_cleared"))
        zero_made = ctx.enter_context(nc.semaphore("sb_zero_made"))
        xs_cleared = ctx.enter_context(nc.semaphore("sb_xs_cleared"))
        zero = st("zero", [P, D])
        staged = signal("sb_staged", 16)
        xT_ps = signal("sb_xT_ps", C)
        xT_done = signal("sb_xT", C)
        dx_done = signal("sb_dx", 1)
        proj_ps = signal("sb_proj_ps", PROJ)
        proj_done = signal("sb_proj", PROJ)
        alone_done = signal("sb_alone", QG * T)
        logits = signal("sb_logits", UNITS)
        kept = signal("sb_keep", UNITS)
        prods = signal("sb_prods", UNITS)
        prods_t = signal("sb_prods_t", UNITS)
        prods_tc = signal("sb_prods_tc", UNITS)
        pv = signal("sb_pv", UNITS)
        sum_done = signal("sb_sum", T)
        oT_done = signal("sb_oT", T)
        out_ps = signal("sb_out_ps", T)
        h_done = signal("sb_h", T)
        every = [moments_done, rstd_done, staged, xT_ps, xT_done, dx_done, proj_ps, proj_done, alone_done,
                 logits, kept, prods, prods_t, prods_tc, pv, sum_done, oT_done, out_ps, h_done]

        FINISH, PROJECT, ADD = 5, 7, 8

        with nc.Block() as block:
            @block.sync
            def _(sp):
                for s in every:
                    sp.sem_inc(s.sem, s.per)
                stage_batches(sp, True, xn, xn_all, norm.normed, staged, xT_ps)
                stage_batches(sp, False, xn, xn_all, norm.normed, staged, xT_ps)
                sp.wait_ge(zero_made, 1)
                sp.dma_start(xs.rearrange("(j p) n -> p j n", p=P),
                             zero.unsqueeze(1).to_broadcast([P, MOE_TILES, D])).then_inc(xs_cleared, 16)
                sp.wait_ge(xs_cleared, 16)

            @block.gpsimd
            def _(pool):
                norm.on_pool(pool, half, [B - 1])
                pool.memset(u, 0.0).then_inc(u_cleared, 1)
                pool.wait_ge(u_cleared, 1)
                ones = u[0:1, 0, :].rearrange("p (h e) -> p h e", e=SB_PAD)[:, :, SB_D:]
                pool.memset(ones, 1.0).then_inc(u_cleared, 1)
                pool.wait_ge(loaded_sb, 16 * 6)
                pool.wait_ge(u_cleared, 2)
                with pool.Fori(0, B) as b:
                    for i in range(T):
                        if i == 0:
                            pool.wait_ge(proj_done.sem, proj_done.at(b, QG))
                        pool.wait_ge(logits.sem, logits.at(b, (i + 1 - 2) * SB_H))
                        for g in range(QG):
                            pool.tensor_tensor(alone[i % 2][:, g, :].rearrange("p (r n) -> p r n", r=PER),
                                               qT[:, g, i * P:(i + 1) * P].unsqueeze(1).to_broadcast([P, PER, P]),
                                               row_kind[:, 2:2 + PER].unsqueeze(2).to_broadcast([P, PER, P]),
                                               ALU.mult).then_inc(alone_done.sem, 1)
                    pool.wait_ge(moments_done.sem, moments_done.at(b, 2 * T + 1))
                    pool.tensor_tensor(rstd, var_eps, half[:, 0:T], ALU.pow).then_inc(rstd_done.sem, 1)

            @block.vector
            def _(dve):
                def finish(b, i):
                    dve.wait_ge(pv.sem, pv.at(b, (i + 1) * SB_H))
                    dve.wait_ge(oT_done.sem, oT_done.at(b, i))
                    if i == 0:
                        dve.wait_ge(proj_done.sem, proj_done.at(b, 2 * QG + G))
                    blk = slice(i * P, (i + 1) * P)
                    dve.tensor_tensor(summed.rearrange("p (c n) -> p c n", c=G),
                                      ps_o[i % 2][:].rearrange("p (c n) -> p c n", c=G), v_add[:, :, blk],
                                      ALU.add).then_inc(sum_done.sem, 1)
                    dve.wait_ge(out_ps.sem, out_ps.at(b, i + 1 - 2))
                    dve.wait_ge(sum_done.sem, sum_done.at(b, i + 1))
                    dve.tensor_tensor(oT[i % 2].rearrange("p (c n) -> p c n", c=G),
                                      summed.rearrange("p (c n) -> p c n", c=G), v_mul[:, :, blk],
                                      ALU.mult).then_inc(oT_done.sem, 1)

                def add(b, i):
                    dve.wait_ge(out_ps.sem, out_ps.at(b, i + 1))
                    hs = batch_slice(h, b, i)
                    dve.tensor_tensor(hs, ps_out[i][:, 0:D], hs, ALU.add).then_inc(h_done.sem, 1)

                norm.on_dve(dve, B - 1, h, xn_all)
                dve.memset(zero, 0.0).then_inc(zero_made, 1)
                with dve.Fori(0, B) as b:
                    dve.wait_ge(proj_ps.sem, proj_ps.at(b, 0))
                    dve.wait_ge(xT_done.sem, xT_done.at(b, C))
                    dve.tensor_tensor(dxT, xT[:, :, 0:N], xT[:, :, 1:N + 1], ALU.subtract).then_inc(dx_done.sem, 1)
                    for n in range(UNITS):
                        i, hd = n // SB_H, n % SB_H
                        w = (i + 1) * P
                        dve.wait_ge(kept.sem, kept.at(b, n + 1))
                        dve.wait_ge(prods_t.sem, prods_t.at(b, n + 1 - 3))
                        dve.tensor_tensor_scan(prod[n % 3][:, 0:w][:, ::-1], keep[n % 2][:, 0:w][:, ::-1],
                                               scan_floor[:, N - w:N][:, ::-1], 0.0, ALU.mult,
                                               ALU.max).then_inc(prods.sem, 1)
                        if i >= 1 and hd == FINISH:
                            finish(b, i - 1)
                        if i >= 1 and hd == ADD:
                            add(b, i - 1)
                    finish(b, T - 1)
                    add(b, T - 1)
                    dve.wait_ge(h_done.sem, h_done.at(b, T))
                    dve.memset(pause[:], 0.0)
                    for t in range(T):
                        dve.bn_stats(stats[:, t, :], batch_slice(h, b, t)).then_inc(moments_done.sem, 1)
                    dve.wait_ge(moments_done.sem, moments_done.at(b, T))
                    dve.memset(pause[:], 0.0)
                    for t in range(T):
                        dve.bn_aggr(moments[:, t, :], stats[:, t, :]).then_inc(moments_done.sem, 1)
                    dve.wait_ge(moments_done.sem, moments_done.at(b, 2 * T))
                    dve.tensor_scalar(var_eps, moments[:, :, 1], EPS_LN, None, ALU.add).then_inc(moments_done.sem, 1)
                    dve.wait_ge(rstd_done.sem, rstd_done.at(b, 1))
                    dve.wait_ge(staged.sem, staged.at(b, 16))
                    for t in range(T):
                        dve.tensor_scalar(batch_slice(xn_all, b, t), batch_slice(h, b, t), moments[:, t, 0:1],
                                          rstd[:, t:t + 1], ALU.subtract, ALU.mult)

            @block.scalar
            def _(act):
                def copy_t(b, n):
                    w = (n // SB_H + 1) * P
                    act.wait_ge(prods_t.sem, prods_t.at(b, n + 1))
                    act.wait_ge(pv.sem, pv.at(b, n + 1 - 2))
                    act.activation(prodT[n % 2][:, 0:w], ps_t[n % 2][:, 0:w], ACT.Copy).then_inc(prods_tc.sem, 1)

                act.wait_ge(u_cleared, 2)
                act.wait_ge(loaded_sb, 16 * 6)
                act.preload_act_table(ACT.Sigmoid)

                def copy_x(b):
                    for c in range(C):
                        act.wait_ge(xT_ps.sem, xT_ps.at(b, c + 1))
                        if c == 0:
                            act.wait_ge(proj_ps.sem, proj_ps.at(b, 0))
                            act.wait_ge(dx_done.sem, dx_done.at(b, 0))
                        act.activation(xT[:, c, 1:N + 1], ps_a[c][:], ACT.Copy).then_inc(xT_done.sem, 1)

                copy_x(0)
                with act.Fori(0, B) as b:
                    for k in range(PROJ):
                        act.wait_ge(proj_ps.sem, proj_ps.at(b, k + 1))
                        src = ps_a[k % 2][:]
                        g = (k - 2 * QG) % G
                        if k == 0:
                            act.wait_ge(logits.sem, logits.at(b, 0))
                            act.wait_ge(alone_done.sem, alone_done.at(b, 0))
                            act.wait_ge(oT_done.sem, oT_done.at(b, 0))
                            act.wait_ge(pv.sem, pv.at(b, 0))
                        if k < 2 * QG:
                            ins = act.activation((qT if k < QG else kT)[:, k % QG, :], src, ACT.Copy)
                        elif k < 2 * QG + G:
                            act.activation(v_add[:, g, :], src, ACT.Copy, scale=row_kind[:, 0:1])
                            ins = act.activation(v_mul[:, g, :], src, ACT.Identity, bias=row_kind[:, 0:1],
                                                 scale=row_kind[:, 1:2])
                        else:
                            ins = act.activation(
                                u[:, k - 2 * QG - G, :].rearrange("p (h e) -> p h e", e=SB_PAD)[:, :, 0:SB_D],
                                ps_a[k % 2][:, 0:D].rearrange("p (h e) -> p h e", e=SB_D), ACT.Copy)
                        ins.then_inc(proj_done.sem, 1)
                    for n in range(UNITS + 2):
                        if n < UNITS:
                            w = (n // SB_H + 1) * P
                            act.wait_ge(logits.sem, logits.at(b, n + 1))
                            act.wait_ge(prods.sem, prods.at(b, n + 1 - 2))
                            act.activation(keep[n % 2][:, 0:w], ps_l[n % 2][:, 0:w], ACT.Sigmoid,
                                           scale=-float(SB_D) ** -0.5).then_inc(kept.sem, 1)
                        if n >= 2:
                            copy_t(b, n - 2)
                    copy_x(b + 1)

            @block.tensor
            def _(pe):
                def transposes(b, n):
                    i = n // SB_H
                    pe.wait_ge(prods.sem, prods.at(b, n + 1))
                    pe.wait_ge(prods_tc.sem, prods_tc.at(b, n + 1 - 2))
                    for c in range(i + 1):
                        last = pe.transpose(ps_t[n % 2][:, c * P:(c + 1) * P], prod[n % 3][:, c * P:(c + 1) * P],
                                            ident[:])
                    last.then_inc(prods_t.sem, 1)

                def weigh(b, n):
                    i, hd = n // SB_H, n % SB_H
                    row, g = hd * SB_PAD % P, hd * SB_PAD // P
                    if hd == 0:
                        pe.wait_ge(sum_done.sem, sum_done.at(b, i + 1 - 2))
                    pe.wait_ge(prods_tc.sem, prods_tc.at(b, n + 1))
                    for c in range(i + 1):
                        last = pe.matmul(ps_o[i % 2][row:row + SB_PAD, g * P:(g + 1) * P],
                                         u[:, c, hd * SB_PAD:(hd + 1) * SB_PAD], prodT[n % 2][:, c * P:(c + 1) * P],
                                         start=(c == 0), stop=(c == i))
                    last.then_inc(pv.sem, 1)

                def project_o(b, i):
                    pe.wait_ge(oT_done.sem, oT_done.at(b, i + 1))
                    pe.wait_ge(h_done.sem, h_done.at(b, i + 1 - 2))
                    for g in range(G):
                        last = pe.matmul(ps_out[i][:, 0:D], oT[i % 2][:, g * P:(g + 1) * P], wo2[:, g, :],
                                         start=(g == 0), stop=(g == G - 1))
                    last.then_inc(out_ps.sem, 1)

                turn_staged(pe, 0, xn, ident, ps_a, staged, xT_ps)
                with pe.Fori(0, B) as b:
                    for k in range(PROJ):
                        if k == 0:
                            pe.wait_ge(xT_done.sem, xT_done.at(b, C))
                            pe.wait_ge(loaded_sb, 16 * 6)
                        if k == 2 * QG + G:
                            pe.wait_ge(dx_done.sem, dx_done.at(b, 1))
                        if k >= 2:
                            pe.wait_ge(proj_done.sem, proj_done.at(b, k - 1))
                        for c in range(C):
                            g = (k - 2 * QG) % G if k >= 2 * QG else k % QG
                            if k < 2 * QG + G:
                                w = wv2 if k >= 2 * QG else (wq, wk)[k // QG]
                                last = pe.matmul(ps_a[k % 2][:], w[:, c, g * P:(g + 1) * P],
                                                 xT[:, c, 1:N + 1], start=(c == 0), stop=(c == C - 1))
                            else:
                                t = k - 2 * QG - G
                                last = pe.matmul(ps_a[k % 2][:, 0:D], dxT[:, c, t * P:(t + 1) * P], wv[:, c, :],
                                                 start=(c == 0), stop=(c == C - 1))
                        last.then_inc(proj_ps.sem, 1)
                    pe.wait_ge(h_done.sem, h_done.at(b, 0))
                    for n in range(UNITS + 4):
                        if n < UNITS:
                            i, hd = n // SB_H, n % SB_H
                            if hd == 0:
                                pe.wait_ge(proj_done.sem, proj_done.at(b, 2 * QG))
                            if hd % PER == 0:
                                pe.wait_ge(alone_done.sem, alone_done.at(b, i * QG + hd // PER + 1))
                            pe.wait_ge(kept.sem, kept.at(b, n + 1 - 2))
                            at = hd % PER * P
                            pe.matmul(ps_l[n % 2][:, 0:(i + 1) * P], alone[i % 2][:, hd // PER, at:at + P],
                                      kT[:, hd // PER, 0:(i + 1) * P], start=True, stop=True).then_inc(logits.sem, 1)
                        if 2 <= n < UNITS + 2:
                            transposes(b, n - 2)
                        if n == 4:
                            pe.wait_ge(proj_done.sem, proj_done.at(b, PROJ))
                        if n >= 4:
                            weigh(b, n - 4)
                        if n >= SB_H and n % SB_H == PROJECT and n < UNITS:
                            project_o(b, n // SB_H - 1)
                    pe.wait_ge(h_done.sem, h_done.at(b, T - 1))
                    turn_staged(pe, b + 1, xn, ident, ps_a, staged, xT_ps)
                    project_o(b, T - 1)


def experts(nc, bank, share, slot, ident, xT, xn_all, router_w, big, xs, ys, router, w13, w2, next_loads, loaded_ca):
    K = MOE_STEP
    STEPS = MOE_TILES // K
    W13 = big[:, 0:MOE_E * C * 2 * MOE_F].rearrange("p (e c f) -> p e c f", e=MOE_E, c=C)
    W2 = big[:, MOE_E * C * 2 * MOE_F:].rearrange("p (e c f) -> p e c f", e=MOE_E, c=MOE_F // P)
    FCH = MOE_F // P
    LEVELS = NT
    xs_tiles = xs.rearrange("(j p) n -> p j n", p=P)
    ys_tiles = ys.rearrange("(j p) n -> p j n", p=P)
    with ExitStack() as ctx:
        def st(name, shape, dt=F32):
            return ctx.enter_context(nc.sbuf_tensor(f"moe_{name}", shape, dt))

        def signal(name, per):
            return Signal(ctx, nc, f"moe_{name}", per)

        def sem(name):
            return ctx.enter_context(nc.semaphore(f"moe_{name}"))

        numbers_i = st("numbers_i", [P, MOE_TILES], I32)
        numbers = st("numbers", [P, MOE_TILES])
        levels = st("levels", [P, LEVELS])
        ones = st("ones", [P, P])
        below = st("below", [P, P])
        going_on = st("going_on", [P, MOE_E, NT])
        best = st("best", [P, NT, MOE_E])
        best_at = st("best_at", [P, NT, MOE_E], U32)
        best_f = st("best_f", [P, NT, MOE_E])
        gap = st("gap", [P, NT])
        chosen = [st(f"chosen{k}", [P, MOE_E, NT]) for k in range(2)]
        either = st("either", [P, MOE_E, NT])
        total = st("total", [P, MOE_E, NT])
        upto = st("upto", [P, MOE_E, NT])
        level_on = st("level_on", [P, MOE_E, LEVELS])
        filled = st("filled", [P, MOE_E])
        end = st("end", [P, MOE_E])
        first = st("first", [P, MOE_E])
        slot_e = st("slot_e", [P, MOE_E, NT])
        slot_f = st("slot_f", [P, 2, NT])
        passed = st("passed", [1, MOE_TILES, MOE_E])
        tile_f = st("tile_f", [1, MOE_TILES])
        tile_e = st("tile_e", [1, MOE_TILES], I32)
        x_in = st("x_in", [P, K, D])
        x_inT = [st(f"x_inT{u}", [P, C * P]) for u in range(2)]
        act_gate = [st(f"act_gate{u}", [P, MOE_F]) for u in range(2)]
        hidden = [st(f"hidden{u}", [P, MOE_F]) for u in range(2)]
        hiddenT = [st(f"hiddenT{u}", [P, MOE_F]) for u in range(2)]
        y_out = st("y_out", [P, K, D])

        loaded_router, loaded_w = sem("loaded_router"), sem("loaded_w")
        xT_ps = sem("xT_ps")
        xT_done = sem("xT")
        routed = sem("routed")
        consts = sem("consts")
        route = sem("route")
        shares = sem("shares")
        counted = sem("counted")
        scattered = sem("scattered")
        x_loaded = signal("x_loaded", 16)
        x_ps = signal("x_ps", K)
        x_done = signal("x", K)
        gate_ps = signal("gate_ps", K)
        up_ps = signal("up_ps", K)
        gated = signal("gated", K)
        hid = signal("hid", K)
        hidT_ps = signal("hidT_ps", K)
        hidT_done = signal("hidT", K)
        down_ps = signal("down_ps", K)
        y_done = signal("y", K)
        stored = sem("stored")
        every = [x_loaded, x_ps, x_done, gate_ps, up_ps, gated, hid, hidT_ps, hidT_done, down_ps, y_done]

        ps_y, ps_gate, ps_up, ps_hT, ps_xT = bank[0:2], bank[2:4], bank[4:6], bank[6], bank[7]

        R_BEST = NT
        R_GAP = R_BEST + 1
        R_INDEX = R_GAP + NT
        R_FLOAT = R_INDEX + 2
        R_CHOSEN = R_FLOAT + 2
        R_EITHER = R_CHOSEN + 1
        R_TOTAL = R_EITHER + 1
        R_UPTO = R_TOTAL + 1
        R_LEVELS = R_UPTO + 1
        R_FILLED = R_LEVELS + 1
        R_END = R_FILLED + 1
        R_FIRST = R_END + 2
        R_RANK = R_FIRST + 1
        R_SLOT_E = R_RANK + 1
        R_PICKED = R_SLOT_E + 2
        R_SLOT_F = R_PICKED + 2
        R_SLOT = R_SLOT_F + 1
        R_PASSED = R_SLOT + 1
        R_TILE_F = R_PASSED + 1
        R_CAPPED = R_TILE_F + 1
        R_TILE_E = R_CAPPED + 1

        with nc.Block() as block:
            @block.sync
            def _(sp):
                for s in every:
                    sp.sem_inc(s.sem, s.per)
                sp.dma_start(router_w[:, :, :], router.rearrange("(c p) n -> p c n", p=P)).then_inc(loaded_router, 16)
                for e in range(MOE_E):
                    sp.dma_start(W13[:, e], w13[e].rearrange("(c p) n -> p c n", p=P)).then_inc(loaded_w, 16)
                    sp.dma_start(W2[:, e], w2[e].rearrange("(c p) n -> p c n", p=P)).then_inc(loaded_w, 16)
                sp.wait_ge(scattered, 16 * 2 * NT)
                with sp.Fori(0, STEPS) as j:
                    sp.wait_ge(x_ps.sem, x_ps.at(j, 0))
                    sp.dma_start(x_in[:, :, :], xs_tiles[:, bass.ds(K * j, K), :]).then_inc(x_loaded.sem, 16)
                for dst, src in next_loads:
                    sp.dma_start(dst, src if len(src.shape) == 2 and src.shape[0] == P
                                 else src.rearrange("(c p) n -> p c n", p=P)).then_inc(loaded_ca, 16)

            @block.gpsimd
            def _(pool):
                pool.iota(numbers_i[:], pattern=[[1, MOE_TILES]], base=0, channel_multiplier=0).then_inc(consts, 1)
                pool.memset(ones[:], 1.0).then_inc(consts, 1)
                pool.memset(below[:], 1.0).then_inc(consts, 1)
                pool.memset(going_on[:, :, :], 1.0).then_inc(consts, 1)
                pool.wait_ge(consts, 4)
                pool.tensor_copy(numbers[:], numbers_i[:]).then_inc(consts, 1)
                pool.affine_select(out=below[:], in_=below[:], compare_op=ALU.is_ge, fill=0.0, base=-1,
                                   pattern=[[1, P]], channel_multiplier=-1).then_inc(consts, 1)
                pool.memset(going_on[:, :, 0:1], 0.0).then_inc(consts, 1)
                pool.wait_ge(route, R_SLOT)
                for t in range(NT):
                    for k in range(2):
                        pool.indirect_dma_start(xs, bass.IndirectOffsetOnAxis(ap=slot[:, k, t:t + 1], axis=0),
                                                xn_all[:, t, :], None).then_inc(scattered, 16)
                with pool.Fori(0, STEPS) as j:
                    pool.wait_ge(y_done.sem, y_done.at(j, K))
                    pool.dma_start(ys_tiles[:, bass.ds(K * j, K), :], y_out[:, :, :]).then_inc(stored, 16)
                pool.wait_ge(stored, 16 * STEPS)

            @block.vector
            def _(dve):
                def logits(t):
                    at = t % T * MOE_E
                    return bank[4 + t // T][:, at:at + MOE_E]

                for t in range(NT):
                    dve.wait_ge(routed, t // T + 1)
                    dve.max(best[:, t, :], logits(t)).then_inc(route, 1)
                dve.wait_ge(route, R_BEST)
                dve.tensor_sub(gap[:], best[:, :, 1], best[:, :, 0]).then_inc(route, 1)
                for t in range(NT):
                    dve.max_index(best_at[:, t, :], best[:, t, :], logits(t)).then_inc(route, 1)
                dve.wait_ge(route, R_INDEX)
                dve.tensor_copy(best_f[:, :, :], best_at[:, :, :]).then_inc(route, 1)
                dve.wait_ge(consts, 7)
                dve.tensor_scalar(levels[:], numbers[:, 0:LEVELS], float(P), None, ALU.mult).then_inc(route, 1)
                dve.wait_ge(route, R_FLOAT)
                for k in range(2):
                    dve.tensor_tensor(chosen[k][:, :, :],
                                      numbers[:, 0:MOE_E].unsqueeze(2).to_broadcast([P, MOE_E, NT]),
                                      best_f[:, :, k].unsqueeze(1).to_broadcast([P, MOE_E, NT]),
                                      ALU.is_equal).then_inc(route, 1)
                dve.wait_ge(route, R_CHOSEN)
                dve.tensor_tensor(either[:, :, :], chosen[0][:, :, :], chosen[1][:, :, :], ALU.add).then_inc(route, 1)
                dve.wait_ge(counted, 1)
                dve.tensor_copy(total[:, :, :].rearrange("p e t -> p (e t)"), bank[3][:, 128:256]).then_inc(route, 1)
                dve.wait_ge(route, R_TOTAL)
                dve.tensor_tensor_scan(upto[:, :, :].rearrange("p e t -> p (e t)"),
                                       going_on[:, :, :].rearrange("p e t -> p (e t)"),
                                       total[:, :, :].rearrange("p e t -> p (e t)"), 0.0, ALU.mult,
                                       ALU.add).then_inc(route, 1)
                dve.wait_ge(route, R_UPTO)
                dve.tensor_tensor(level_on[:, :, :],
                                  upto[:, :, NT - 1].unsqueeze(2).to_broadcast([P, MOE_E, LEVELS]),
                                  levels[:].unsqueeze(1).to_broadcast([P, MOE_E, LEVELS]),
                                  ALU.is_gt).then_inc(route, 1)
                dve.wait_ge(route, R_LEVELS)
                dve.tensor_reduce(filled[:], level_on[:, :, :], AX.X, ALU.add).then_inc(route, 1)
                dve.wait_ge(route, R_FILLED)
                dve.tensor_tensor_scan(end[:], ones[:, 0:MOE_E], filled[:], 0.0, ALU.mult, ALU.add).then_inc(route, 1)
                dve.wait_ge(route, R_END)
                dve.tensor_tensor(first[:], end[:], filled[:], ALU.subtract).then_inc(route, 1)
                dve.tensor_tensor(slot_e[:, :, :], upto[:, :, :], total[:, :, :], ALU.subtract).then_inc(route, 1)
                dve.wait_ge(route, R_FIRST)
                dve.tensor_tensor(slot_e[:, :, :], bank[3][:, 0:128].rearrange("p (e t) -> p e t", e=MOE_E),
                                  slot_e[:, :, :], ALU.add).then_inc(route, 1)
                dve.wait_ge(route, R_RANK)
                dve.scalar_tensor_tensor(slot_e[:, :, :], first[:].unsqueeze(2).to_broadcast([P, MOE_E, NT]),
                                         float(P), slot_e[:, :, :], ALU.mult, ALU.add).then_inc(route, 1)
                dve.wait_ge(route, R_SLOT_E)
                for k in range(2):
                    dve.tensor_tensor(chosen[k][:, :, :], chosen[k][:, :, :], slot_e[:, :, :],
                                      ALU.mult).then_inc(route, 1)
                dve.wait_ge(route, R_PICKED)
                for k in range(2):
                    dve.tensor_reduce(slot_f[:, k, :], chosen[k][:, :, :].rearrange("p e t -> p t e"), AX.X,
                                      ALU.add).then_inc(route, 1)
                dve.wait_ge(route, R_SLOT_F)
                dve.tensor_copy(slot[:, :, :], slot_f[:, :, :]).then_inc(route, 1)
                dve.tensor_tensor(passed[:, :, :], end[0:1, :].unsqueeze(1).to_broadcast([1, MOE_TILES, MOE_E]),
                                  numbers[0:1, :].unsqueeze(2).to_broadcast([1, MOE_TILES, MOE_E]),
                                  ALU.is_le).then_inc(route, 1)
                dve.wait_ge(route, R_PASSED)
                dve.tensor_reduce(tile_f[:], passed[:, :, :], AX.X, ALU.add).then_inc(route, 1)
                dve.wait_ge(route, R_TILE_F)
                dve.tensor_scalar(tile_f[:], tile_f[:], float(MOE_E - 1), None, ALU.min).then_inc(route, 1)
                dve.wait_ge(route, R_CAPPED)
                dve.tensor_copy(tile_e[:], tile_f[:]).then_inc(route, 1)

                with dve.Fori(0, STEPS) as j:
                    def hide(u):
                        dve.wait_ge(gated.sem, gated.at(j, u + 1))
                        dve.wait_ge(up_ps.sem, up_ps.at(j, u + 1))
                        dve.wait_ge(hidT_ps.sem, hidT_ps.at(j, u + 1 - 2))
                        dve.tensor_tensor(hidden[u % 2][:], ps_up[u % 2][:], act_gate[u % 2][:],
                                          ALU.mult).then_inc(hid.sem, 1)

                    def copy_y(u):
                        dve.wait_ge(down_ps.sem, down_ps.at(j, u + 1))
                        dve.wait_ge(stored, j * 16)
                        dve.tensor_copy(y_out[:, u, :], ps_y[u % 2][:, 0:D]).then_inc(y_done.sem, 1)

                    for u in range(K):
                        hide(u)
                        if u >= 1:
                            copy_y(u - 1)
                    copy_y(K - 1)

            @block.scalar
            def _(act):
                for b in range(B):
                    for c in range(C):
                        act.wait_ge(xT_ps, b * C + c + 1)
                        if b >= 1:
                            act.wait_ge(routed, b)
                        act.activation(xT[:, c, 1:N + 1], bank[b % 2 * C + c][:], ACT.Copy).then_inc(xT_done, 1)
                act.wait_ge(route, R_GAP)
                act.activation(share[:, 0, :], gap[:], ACT.Sigmoid, scale=-1.0).then_inc(shares, 1)
                act.activation(share[:, 1, :], gap[:], ACT.Sigmoid).then_inc(shares, 1)
                act.preload_act_table(ACT.Silu)
                with act.Fori(0, STEPS) as j:
                    def copy_x(u):
                        act.wait_ge(x_ps.sem, x_ps.at(j, u + 1))
                        act.wait_ge(up_ps.sem, up_ps.at(j, u + 1 - 2))
                        act.activation(x_inT[u % 2][:], ps_xT[:, 0:D], ACT.Copy).then_inc(x_done.sem, 1)

                    def copy_hidden(u):
                        act.wait_ge(hidT_ps.sem, hidT_ps.at(j, u + 1))
                        act.wait_ge(down_ps.sem, down_ps.at(j, u + 1 - 2))
                        act.activation(hiddenT[u % 2][:], ps_hT[:], ACT.Copy).then_inc(hidT_done.sem, 1)

                    copy_x(0)
                    for u in range(K):
                        act.wait_ge(gate_ps.sem, gate_ps.at(j, u + 1))
                        act.wait_ge(hid.sem, hid.at(j, u + 1 - 2))
                        act.activation(act_gate[u % 2][:], ps_gate[u % 2][:], ACT.Silu).then_inc(gated.sem, 1)
                        if u + 1 < K:
                            copy_x(u + 1)
                        if u >= 1:
                            copy_hidden(u - 1)
                    copy_hidden(K - 1)

            @block.tensor
            def _(pe):
                def turn(b):
                    for c in range(C):
                        if b >= 2:
                            pe.wait_ge(xT_done, (b - 2) * C + c + 1)
                        for t in range(T):
                            last = pe.transpose(bank[b % 2 * C + c][:, t * P:(t + 1) * P],
                                                xn_all[:, b * T + t, c * P:(c + 1) * P], ident[:])
                        last.then_inc(xT_ps, 1)

                turn(0)
                pe.wait_ge(loaded_router, 16)
                for b in range(B):
                    if b + 1 < B:
                        turn(b + 1)
                    pe.wait_ge(xT_done, (b + 1) * C)
                    for t in range(T):
                        for c in range(C):
                            last = pe.matmul(bank[4 + b][:, t * MOE_E:(t + 1) * MOE_E],
                                             xT[:, c, 1 + t * P:1 + (t + 1) * P], router_w[:, c, :],
                                             start=(c == 0), stop=(c == C - 1))
                    last.then_inc(routed, 1)

                pe.wait_ge(consts, 7)
                pe.wait_ge(route, R_EITHER)
                chose = either[:, :, :].rearrange("p e t -> p (e t)")
                pe.matmul(bank[3][:, 0:128], below[:], chose, start=True, stop=True)
                pe.matmul(bank[3][:, 128:256], ones[:], chose, start=True, stop=True).then_inc(counted, 1)
                pe.wait_ge(loaded_w, 16 * 2 * MOE_E)
                pe.wait_ge(route, R_TILE_E)
                with pe.Fori(0, STEPS) as j:
                    def turn_in(u):
                        pe.wait_ge(x_loaded.sem, x_loaded.at(j, 16))
                        pe.wait_ge(x_done.sem, x_done.at(j, u))
                        for c in range(C):
                            last = pe.transpose(ps_xT[:, c * P:(c + 1) * P], x_in[:, u, c * P:(c + 1) * P], ident[:])
                        last.then_inc(x_ps.sem, 1)

                    def widen(u, part, ps, done):
                        for c in range(C):
                            w = W13[:, bass.ds(expert[u], 1), c, part * MOE_F:(part + 1) * MOE_F]
                            last = pe.matmul(ps[u % 2][:], x_inT[u % 2][:, c * P:(c + 1) * P],
                                             w.rearrange("p e f -> p (e f)"), start=(c == 0), stop=(c == C - 1))
                        last.then_inc(done.sem, 1)

                    def turn_hidden(u):
                        pe.wait_ge(hid.sem, hid.at(j, u + 1))
                        pe.wait_ge(hidT_done.sem, hidT_done.at(j, u))
                        for c in range(FCH):
                            last = pe.transpose(ps_hT[:, c * P:(c + 1) * P], hidden[u % 2][:, c * P:(c + 1) * P],
                                                ident[:])
                        last.then_inc(hidT_ps.sem, 1)

                    def narrow(u):
                        pe.wait_ge(hidT_done.sem, hidT_done.at(j, u + 1))
                        pe.wait_ge(y_done.sem, y_done.at(j, u + 1 - 2))
                        for c in range(FCH):
                            last = pe.matmul(ps_y[u % 2][:, 0:D], hiddenT[u % 2][:, c * P:(c + 1) * P],
                                             W2[:, bass.ds(expert[u], 1), c, :].rearrange("p e f -> p (e f)"),
                                             start=(c == 0), stop=(c == FCH - 1))
                        last.then_inc(down_ps.sem, 1)

                    def load_expert(u):
                        expert.append(pe.value_load(tile_e[0:1, bass.ds(K * j + u, 1)], min_val=0, max_val=MOE_E - 1))

                    expert = []
                    load_expert(0)
                    turn_in(0)
                    for u in range(K):
                        pe.wait_ge(x_done.sem, x_done.at(j, u + 1))
                        pe.wait_ge(gated.sem, gated.at(j, u + 1 - 2))
                        widen(u, 0, ps_gate, gate_ps)
                        if u + 1 < K:
                            turn_in(u + 1)
                        if u >= 1:
                            turn_hidden(u - 1)
                        pe.wait_ge(hid.sem, hid.at(j, u + 1 - 2))
                        widen(u, 1, ps_up, up_ps)
                        if u + 1 < K:
                            load_expert(u + 1)
                        if u >= 1:
                            narrow(u - 1)
                    turn_hidden(K - 1)
                    narrow(K - 1)


class Attention:

    def __init__(self, ctx, nc, bank, name, keys, masks, ident, ident_bf, window_mask, wo, q_odd):
        def st(what, shape):
            return ctx.enter_context(nc.sbuf_tensor(f"{name}_{what}", shape, F32))

        def signal(what, per):
            return Signal(ctx, nc, f"{name}_{what}", per)

        self.keys, self.masks = keys, masks
        self.ident, self.ident_bf, self.window_mask, self.wo = ident, ident_bf, window_mask, wo
        self.UNITS = T * CA_H
        self.q = [st("q_even", [P, INNER // P, N])[:, :, :], q_odd.rearrange("p (c n) -> p c n", n=N)]
        self.q_cleared = ctx.enter_context(nc.semaphore(f"{name}_q_cleared"))
        self.kT = st("kT", [P, INNER // P, N])
        self.v = st("v", [P, T, INNER])
        self.neg_max = st("neg_max", [P, self.UNITS])
        self.sums = st("sums", [P, self.UNITS])
        self.inv = st("inv", [P, self.UNITS])
        self.prob = [st(f"prob{i}", [P, N]) for i in range(4)]
        self.probT = [st(f"probT{i}", [P, N]) for i in range(2)]
        self.oT_all = st("oT", [P, 2, INNER // P, P])
        self.oT = [self.oT_all[:, i] for i in range(2)]
        self.ps_a, self.ps_l, self.ps_t, self.ps_o = bank[0:2], bank[2:4], bank[4:6], bank[6:8]
        self.ps_out = [self.ps_a[i % 2] for i in range(T)]
        self.logits = signal("logits", self.UNITS)
        self.maxed = signal("maxed", self.UNITS)
        self.probs = signal("probs", self.UNITS)
        self.inverted = signal("inverted", self.UNITS)
        self.scaled = signal("scaled", self.UNITS)
        self.probs_t = signal("probs_t", self.UNITS)
        self.probs_tc = signal("probs_tc", self.UNITS)
        self.pv = signal("pv", self.UNITS)
        self.oT_done = signal("oT", T)
        self.out_ps = signal("out_ps", T)
        self.h_done = signal("h", T)
        self.every = [self.logits, self.maxed, self.probs, self.inverted, self.scaled, self.probs_t,
                      self.probs_tc, self.pv, self.oT_done, self.out_ps, self.h_done]


def clear_q(dve, a):
    for parity in range(2):
        dve.memset(a.q[parity], 0.0).then_inc(a.q_cleared, 1)


def copy_q(act, a, chunks, tokens, src, scale=1.0):
    for parity in range(2):
        own = slice(parity * CA_D, (parity + 1) * CA_D)
        last = act.activation(a.q[parity][own, chunks, tokens], src[own], ACT.Copy, scale=scale)
    return last


TAIL = 5


def attend_pe(pe, b, a, between=()):
    def others(n):
        for at, step in between:
            if at == n:
                step()

    def transposes(n):
        w = len(a.keys(n // CA_H))
        pe.wait_ge(a.scaled.sem, a.scaled.at(b, n + 1))
        pe.wait_ge(a.probs_tc.sem, a.probs_tc.at(b, n + 1 - 2))
        for c in range(w):
            last = pe.transpose(a.ps_t[n % 2][:, c * P:(c + 1) * P], a.prob[n % 4][:, c * P:(c + 1) * P],
                                a.ident[:])
        last.then_inc(a.probs_t.sem, 1)

    def weigh(n):
        i, hd = n // CA_H, n % CA_H
        row, ch = hd % 2 * CA_D, hd // 2
        if hd == 0:
            pe.wait_ge(a.oT_done.sem, a.oT_done.at(b, i + 1 - 2))
        pe.wait_ge(a.probs_tc.sem, a.probs_tc.at(b, n + 1))
        keys = a.keys(i)
        for c, key in enumerate(keys):
            last = pe.matmul(a.ps_o[i % 2][row:row + CA_D, ch * P:(ch + 1) * P],
                             a.v[:, key, hd * CA_D:(hd + 1) * CA_D], a.probT[n % 2][:, c * P:(c + 1) * P],
                             start=(c == 0), stop=(c == len(keys) - 1))
        last.then_inc(a.pv.sem, 1)

    def project_o(i):
        pe.wait_ge(a.oT_done.sem, a.oT_done.at(b, i + 1))
        pe.wait_ge(a.h_done.sem, a.h_done.at(b, i + 1 - 2))
        for c in range(INNER // P):
            last = pe.matmul(a.ps_out[i][:, 0:D], a.oT[i % 2][:, c, :], a.wo[:, c, :], start=(c == 0),
                             stop=(c == INNER // P - 1))
        last.then_inc(a.out_ps.sem, 1)

    for n in range(a.UNITS + 4):
        if n < a.UNITS:
            others(n)
            i, hd = n // CA_H, n % CA_H
            keys, m = a.keys(i), a.masks(i)
            w = len(keys) * P
            ch = hd // 2
            pe.wait_ge(a.probs.sem, a.probs.at(b, n + 1 - 2))
            q = a.q[hd % 2][:, ch, i * P:(i + 1) * P]
            cut, first = w - m * P, keys[0] * P
            if cut:
                pe.matmul(a.ps_l[n % 2][:, 0:cut], q, a.kT[:, ch, first:first + cut], start=True,
                          stop=True)
            pe.matmul(a.ps_l[n % 2][:, cut:w], a.ident_bf[:],
                      a.window_mask[:, 2 - m:2, :].rearrange("p m k -> p (m k)"), start=True, stop=False)
            pe.matmul(a.ps_l[n % 2][:, cut:w], q, a.kT[:, ch, first + cut:first + w], start=False,
                      stop=True).then_inc(a.logits.sem, 1)
        if 2 <= n < a.UNITS + 2:
            transposes(n - 2)
        if 4 <= n:
            weigh(n - 4)
        if n >= CA_H and n % CA_H == TAIL and n < a.UNITS:
            project_o(n // CA_H - 1)
    others(a.UNITS)
    project_o(T - 1)


def attend_act(act, b, a, between=()):
    def copy_t(n):
        w = len(a.keys(n // CA_H)) * P
        act.wait_ge(a.probs_t.sem, a.probs_t.at(b, n + 1))
        act.wait_ge(a.pv.sem, a.pv.at(b, n + 1 - 2))
        act.activation(a.probT[n % 2][:, 0:w], a.ps_t[n % 2][:, 0:w], ACT.Copy).then_inc(a.probs_tc.sem, 1)

    def copy_o(i):
        act.wait_ge(a.pv.sem, a.pv.at(b, (i + 1) * CA_H))
        act.wait_ge(a.out_ps.sem, a.out_ps.at(b, i + 1 - 2))
        act.activation(a.oT[i % 2].rearrange("p c n -> p (c n)"), a.ps_o[i % 2][:],
                       ACT.Copy).then_inc(a.oT_done.sem, 1)

    for n in range(a.UNITS + 3):
        for at, step in between:
            if at == n:
                step()
        if n < a.UNITS:
            w = len(a.keys(n // CA_H)) * P
            act.wait_ge(a.maxed.sem, a.maxed.at(b, n + 1))
            act.wait_ge(a.probs_t.sem, a.probs_t.at(b, n + 1 - 4))
            act.activation(a.prob[n % 4][:, 0:w], a.ps_l[n % 2][:, 0:w], ACT.Exp, bias=a.neg_max[:, n:n + 1],
                           accum_out=a.sums[:, n:n + 1]).then_inc(a.probs.sem, 1)
        if n >= 3:
            copy_t(n - 3)
        if n >= CA_H and n % CA_H == TAIL - 1 and n < a.UNITS:
            copy_o(n // CA_H - 1)
    copy_o(T - 1)


def attend_dve(dve, b, a, h, gate, between=()):
    def scale(n):
        i, hd = n // CA_H, n % CA_H
        w = len(a.keys(i)) * P
        dve.wait_ge(a.probs.sem, a.probs.at(b, n + 1))
        dve.reciprocal(a.inv[:, n:n + 1], a.sums[:, n:n + 1]).then_inc(a.inverted.sem, 1)
        dve.wait_ge(a.inverted.sem, a.inverted.at(b, n + 1))
        prob = a.prob[n % 4][:, 0:w]
        if gate is None:
            dve.tensor_scalar(prob, prob, a.inv[:, n:n + 1], None, ALU.mult).then_inc(a.scaled.sem, 1)
        else:
            dve.tensor_scalar(prob, prob, a.inv[:, n:n + 1], gate[:, i, hd:hd + 1], ALU.mult,
                              ALU.mult).then_inc(a.scaled.sem, 1)

    def add(i):
        dve.wait_ge(a.out_ps.sem, a.out_ps.at(b, i + 1))
        hs = batch_slice(h, b, i)
        dve.tensor_tensor(hs, a.ps_out[i][:, 0:D], hs, ALU.add).then_inc(a.h_done.sem, 1)

    for n in range(a.UNITS + 1):
        for at, step in between:
            if at == n:
                step()
        if n < a.UNITS:
            w = len(a.keys(n // CA_H)) * P
            dve.wait_ge(a.logits.sem, a.logits.at(b, n + 1))
            dve.tensor_reduce(a.neg_max[:, n:n + 1], a.ps_l[n % 2][:, 0:w], AX.X, ALU.max,
                              negate=True).then_inc(a.maxed.sem, 1)
        if n >= 1:
            scale(n - 1)
        if n >= CA_H and n % CA_H == TAIL + 2 and n < a.UNITS:
            add(n // CA_H - 1)
    add(T - 1)


def causal(nc, bank, h, half, share, slot, ys, big, ident, ident_bf, window_mask, xn_all, xn, xT, ca_w, ca_wo_w,
           gates_w, rms_col, early_w, late_loads, loaded_late, loaded_ca):
    QC = INNER // P
    PROJ = 2 * QC + T + 1
    with ExitStack() as ctx:
        def st(name, shape, dt=F32):
            return ctx.enter_context(nc.sbuf_tensor(f"ca_{name}", shape, dt))

        def signal(name, per):
            return Signal(ctx, nc, name, per)

        a = Attention(ctx, nc, bank, "ca", lambda i: list(range(i + 1)), lambda i: 1, ident, ident_bf,
                      window_mask, ca_wo_w, early_w[:, EARLY_SIZE - INNER // P * N:EARLY_SIZE])
        gate_e, gate = st("gate_e", [P, T, CA_H]), st("gate", [P, T, CA_H])

        a.ps_out[T - 1] = a.ps_l[0]
        norm = Normalizer(ctx, nc, "ca_norm", rms=True)
        y_in = big[:, 0:2 * NT * D].rearrange("p (k t n) -> p k t n", k=2, t=NT)
        gathered = [ctx.enter_context(nc.semaphore(f"ca_gathered{b}")) for b in range(B)]
        combined = ctx.enter_context(nc.semaphore("ca_combined"))
        staged = signal("ca_staged", 16)
        xT_ps = signal("ca_xT_ps", C)
        xT_done = signal("ca_xT", C)
        proj_ps = signal("ca_proj_ps", PROJ)
        proj_done = signal("ca_proj", PROJ)
        gate_done = signal("ca_gate", 2)
        every = [staged, xT_ps, xT_done, proj_ps, proj_done, gate_done] + a.every

        with nc.Block() as block:
            @block.sync
            def _(sp):
                for s in every:
                    sp.sem_inc(s.sem, s.per)
                stage_batches(sp, True, xn, xn_all, norm.normed, staged, xT_ps)
                sp.wait_ge(combined, 2 * NT)
                for dst, src in late_loads:
                    sp.dma_start(dst, src).then_inc(loaded_late, 16)
                stage_batches(sp, False, xn, xn_all, norm.normed, staged, xT_ps)

            @block.gpsimd
            def _(pool):
                for b in range(B):
                    for t in range(b * T, (b + 1) * T):
                        for k in range(2):
                            pool.indirect_dma_start(y_in[:, k, t, :], None, ys,
                                                    bass.IndirectOffsetOnAxis(ap=slot[:, k, t:t + 1],
                                                                              axis=0)).then_inc(gathered[b], 16)
                    if b >= 1:
                        norm.on_pool(pool, half, [b - 1])
                norm.on_pool(pool, half, [B - 1])

            @block.vector
            def _(dve):
                clear_q(dve, a)
                for b in range(B):
                    dve.wait_ge(gathered[b], 16 * 2 * T)
                    for k in range(2):
                        if k == 1:
                            dve.wait_ge(combined, (2 * b + 1) * T)
                        for t in range(b * T, (b + 1) * T):
                            dve.scalar_tensor_tensor(h[:, t, :], y_in[:, k, t, :], share[:, k, t:t + 1], h[:, t, :],
                                                     ALU.mult, ALU.add).then_inc(combined, 1)
                    dve.wait_ge(combined, 2 * T * (b + 1))
                    norm.on_dve(dve, b, h, xn_all)
                with dve.Fori(0, B) as b:
                    dve.wait_ge(proj_done.sem, proj_done.at(b, PROJ))
                    dve.tensor_scalar(gate_e[:, :, :], gate_e[:, :, :], 1.0, None, ALU.add).then_inc(gate_done.sem, 1)
                    dve.wait_ge(gate_done.sem, gate_done.at(b, 1))
                    dve.reciprocal(gate[:, :, :], gate_e[:, :, :]).then_inc(gate_done.sem, 1)
                    dve.wait_ge(gate_done.sem, gate_done.at(b, 2))
                    attend_dve(dve, b, a, h, gate)

            @block.scalar
            def _(act):
                act.wait_ge(loaded_ca, 16 * 6)
                act.preload_act_table(ACT.Exp)

                def copy_x(b):
                    for c in range(C):
                        act.wait_ge(proj_ps.sem, proj_ps.at(b, 0))
                        act.wait_ge(xT_ps.sem, xT_ps.at(b, c + 1))
                        act.activation(xT[:, c, 1:N + 1], a.ps_a[c][:], ACT.Identity,
                                       scale=rms_col[:, c:c + 1]).then_inc(xT_done.sem, 1)

                copy_x(0)
                act.wait_ge(a.q_cleared, 2)
                with act.Fori(0, B) as b:
                    for k in range(PROJ):
                        if k == 0:
                            act.wait_ge(a.pv.sem, a.pv.at(b, 0))
                            act.wait_ge(gate_done.sem, gate_done.at(b, 0))
                        act.wait_ge(proj_ps.sem, proj_ps.at(b, k + 1))
                        src = a.ps_a[k % 2][:]
                        if k < QC:
                            ins = copy_q(act, a, k, slice(0, N), src, float(CA_D) ** -0.5)
                        elif k < 2 * QC:
                            ins = act.activation(a.kT[:, k - QC, :], src, ACT.Copy)
                        elif k < 2 * QC + T:
                            ins = act.activation(a.v[:, k - 2 * QC, :], src, ACT.Copy)
                        else:
                            ins = act.activation(gate_e[:, :, :].rearrange("p t h -> p (t h)"),
                                                 a.ps_a[k % 2][:, 0:T * CA_H], ACT.Exp, scale=-1.0)
                        ins.then_inc(proj_done.sem, 1)
                    attend_act(act, b, a)
                    copy_x(b + 1)

            @block.tensor
            def _(pe):
                pe.wait_ge(loaded_ca, 16 * 6)
                turn_staged(pe, 0, xn, ident, a.ps_a, staged, xT_ps)
                with pe.Fori(0, B) as b:
                    def turn_next():
                        pe.wait_ge(a.h_done.sem, a.h_done.at(b, T - 1))
                        turn_staged(pe, b + 1, xn, ident, a.ps_a, staged, xT_ps)

                    for k in range(PROJ):
                        if k == 0:
                            pe.wait_ge(xT_done.sem, xT_done.at(b, C))
                        if k >= 2:
                            pe.wait_ge(proj_done.sem, proj_done.at(b, k - 1))
                        if k < 2 * QC:
                            for c in range(C):
                                last = pe.matmul(a.ps_a[k % 2][:], ca_w[:, c, k * P:(k + 1) * P],
                                                 xT[:, c, 1:N + 1], start=(c == 0), stop=(c == C - 1))
                        elif k < 2 * QC + T:
                            t = k - 2 * QC
                            for c in range(C):
                                last = pe.matmul(a.ps_a[k % 2][:], xT[:, c, 1 + t * P:1 + (t + 1) * P],
                                                 ca_w[:, c, 2 * INNER:], start=(c == 0), stop=(c == C - 1))
                        else:
                            for t in range(T):
                                for c in range(C):
                                    last = pe.matmul(a.ps_a[k % 2][:, t * CA_H:(t + 1) * CA_H],
                                                     xT[:, c, 1 + t * P:1 + (t + 1) * P], gates_w[:, c, :],
                                                     start=(c == 0), stop=(c == C - 1))
                        last.then_inc(proj_ps.sem, 1)
                    pe.wait_ge(proj_done.sem, proj_done.at(b, PROJ))
                    pe.wait_ge(a.h_done.sem, a.h_done.at(b, 0))
                    attend_pe(pe, b, a, [(a.UNITS, turn_next)])


LATE_SHAPES = {
    "wqkv": [DEPTH, C, 3 * INNER],
    "wo": [DEPTH, INNER // P, D],
    "w1": [DEPTH, C, 2 * HID],
    "w2": [DEPTH, FC, D],
    "ln_g": [DEPTH, C],
    "ln_b": [DEPTH, C],
    "b1": [DEPTH, 2, FC],
    "trig": [T, 4 * CA_D],
    "qk_scale": [DEPTH, 4 * CA_D],
    "spare": [FC * N],
}
LATE_SIZE = sum(int(np.prod(x)) for x in LATE_SHAPES.values())


def late_views(big):
    views, at = {}, 0
    for name, shape in LATE_SHAPES.items():
        size = int(np.prod(shape))
        flat = big[:, at:at + size]
        letters = "abc"[:len(shape)]
        views[name] = flat.rearrange(f"p ({' '.join(letters)}) -> p {' '.join(letters)}",
                                     **{x: n for x, n in zip(letters[:-1], shape[:-1])})
        at += size
    return views


def late_loads(views, b2_row, wqkv, ffn_wo, w1, w2f, trig, qk_scale, ln_g, ln_b, b1, b2):
    loads = []
    full = (FC - 1) * P
    for l in range(DEPTH):
        loads += [(views["wqkv"][:, l], wqkv[l].rearrange("(c p) n -> p c n", p=P)),
                  (views["wo"][:, l], ffn_wo[l].rearrange("(c p) n -> p c n", p=P)),
                  (views["w1"][:, l], w1[l].rearrange("(c p) n -> p c n", p=P)),
                  (views["w2"][:, l, 0:FC - 1], w2f[l, 0:full, :].rearrange("(c p) n -> p c n", p=P)),
                  (views["w2"][0:HID - full, l, FC - 1], w2f[l, full:HID, :])]
    loads += [(views["ln_g"], ln_g.rearrange("p (l c) -> p l c", c=C)),
              (views["ln_b"], ln_b.rearrange("p (l c) -> p l c", c=C)),
              (views["b1"], b1), (views["trig"], trig), (views["qk_scale"], qk_scale), (b2_row[:, :], b2)]
    return loads


def local_layers(nc, bank, h, pause, ident, ident_bf, window_mask, half, one_row, xn, xT, w, b2_row, kept,
                 loaded_late, n_late):
    HD2 = CA_D // 2
    TH, NH = T // 2, N // 2
    LN_STEPS = 3 * TH + 1
    DOWN_AFTER = [FC + 2, FC + 3]
    TURN_N = 5
    TURN_AT, COPY_AT, SCALE_AT, NORM_AT = 7, 8, 4, 3 * CA_H + 3
    with ExitStack() as ctx:
        def st(name, shape, dt=F32):
            return ctx.enter_context(nc.sbuf_tensor(f"local_{name}", shape, dt))

        def signal(name, per):
            return Signal(ctx, nc, f"local_{name}", per)

        a = Attention(ctx, nc, bank, "local", lambda i: list(range(max(i - 1, 0), i + 1)),
                      lambda i: min(i + 1, 2), ident, ident_bf, window_mask, None,
                      w["early_a"][:, EARLY_SIZE - INNER // P * N:EARLY_SIZE])
        straight = [w["early_a"][:, i * 2 * INNER:(i + 1) * 2 * INNER] for i in range(2)]
        table = w["early_b"][:, 0:T * 4 * CA_D].rearrange("p (t n) -> p t n", t=T)
        squares = [w["spare"][:, i * 2 * INNER:(i + 1) * 2 * INNER] for i in range(2)]
        crossed = [w["spare"][:, 4 * INNER:6 * INNER],
                   a.oT_all[:, :, :, :].rearrange("p i c n -> p (i c n)")]
        norm_sq, rnorm = st("norm_sq", [P, T, 16]), st("rnorm", [P, T, 16])
        shifted = st("shifted", [P, T, P])
        stats, moments = st("stats", [P, T, 12]), st("moments", [P, T, 2])
        var_eps, rstd = st("var_eps", [P, T]), st("rstd", [P, T])
        act_gate = [a.prob[0], a.prob[1]]
        hidden = w["spare"].rearrange("p (c n) -> p c n", c=FC)

        norm = Normalizer(ctx, nc, "enter_norm")
        copied = ctx.enter_context(nc.semaphore("enter_kept"))
        table_done = ctx.enter_context(nc.semaphore("local_table"))
        staged = signal("staged", 16)
        xT_ps = signal("xT_ps", C)
        xT_done = signal("xT", C)
        qkv_ps = signal("qkv_ps", 3 * T)
        squared = signal("squared", 2 * T)
        v_done = signal("v", T)
        rotary = signal("rotary", 4 * T)
        norms = signal("norms", 2 * T)
        rnorm_done = signal("rnorm", T)
        rotated = signal("rotated", 2 * T)
        q_scaled = signal("q_scaled", T)
        qkT_ps = signal("qkT_ps", T)
        qkT_done = signal("qkT", 2 * T)
        shift_done = [signal(f"shift{half}", 32) for half in range(2)]
        moments_done = signal("moments", 2 * LN_STEPS)
        rstd_done = signal("rstd", 2)
        normed = signal("normed", 2 * T)
        nT_ps = signal("nT_ps", 2)
        nT_done = signal("nT", 2 * C)
        up_ps = signal("up_ps", 2 * FC)
        gated = signal("gated", 2 * FC)
        hid = signal("hidden", 2 * FC)
        down_ps = signal("down_ps", T)
        h_done = signal("h2", T)
        every = [staged, xT_ps, xT_done, qkv_ps, squared, v_done, rotary, norms, rnorm_done, rotated,
                 q_scaled, qkT_ps, qkT_done, *shift_done, moments_done, rstd_done, normed, nT_ps, nT_done, up_ps, gated,
                 hid, down_ps, h_done] + a.every
        ps_a = a.ps_a

        for layer in range(DEPTH):
            wqkv, w1, w2 = w["wqkv"][:, layer], w["w1"][:, layer], w["w2"][:, layer]
            a.wo = w["wo"][:, layer]
            with nc.Block() as block:
                @block.sync
                def _(sp):
                    if layer == 0:
                        for s in every:
                            sp.sem_inc(s.sem, s.per)
                    with sp.Fori(0, B) as b:
                        if layer == 0:
                            sp.wait_ge(norm.normed, b * T + T)
                        sp.wait_ge(nT_ps.sem, nT_ps.at(b, 0))
                        sp.dma_start(xn[:, :, :], h[:, bass.ds(b * T, T), :]).then_inc(staged.sem, 16)
                        for u in range(2):
                            t0 = u * TH
                            sp.wait_ge(a.h_done.sem, a.h_done.at(b, t0 + TH))
                            sp.dma_start(shifted[1:P, t0:t0 + TH, :],
                                         h[0:P - 1, t0:NT, P:2 * P][:, bass.ds(b * T, TH), :]).then_inc(shift_done[u].sem, 16)
                            t1 = max(t0, 1)
                            sp.dma_start(shifted[0:1, t1:t0 + TH, :],
                                         h[P - 1:P, t1 - 1:NT, P:2 * P][:, bass.ds(b * T, t0 + TH - t1), :]).then_inc(shift_done[u].sem, 16)

                    end_staging(sp, staged)

                @block.gpsimd
                def _(pool):
                    if layer == 0:
                        norm.on_pool(pool, half)
                    with pool.Fori(0, B) as b:
                        for t in range(T):
                            pool.wait_ge(rotary.sem, rotary.at(b, 4 * t + 4))
                            pool.wait_ge(qkT_ps.sem, qkT_ps.at(b, t + 1 - 2))
                            pool.tensor_tensor(straight[t % 2], straight[t % 2], crossed[t % 2],
                                               ALU.add).then_inc(rotated.sem, 1)
                            pool.wait_ge(norms.sem, norms.at(b, 2 * t + 2))
                            pool.tensor_tensor(rnorm[:, t, :], norm_sq[:, t, :], half[:], ALU.pow).then_inc(rnorm_done.sem, 1)
                            pool.wait_ge(rnorm_done.sem, rnorm_done.at(b, t + 1))
                            pool.wait_ge(rotated.sem, rotated.at(b, 2 * t + 1))
                            keys = straight[t % 2][:, INNER:].rearrange("p (h d) -> p h d", d=CA_D)
                            pool.tensor_tensor(keys, keys, rnorm[:, t, CA_H:].unsqueeze(2).to_broadcast([P, CA_H, CA_D]),
                                               ALU.mult).then_inc(rotated.sem, 1)
                        for u in range(2):
                            pool.wait_ge(moments_done.sem, moments_done.at(b, (u + 1) * LN_STEPS))
                            mine = slice(u * TH, (u + 1) * TH)
                            pool.tensor_tensor(rstd[:, mine], var_eps[:, mine], half[:, 0:TH],
                                               ALU.pow).then_inc(rstd_done.sem, 1)

                @block.vector
                def _(dve):
                    def add_down(b, t):
                        dve.wait_ge(down_ps.sem, down_ps.at(b, t + 1))
                        hs = batch_slice(h, b, t)
                        dve.tensor_tensor(hs, bank[6 + t % 2][:, 0:D], hs, ALU.add).then_inc(h_done.sem, 1)

                    if layer == 0:
                        dve.memset(shifted[0:1, 0, :], 0.0)
                        for b in range(B):
                            dve.wait_ge(copied, b + 1)
                            norm.on_dve(dve, b, h, h)
                            if b == 0:
                                clear_q(dve, a)
                    dve.wait_ge(loaded_late, 16 * n_late)
                    dve.tensor_tensor(table[:, :, :], w["trig"],
                                      w["qk_scale"][:, layer, :].unsqueeze(1).to_broadcast([P, T, 4 * CA_D]),
                                      ALU.mult).then_inc(table_done, 1)
                    dve.wait_ge(table_done, layer + 1)
                    with dve.Fori(0, B) as b:
                        def scale_q(t):
                            dve.wait_ge(rnorm_done.sem, rnorm_done.at(b, t + 1))
                            dve.wait_ge(rotated.sem, rotated.at(b, 2 * t + 1))
                            queries = straight[t % 2][:, 0:INNER].rearrange("p (h d) -> p h d", d=CA_D)
                            dve.tensor_tensor(queries, queries,
                                              rnorm[:, t, 0:CA_H].unsqueeze(2).to_broadcast([P, CA_H, CA_D]),
                                              ALU.mult).then_inc(q_scaled.sem, 1)

                        def own_half(u):
                            tiles = range(u * TH, (u + 1) * TH)
                            dve.wait_ge(a.h_done.sem, a.h_done.at(b, (u + 1) * TH))
                            dve.memset(pause[:], 0.0)
                            for t in tiles:
                                dve.bn_stats(stats[:, t, 0:6], batch_slice(h, b, t)[:, 0:P]).then_inc(moments_done.sem, 1)

                        def shifted_half(u):
                            tiles = range(u * TH, (u + 1) * TH)
                            dve.wait_ge(shift_done[u].sem, shift_done[u].at(b, 32))
                            for t in tiles:
                                dve.bn_stats(stats[:, t, 6:12], shifted[:, t, :]).then_inc(moments_done.sem, 1)
                            dve.wait_ge(moments_done.sem, moments_done.at(b, u * LN_STEPS + 2 * TH))
                            dve.memset(pause[:], 0.0)
                            for t in tiles:
                                dve.bn_aggr(moments[:, t, :], stats[:, t, :]).then_inc(moments_done.sem, 1)
                            dve.wait_ge(moments_done.sem, moments_done.at(b, u * LN_STEPS + 3 * TH))
                            mine = slice(u * TH, (u + 1) * TH)
                            dve.tensor_scalar(var_eps[:, mine], moments[:, mine, 1], EPS_LN, None,
                                              ALU.add).then_inc(moments_done.sem, 1)

                        def center(u):
                            dve.wait_ge(xT_ps.sem, xT_ps.at(b, C))
                            dve.wait_ge(rstd_done.sem, rstd_done.at(b, u + 1))
                            for t in range(u * TH, (u + 1) * TH):
                                for c, src in enumerate([batch_slice(h, b, t)[:, 0:P], shifted[:, t, :]]):
                                    dve.tensor_scalar(xn[:, t, c * P:(c + 1) * P], src, moments[:, t, 0:1],
                                                      rstd[:, t:t + 1], ALU.subtract, ALU.mult).then_inc(normed.sem, 1)

                        dve.wait_ge(down_ps.sem, down_ps.at(b, 0))
                        dve.wait_ge(a.out_ps.sem, a.out_ps.at(b, 0))
                        for t in range(T):
                            dve.wait_ge(rotated.sem, rotated.at(b, 2 * (t + 1 - 2)))
                            dve.wait_ge(qkT_ps.sem, qkT_ps.at(b, t + 1 - 2))
                            for k in range(2):
                                dve.wait_ge(squared.sem, squared.at(b, 2 * t + k + 1))
                                ps = bank[2 + 2 * k + t % 2][:]
                                cos = table[:, t, 2 * k * CA_D:(2 * k + 1) * CA_D]
                                sin = table[:, t, (2 * k + 1) * CA_D:(2 * k + 2) * CA_D]
                                cols = slice(k * INNER, (k + 1) * INNER)
                                dve.tensor_tensor(straight[t % 2][:, cols].rearrange("p (h d) -> p h d", d=CA_D),
                                                  ps.rearrange("p (h d) -> p h d", d=CA_D),
                                                  cos.unsqueeze(1).to_broadcast([P, CA_H, CA_D]),
                                                  ALU.mult).then_inc(rotary.sem, 1)
                                for s in range(2):
                                    ins = dve.tensor_tensor(
                                        crossed[t % 2][:, cols].rearrange("p (h s d) -> p h s d", s=2, d=HD2)[:, :, s, :],
                                        ps.rearrange("p (h s d) -> p h s d", s=2, d=HD2)[:, :, 1 - s, :],
                                        sin[:, s * HD2:(s + 1) * HD2].unsqueeze(1).to_broadcast([P, CA_H, HD2]),
                                        ALU.mult)
                                ins.then_inc(rotary.sem, 1)
                                if k == 0 and t >= 1:
                                    scale_q(t - 1)
                            dve.tensor_reduce(norm_sq[:, t, :], squares[t % 2].rearrange("p (h d) -> p h d", d=CA_D),
                                              AX.X, ALU.add).then_inc(norms.sem, 1)
                            dve.wait_ge(norms.sem, norms.at(b, 2 * t + 1))
                            dve.tensor_scalar(norm_sq[:, t, :], norm_sq[:, t, :], 1e-24, None,
                                              ALU.max).then_inc(norms.sem, 1)
                        attend_dve(dve, b, a, h, None, [(SCALE_AT, lambda: scale_q(T - 1)),
                                                        (NORM_AT, lambda: own_half(0)),
                                                        (NORM_AT, lambda: shifted_half(0)),
                                                        (NORM_AT + 2, lambda: center(0))])
                        own_half(1)
                        for u in range(2 * FC):
                            n, cols = u % FC, slice(u // FC * NH, (u // FC + 1) * NH)
                            if u == 1:
                                shifted_half(1)
                            if u == 3:
                                center(1)
                            dve.wait_ge(gated.sem, gated.at(b, u + 1))
                            dve.scalar_tensor_tensor(hidden[0:FW[n], n, cols], bank[2 + u % 2][0:FW[n], 0:NH],
                                                     w["b1"][0:FW[n], layer, 0, n:n + 1],
                                                     act_gate[u % 2][0:FW[n], 0:NH],
                                                     ALU.add, ALU.mult).then_inc(hid.sem, 1)
                            if u in DOWN_AFTER:
                                add_down(b, DOWN_AFTER.index(u))
                        for t in range(TH, T):
                            add_down(b, t)

                @block.scalar
                def _(act):
                    def copy_qk(b, t):
                        act.wait_ge(qkT_ps.sem, qkT_ps.at(b, t + 1))
                        tokens = slice(t * P, (t + 1) * P)
                        qT, kT = (ps_a[k][:].rearrange("p (c n) -> p c n", c=INNER // P) for k in range(2))
                        copy_q(act, a, slice(0, INNER // P), tokens, qT).then_inc(qkT_done.sem, 1)
                        act.activation(a.kT[:, :, tokens], kT, ACT.Copy).then_inc(qkT_done.sem, 1)

                    if layer == 0:
                        for b in range(B):
                            act.activation(kept[b], h[:, b * T:(b + 1) * T, :].rearrange("p t d -> p (t d)"),
                                           ACT.Copy).then_inc(copied, 1)
                    def copy_x(b):
                        for c in range(C):
                            act.wait_ge(up_ps.sem, up_ps.at(b, 0))
                            act.wait_ge(xT_ps.sem, xT_ps.at(b, c + 1))
                            act.activation(xT[:, c, 1:N + 1], ps_a[c][:], ACT.Copy).then_inc(xT_done.sem, 1)

                    act.preload_act_table(ACT.Exp)
                    copy_x(0)
                    act.wait_ge(a.q_cleared, 2)
                    with act.Fori(0, B) as b:
                        act.wait_ge(down_ps.sem, down_ps.at(b, 0))
                        for t in range(T):
                            act.wait_ge(norms.sem, norms.at(b, 2 * (t + 1 - 2)))
                            for k in range(2):
                                act.wait_ge(qkv_ps.sem, qkv_ps.at(b, 3 * t + k + 1))
                                act.activation(squares[t % 2][:, k * INNER:(k + 1) * INNER], bank[2 + 2 * k + t % 2][:],
                                               ACT.Square).then_inc(squared.sem, 1)
                            act.wait_ge(qkv_ps.sem, qkv_ps.at(b, 3 * t + 3))
                            act.activation(a.v[:, t, :], bank[6 + t % 2][:], ACT.Copy).then_inc(v_done.sem, 1)
                            if t >= 1:
                                copy_qk(b, t - 1)
                        def copy_n(half):
                            act.wait_ge(nT_ps.sem, nT_ps.at(b, half + 1))
                            for c in range(C):
                                act.activation(xT[:, c, 1 + half * NH:1 + (half + 1) * NH],
                                               ps_a[half][:, c * NH:(c + 1) * NH], ACT.Identity,
                                               bias=w["ln_b"][:, layer, c:c + 1],
                                               scale=w["ln_g"][:, layer, c:c + 1]).then_inc(nT_done.sem, 1)

                        attend_act(act, b, a, [(COPY_AT, lambda: copy_qk(b, T - 1))])
                        act.preload_act_table(ACT.Gelu)
                        copy_n(0)
                        for u in range(2 * FC):
                            n = u % FC
                            if u == TURN_N:
                                copy_n(1)
                            act.wait_ge(up_ps.sem, up_ps.at(b, u + 1))
                            act.wait_ge(hid.sem, hid.at(b, u + 1 - 2))
                            act.activation(act_gate[u % 2][0:FW[n], 0:NH], bank[4 + u % 2][0:FW[n], 0:NH], ACT.Gelu,
                                           bias=w["b1"][0:FW[n], layer, 1, n:n + 1]).then_inc(gated.sem, 1)
                        act.preload_act_table(ACT.Exp)
                        copy_x(b + 1)

                @block.tensor
                def _(pe):
                    def turn_qk(b, t):
                        pe.wait_ge(rotated.sem, rotated.at(b, 2 * t + 2))
                        pe.wait_ge(q_scaled.sem, q_scaled.at(b, t + 1))
                        if t == 0:
                            pe.wait_ge(xT_done.sem, xT_done.at(b, C))
                        pe.wait_ge(qkT_done.sem, qkT_done.at(b, 2 * t))
                        for k in range(2):
                            for c in range(INNER // P):
                                at = k * INNER + c * P
                                last = pe.transpose(ps_a[k][:, c * P:(c + 1) * P], straight[t % 2][:, at:at + P], ident[:])
                        last.then_inc(qkT_ps.sem, 1)

                    pe.wait_ge(loaded_late, 16 * n_late)
                    turn_staged(pe, 0, xn, ident, ps_a, staged, xT_ps)
                    with pe.Fori(0, B) as b:
                        pe.wait_ge(xT_done.sem, xT_done.at(b, C))
                        pe.wait_ge(hid.sem, hid.at(b, 0))
                        pe.wait_ge(h_done.sem, h_done.at(b, 0))
                        for t in range(T):
                            for k in range(3):
                                if k < 2:
                                    pe.wait_ge(rotary.sem, rotary.at(b, 4 * (t + 1 - 2)))
                                    pe.wait_ge(squared.sem, squared.at(b, 2 * (t + 1 - 2)))
                                else:
                                    pe.wait_ge(v_done.sem, v_done.at(b, t + 1 - 2))
                                for c in range(C):
                                    last = pe.matmul(bank[2 + 2 * k + t % 2][:], xT[:, c, 1 - c + t * P:1 - c + (t + 1) * P],
                                                     wqkv[:, c, k * INNER:(k + 1) * INNER], start=(c == 0),
                                                     stop=(c == C - 1))
                                last.then_inc(qkv_ps.sem, 1)
                            if t >= 1:
                                turn_qk(b, t - 1)
                        pe.wait_ge(rotary.sem, rotary.at(b, 4 * T))
                        pe.wait_ge(v_done.sem, v_done.at(b, T))

                        def turn_n(half):
                            for c in range(C):
                                for t in range(half * TH, (half + 1) * TH):
                                    pe.wait_ge(normed.sem, normed.at(b, 2 * t + c + 1))
                                    at = c * NH + (t - half * TH) * P
                                    last = pe.transpose(ps_a[half][:, at:at + P], xn[:, t, c * P:(c + 1) * P], ident[:])
                            last.then_inc(nT_ps.sem, 1)

                        def up(u):
                            half, n = u // FC, u % FC
                            pe.wait_ge(hid.sem, hid.at(b, u + 1 - 2))
                            if n == 0:
                                pe.wait_ge(nT_done.sem, nT_done.at(b, (half + 1) * C))
                            for part in range(2):
                                for c in range(C):
                                    at = part * HID + n * P
                                    last = pe.matmul(bank[2 + 2 * part + u % 2][0:FW[n], 0:NH], w1[:, c, at:at + FW[n]],
                                                     xT[:, c, 1 + half * NH:1 + (half + 1) * NH],
                                                     start=(c == 0), stop=(c == C - 1))
                            last.then_inc(up_ps.sem, 1)

                        def down(t):
                            if t >= 2:
                                pe.wait_ge(h_done.sem, h_done.at(b, t + 1 - 2))
                            pe.matmul(bank[6 + t % 2][:, 0:D], one_row[:], b2_row[:, layer * D:(layer + 1) * D],
                                      start=True, stop=False)
                            for n in range(FC):
                                pe.wait_ge(hid.sem, hid.at(b, t // TH * FC + n + 1))
                                last = pe.matmul(bank[6 + t % 2][:, 0:D], hidden[0:FW[n], n, t * P:(t + 1) * P],
                                                 w2[0:FW[n], n, :], start=False, stop=(n == FC - 1))
                            last.then_inc(down_ps.sem, 1)

                        pe.wait_ge(qkT_done.sem, qkT_done.at(b, 2 * (T - 1)))
                        attend_pe(pe, b, a, [(TURN_AT, lambda: turn_qk(b, T - 1)),
                                             ((T - 1) * CA_H, lambda: pe.wait_ge(qkT_done.sem, qkT_done.at(b, 2 * T))),
                                             (a.UNITS, lambda: turn_n(0))])
                        for u in range(2 * FC):
                            if u == TURN_N:
                                pe.wait_ge(a.h_done.sem, a.h_done.at(b, T))
                                turn_n(1)
                            up(u)
                            if u in DOWN_AFTER:
                                down(DOWN_AFTER.index(u))
                        turn_staged(pe, b + 1, xn, ident, ps_a, staged, xT_ps)
                        for t in range(TH, T):
                            down(t)
            for s in every:
                s.passed += B
            for s in [staged, xT_ps, xT_done]:
                s.passed += 1


def turn_staged(pe, b, xn, ident, banks, staged, xT_ps):
    pe.wait_ge(staged.sem, staged.at(b, staged.per))
    for c in range(C):
        for t in range(T):
            last = pe.transpose(banks[c][:, t * P:(t + 1) * P], xn[:, t, c * P:(c + 1) * P], ident[:])
        last.then_inc(xT_ps.sem, 1)


def rotary_tables():
    f = np.float32
    half_idx = np.arange(0, CA_D, 2, dtype=f)
    inv_freq = f(1.0) / f(10000.0) ** (half_idx / f(CA_D))
    t = np.arange(N, dtype=f)
    freqs = t[:, None] * inv_freq[None, :]
    freqs = np.concatenate([freqs, freqs], axis=-1)
    base = (half_idx + f(0.4 * CA_D)) / f(1.4 * CA_D)
    power = (t - f(N // 2)) / f(64.0)
    scale = base[None, :] ** power[:, None]
    scale = np.concatenate([scale, scale], axis=-1)
    sign = np.where(np.arange(CA_D) < CA_D // 2, f(-1.0), f(1.0))
    cos, sin = np.cos(freqs), np.sin(freqs) * sign
    tables = np.stack([f(8.0) * cos * scale, f(8.0) * sin * scale, cos / scale, sin / scale], axis=1)
    return np.ascontiguousarray(tables.astype(f).reshape(T, P, 4 * CA_D).transpose(1, 0, 2))


def kernel(x, L0_tok_emb0, L0_tok_emb1, L0_tok_emb2, L0_tok_emb3, L0_tok_proj0, L0_tok_proj1, L0_tok_proj2,
           L0_tok_proj3, L0_attn_Wq, L0_attn_Wk, L0_attn_Wv, L0_attn_Wo, L0_ffn_moe_router, L0_ffn_moe_w13,
           L0_ffn_moe_w2, L1_attn_wq, L1_attn_wk, L1_attn_wv, L1_attn_wo, L1_attn_w_lr, L1_attn_w_target,
           L1_attn_w_gates, L1_attn_rms_w, L1_ffn_wqkv, L1_ffn_q_scale, L1_ffn_k_scale, L1_ffn_wo, L1_ffn_ln_g,
           L1_ffn_ln_b, L1_ffn_w1, L1_ffn_b1, L1_ffn_w2, L1_ffn_b2):
    import concourse.bacc as bacc
    from concourse.bass_utils import run_bass_kernel_spmd

    tables = [np.asarray(t) for t in (L0_tok_emb0, L0_tok_emb1, L0_tok_emb2, L0_tok_emb3)]
    projs = [np.asarray(t) for t in (L0_tok_proj0, L0_tok_proj1, L0_tok_proj2, L0_tok_proj3)]
    emb = np.zeros((CUTOFFS[-1], D), tables[0].dtype)
    for k, t in enumerate(tables):
        emb[CUTOFFS[k]:CUTOFFS[k + 1], 0:EMB_W[k]] = t
    proj = np.zeros((3 * P, D), projs[0].dtype)
    for k, t in enumerate(projs):
        proj[EMB_AT[k]:EMB_AT[k] + EMB_W[k]] = t.T

    def twice_columns(w):
        one = w.T.reshape(D, SB_H, 1, SB_D)
        return np.ascontiguousarray(np.broadcast_to(one, (D, SB_H, 2, SB_D)).reshape(D, SB_H * SB_PAD))

    def twice_rows(w):
        one = w.T.reshape(SB_H, 1, SB_D, D)
        return np.ascontiguousarray(np.broadcast_to(one, (SB_H, 2, SB_D, D)).reshape(SB_H * SB_PAD, D))

    low = (np.arange(P) % SB_PAD < SB_D).astype(np.float32)
    own_rows = (np.arange(P)[:, None] // SB_D == np.arange(P // SB_D)).astype(np.float32)
    kinds = np.concatenate([low[:, None], 1 - low[:, None], own_rows], axis=1)

    def heads_last(w):
        return np.ascontiguousarray(np.asarray(w).transpose(1, 0, 2).reshape(D, INNER))

    def columns(w):
        return np.ascontiguousarray(np.asarray(w).reshape(-1, P).T)

    q_s, k_s = np.asarray(L1_ffn_q_scale), np.asarray(L1_ffn_k_scale)
    qk_scale = np.stack([q_s, np.roll(q_s, CA_D // 2, axis=1), k_s, np.roll(k_s, CA_D // 2, axis=1)], axis=1)
    qk_scale = np.ascontiguousarray(np.broadcast_to(qk_scale.reshape(1, DEPTH, 4 * CA_D), (P, DEPTH, 4 * CA_D)))
    b1 = np.zeros((DEPTH, 2, FC * P), q_s.dtype)
    b1[:, :, 0:HID] = np.asarray(L1_ffn_b1).reshape(DEPTH, 2, HID)
    b1 = np.ascontiguousarray(b1.reshape(DEPTH, 2, FC, P).transpose(3, 0, 1, 2))

    arrays = {
        "ids": np.ascontiguousarray(np.asarray(x).reshape(NT, P).T),
        "emb": emb,
        "proj": proj.reshape(3, P, D),
        "sb_wq": np.ascontiguousarray(np.asarray(L0_attn_Wq).T), "sb_wk": np.ascontiguousarray(np.asarray(L0_attn_Wk).T),
        "sb_wv": np.ascontiguousarray(np.asarray(L0_attn_Wv).T),
        "sb_wv2": twice_columns(np.asarray(L0_attn_Wv)),
        "sb_wo2": twice_rows(np.asarray(L0_attn_Wo)), "kinds": kinds,
        "router": np.asarray(L0_ffn_moe_router), "w13": np.asarray(L0_ffn_moe_w13), "w2": np.asarray(L0_ffn_moe_w2),
        "ca_wq": heads_last(L1_attn_wq), "ca_wk": heads_last(L1_attn_wk), "ca_wv": heads_last(L1_attn_wv),
        "ca_wo": np.asarray(L1_attn_wo).reshape(INNER, D), "w_gates": np.asarray(L1_attn_w_gates),
        "rms_w": columns(L1_attn_rms_w),
        "trig": rotary_tables(),
        "wqkv": np.asarray(L1_ffn_wqkv), "qk_scale": qk_scale,
        "ffn_wo": np.asarray(L1_ffn_wo), "ln_g": columns(L1_ffn_ln_g), "ln_b": columns(L1_ffn_ln_b),
        "w1": np.asarray(L1_ffn_w1), "b1": b1, "w2f": np.asarray(L1_ffn_w2),
        "b2": np.asarray(L1_ffn_b2).reshape(1, DEPTH * D),
    }
    nc = bacc.Bacc("TRN2", target_bir_lowering=False, num_devices=1)
    args = [nc.dram_tensor(k, a.shape, mybir.dt.from_np(a.dtype), kind="ExternalInput").ap() for k, a in arrays.items()]
    out = nc.dram_tensor("out", (B * N, D), F32, kind="ExternalOutput").ap()
    slots = [nc.dram_tensor(name, (MOE_TILES * P, D), F32, kind="Internal").ap() for name in ("moe_in", "moe_out")]
    program(nc, *args, *slots, out)
    r = run_bass_kernel_spmd(nc, [arrays], core_ids=[0])
    return r.results[0]["out"].reshape(B, N, D)
```
